# Optimizing a Trainium2 kernel written in Bass

```python
import numpy as np
import jax
import jax.numpy as jnp

def _softmax(x, axis=-1):
    return jax.nn.softmax(x, axis=axis)

def _gelu(x):
    return jax.nn.gelu(x, approximate=True)

def _silu(x):
    return jax.nn.silu(x)

def _sigmoid(x):
    return jax.nn.sigmoid(x)

def _layernorm(x, axis=-1, eps=1e-05):
    m = jnp.mean(x, axis=axis, keepdims=True)
    v = jnp.var(x, axis=axis, keepdims=True)
    return (x - m) / jnp.sqrt(v + eps)

def _scatter_add(tgt, idx, src, axis=0):
    return tgt.at[idx].add(src)

def _segment_sum(src, seg, n):
    return jax.ops.segment_sum(src, seg, n)
kernel_name = 'mk_adj_resnorm_d4_adj_r2_32558c'

def setup_inputs(seed: int=0):
    np.random.seed(seed)
    _w = jnp.asarray

    def _rec_inputs():
        import jax
        import jax.numpy as jnp
        _gk = jax.random.key(seed)
        x = -0.000929 + 1 * jax.random.normal(jax.random.fold_in(_gk, 1), (8, 1024, 64), jnp.float32)
        _w = (1.0 + jnp.arange(1024, dtype=jnp.float32)) ** (-0.5)
        _w = _w / _w.mean()
        _pij = jnp.clip(0.00195312 * _w[:, None] * _w[None, :], 0.0, 1.0)
        _a = jax.random.uniform(jax.random.fold_in(_gk, 2), (1024, 1024)) < _pij
        _a = jnp.logical_or(_a, jnp.eye(1024, dtype=bool))
        _af = _a.astype(jnp.float32)
        adj = _af
        return (x, adj)
    x, adj = _rec_inputs()

    def _L0_gnn_setup():
        import jax, jax.numpy as jnp
        import numpy as np
        NEG = -1000000000.0
        key = jax.random.key(seed)
        ks = jax.random.split(key, 14)
        B, N, E, NF, NH = (8, 1024, 64, 64, 64)
        x = jax.random.normal(ks[0], (B, N, NF), dtype=jnp.float32)
        base = jax.nn.one_hot(jax.random.randint(ks[1], (N,), 0, E), E, dtype=jnp.float32)
        extra = (jax.random.uniform(ks[2], (N, E)) < 0.03).astype(jnp.float32)
        H = jnp.clip(base + extra, 0.0, 1.0)
        adj = (jax.random.uniform(ks[3], (N, N)) < 0.01).astype(jnp.float32)
        adj = jnp.clip(adj + jnp.eye(N, dtype=jnp.float32), 0.0, 1.0)
        s_in = 1.0 / np.sqrt(NF)
        s_h = 1.0 / np.sqrt(NH)
        W = jax.random.normal(ks[4], (NF, NH), dtype=jnp.float32) * s_in
        W_ind = jax.random.normal(ks[5], (NF, NH), dtype=jnp.float32) * s_in
        a_node = jax.random.normal(ks[6], (NH,), dtype=jnp.float32) * s_h
        a_gn = jax.random.normal(ks[7], (NH,), dtype=jnp.float32) * s_h
        a_ge = jax.random.normal(ks[8], (NH,), dtype=jnp.float32) * s_h
        fcW = jax.random.normal(ks[9], (NH, 2 * NH), dtype=jnp.float32) * s_h
        fcb = jnp.zeros((2 * NH,), dtype=jnp.float32)
        av = jax.random.normal(ks[10], (2 * NH,), dtype=jnp.float32) / np.sqrt(2 * NH)
        return {'x': x, 'H': H, 'adj': adj, 'nhid': NH, 'W': W, 'W_ind': W_ind, 'a_node': a_node, 'a_gn': a_gn, 'a_ge': a_ge, 'fcW': fcW, 'fcb': fcb, 'av': av}
    _L0_gnn_all = _L0_gnn_setup()
    _L0_gnn_in = {k: v for k, v in _L0_gnn_all.items() if k in ('H', 'W', 'W_ind', 'a_node', 'a_gn', 'a_ge', 'fcW', 'fcb', 'av')}
    del _L0_gnn_all

    def _L1_gnn_setup():
        import jax, jax.numpy as jnp
        import numpy as np
        B, N, C_IN, C_OUT, EMBED = (8, 1024, 64, 64, 16)

        def _sym_norm_softmax_adj(W):
            Wn = W + 0.5 * jnp.eye(N, dtype=W.dtype)
            d = 1.0 / jnp.sum(Wn, axis=1)
            sd = jnp.sqrt(d)
            A = sd[:, None] * Wn * sd[None, :]
            return jax.nn.softmax(A, axis=1)
        key = jax.random.key(seed)
        ks = jax.random.split(key, 8)
        x = jax.random.normal(ks[0], (B, N, C_IN), dtype=jnp.float32)
        adj_raw = jax.random.uniform(ks[1], (N, N), dtype=jnp.float32)
        adj = _sym_norm_softmax_adj(adj_raw)
        node_embeddings = jax.random.normal(ks[2], (N, EMBED), dtype=jnp.float32)
        s = 1.0 / np.sqrt(C_IN)
        Wq = jax.random.uniform(ks[3], (C_IN, C_OUT), jnp.float32, -s, s)
        bq = jax.random.uniform(ks[4], (C_OUT,), jnp.float32, -s, s)
        Wk = jax.random.uniform(ks[5], (C_IN, C_OUT), jnp.float32, -s, s)
        bk = jax.random.uniform(ks[6], (C_OUT,), jnp.float32, -s, s)
        Wv = jax.random.uniform(ks[7], (C_IN, C_OUT), jnp.float32, -s, s)
        return {'x': x, 'adj': adj, 'node_embeddings': node_embeddings, 'Wq': Wq, 'bq': bq, 'Wk': Wk, 'bk': bk, 'Wv': Wv}
    _L1_gnn_all = _L1_gnn_setup()
    _L1_gnn_in = {k: v for k, v in _L1_gnn_all.items() if k in ('node_embeddings', 'Wq', 'bq', 'Wk', 'bk', 'Wv')}
    del _L1_gnn_all

    def _L2_gnn_setup():
        import jax, jax.numpy as jnp
        import numpy as np
        key = jax.random.key(seed)
        ks = jax.random.split(key, 5)
        B, N, IN, OUT, K, D = (32, 1024, 64, 64, 3, 16)
        x = jax.random.normal(ks[0], (B, N, IN), dtype=jnp.float32)
        A = jax.random.uniform(ks[1], (N, N), dtype=jnp.float32)
        A = A / jnp.sum(A, axis=-1, keepdims=True)
        embedding = jax.random.normal(ks[2], (N, D), dtype=jnp.float32) * 0.3
        weight = jax.random.normal(ks[3], (D, K, IN, OUT), dtype=jnp.float32) * 0.1
        bias = jax.random.normal(ks[4], (D, OUT), dtype=jnp.float32) * 0.1
        return {'x': x, 'A': A, 'embedding': embedding, 'weight': weight, 'bias': bias}
    _L2_gnn_all = _L2_gnn_setup()
    _L2_gnn_in = {k: v for k, v in _L2_gnn_all.items() if k in ('embedding', 'weight', 'bias')}
    del _L2_gnn_all

    def _L3_gnn_setup():
        import jax, jax.numpy as jnp
        import numpy as np
        B, N, F, L = (4, 4096, 64, 2)
        key = jax.random.key(seed)
        k1, k2, k3 = jax.random.split(key, 3)
        x = jax.random.normal(k1, (B, N, F), dtype=jnp.float32)
        net_params = jax.random.normal(k2, (L * F * F,), dtype=jnp.float32)
        A = jax.random.normal(k3, (N, N), dtype=jnp.float32)
        return {'x': x, 't': 0, 'net_params': net_params, 'A': A}
    _L3_gnn_all = _L3_gnn_setup()
    _L3_gnn_in = {k: v for k, v in _L3_gnn_all.items() if k in ('net_params',)}
    del _L3_gnn_all
    return {'x': x, 'adj': adj, 'L0_gnn_H': _L0_gnn_in['H'], 'L0_gnn_W': _L0_gnn_in['W'], 'L0_gnn_W_ind': _L0_gnn_in['W_ind'], 'L0_gnn_a_node': _L0_gnn_in['a_node'], 'L0_gnn_a_gn': _L0_gnn_in['a_gn'], 'L0_gnn_a_ge': _L0_gnn_in['a_ge'], 'L0_gnn_fcW': _L0_gnn_in['fcW'], 'L0_gnn_fcb': _L0_gnn_in['fcb'], 'L0_gnn_av': _L0_gnn_in['av'], 'L1_gnn_node_embeddings': _L1_gnn_in['node_embeddings'], 'L1_gnn_Wq': _L1_gnn_in['Wq'], 'L1_gnn_bq': _L1_gnn_in['bq'], 'L1_gnn_Wk': _L1_gnn_in['Wk'], 'L1_gnn_bk': _L1_gnn_in['bk'], 'L1_gnn_Wv': _L1_gnn_in['Wv'], 'L2_gnn_embedding': _L2_gnn_in['embedding'], 'L2_gnn_weight': _L2_gnn_in['weight'], 'L2_gnn_bias': _L2_gnn_in['bias'], 'L3_gnn_net_params': _L3_gnn_in['net_params']}

def reference(x, adj, L0_gnn_H, L0_gnn_W, L0_gnn_W_ind, L0_gnn_a_node, L0_gnn_a_gn, L0_gnn_a_ge, L0_gnn_fcW, L0_gnn_fcb, L0_gnn_av, L1_gnn_node_embeddings, L1_gnn_Wq, L1_gnn_bq, L1_gnn_Wk, L1_gnn_bk, L1_gnn_Wv, L2_gnn_embedding, L2_gnn_weight, L2_gnn_bias, L3_gnn_net_params):
    import jax
    import jax.numpy as jnp

    def _L0_gnn_ref(x, H, adj, nhid, W, W_ind, a_node, a_gn, a_ge, fcW, fcb, av):
        import jax, jax.numpy as jnp
        import numpy as np
        NEG = -1000000000.0
        h = x @ W
        maskEN = H.T
        s = jax.nn.leaky_relu(h @ a_node, 0.2)
        logits = jnp.where(maskEN[None, :, :] > 0, s[:, None, :], NEG)
        alpha = jax.nn.softmax(logits, axis=-1)
        agg = jnp.einsum('ben,bnf->bef', alpha, h)
        beta = jax.nn.sigmoid((h @ a_gn)[:, None, :] + (agg @ a_ge)[:, :, None])
        all_he = beta[..., None] * h[:, None, :, :] + (1.0 - beta[..., None]) * agg[:, :, None, :]
        deg = jnp.maximum(adj.sum(-1), 1.0)[:, None]
        industry = jnp.einsum('nm,bmf->bnf', adj / deg, x @ W_ind)
        all_he = jax.nn.elu(all_he)
        he = jax.nn.elu(agg)

        def attn_scores(f):
            return jnp.tanh(f @ fcW + fcb) @ av
        se = attn_scores(he)
        logits2 = jnp.where(H[None, :, :] > 0, se[:, None, :], NEG)
        coefs1 = jax.nn.softmax(logits2, axis=-1)
        g = jnp.einsum('bne,benf->bnf', coefs1, all_he)
        pair = jnp.stack([industry, g], axis=2)
        coefs2 = jax.nn.softmax(attn_scores(pair), axis=-1)
        out = jnp.einsum('bnk,bnkf->bnf', coefs2, pair)
        return out

    def _L1_gnn_ref(x, adj, node_embeddings, Wq, bq, Wk, bk, Wv):
        import jax, jax.numpy as jnp
        import numpy as np
        B, N, C_IN, C_OUT, EMBED = (8, 1024, 64, 64, 16)

        def _sym_norm_softmax_adj(W):
            Wn = W + 0.5 * jnp.eye(N, dtype=W.dtype)
            d = 1.0 / jnp.sum(Wn, axis=1)
            sd = jnp.sqrt(d)
            A = sd[:, None] * Wn * sd[None, :]
            return jax.nn.softmax(A, axis=1)
        Q = x @ Wq + bq
        K = x @ Wk + bk
        V = x @ Wv
        score = jnp.einsum('bnc,bmc->bnm', Q, K)
        score = jax.nn.softmax(score, axis=1)
        score = jnp.einsum('bnm,mc->bnc', score, adj)
        out = jnp.einsum('bnm,bmc->bnc', score, V)
        return jax.nn.relu(out)

    def _L2_gnn_ref(x, A, embedding, weight, bias):
        import jax, jax.numpy as jnp
        import numpy as np
        K = weight.shape[1]
        N = A.shape[-2]
        w = jnp.einsum('nd,dkio->nkio', embedding, weight)
        b = jnp.einsum('nd,do->no', embedding, bias)
        As = [jnp.eye(N, dtype=x.dtype)]
        if K > 1:
            As.append(A)
        for _ in range(2, K):
            As.append(2.0 * (A @ As[-1]) - As[-2])
        A_stack = jnp.stack(As, 0)
        x_g = jnp.einsum('knm,bmc->bnkc', A_stack, x)
        out = jnp.einsum('bnki,nkio->bno', x_g, w)
        return out + b

    def _L3_gnn_ref(x, t, net_params, A):
        import jax, jax.numpy as jnp
        import numpy as np
        B, N, F, L = (4, 4096, 64, 2)
        weights = net_params.reshape(L, F, F)
        z = x.reshape(-1, A.shape[1], F)
        for i in range(L):
            h = jnp.einsum('mn,bnf->bmf', A, z)
            z = jnp.einsum('bmf,fg->bmg', h, weights[i])
            z = jax.nn.relu(z)
        return z
    x = _layernorm(x + _L0_gnn_ref(x, L0_gnn_H, adj, 64, L0_gnn_W, L0_gnn_W_ind, L0_gnn_a_node, L0_gnn_a_gn, L0_gnn_a_ge, L0_gnn_fcW, L0_gnn_fcb, L0_gnn_av), axis=-1)
    x = _layernorm(x + _L1_gnn_ref(x, adj, L1_gnn_node_embeddings, L1_gnn_Wq, L1_gnn_bq, L1_gnn_Wk, L1_gnn_bk, L1_gnn_Wv), axis=-1)
    x = _layernorm(x + _L2_gnn_ref(x, adj, L2_gnn_embedding, L2_gnn_weight, L2_gnn_bias), axis=-1)
    x = _layernorm(x + _L3_gnn_ref(x, 0, L3_gnn_net_params, adj), axis=-1)
    return x

_drawn_inputs = setup_inputs


def setup_inputs(seed=0):
    import zlib

    import numpy as np

    out = dict(_drawn_inputs(seed))
    spreads = {'L0_gnn_fcb': (0.0, 0.8)}
    factors = {'L0_gnn_a_ge': 3.397, 'L1_gnn_bq': 8.0}
    for name, (base, spread) in spreads.items():
        noise = np.random.default_rng([zlib.crc32(name.encode()), seed]).standard_normal(out[name].shape)
        drawn = base * np.exp(spread * noise) if base else spread * noise
        out[name] = jnp.asarray(drawn.astype(out[name].dtype))
    for name, factor in factors.items():
        out[name] = (out[name] * factor).astype(out[name].dtype)
    return out
```

```python
from contextlib import ExitStack

import concourse.bass as bass
from concourse import mybir

F32 = mybir.dt.float32
BF16 = mybir.dt.bfloat16
I32 = mybir.dt.int32
ALU = mybir.AluOpType
ACT = mybir.ActivationFunctionType
AX = mybir.AxisListType

P = 128
B = 8
N = 1024
F = 64
E = 64
NT = N // P
BP = B // 2
BF = B * F
HALF = N // 2
D = 16
SLOTS = 4
QUADS = E // SLOTS
NEG = -1e9
BIG = 3e38
EPS = 1e-5

C_ID = 0
C_ID2 = C_ID + P
C_ONE = C_ID2 + F
C_UP = C_ONE + P
C_TRI = C_UP + P
C_STEP = C_TRI + NT + 1
C_RANK = C_STEP + QUADS
C_M1 = C_RANK + E + SLOTS
CW = C_M1 + 1

W_H = 0
W_IND = W_H + P
W_AN = W_IND + P
W_GN = W_AN + P
W_FC = W_GN + 2
W_FCB = W_FC + P
W_AV = W_FCB + 1
W_GE = W_AV + 1
W_Q = W_GE + F
W_K = W_Q + P
W_V = W_K + P
W_BQ = W_V + P
W_BK = W_BQ + 1
W_EMB = W_BK + 1
W_EMBT = W_EMB + NT * D
W_BIAS = W_EMBT + N
W_L3 = W_BIAS + F
WW = W_L3 + 2 * P


def program(nc, x_nat, x_tr, adj_tr, h_nat, h_tr, consts, weights, w01, w2, out):
    ctx = ExitStack()
    with ctx:
        def sb(name, shape, dt=F32):
            return ctx.enter_context(nc.sbuf_tensor(name, shape, dt))

        def sem(name):
            return ctx.enter_context(nc.semaphore(name))

        PS = ctx.enter_context(nc.psum_tensor("PS", [P, 8, 512], F32))

        adjT = sb("adjT", [P, NT, N])
        CN = sb("CN", [P, CW])
        WT = sb("WT", [P, WW])
        arena = sb("arena", [P, 9 * 4096])

        def node_major(slot):
            return arena[:, slot * 4096:(slot + 1) * 4096].rearrange("p (t c) -> p t c", t=NT)

        def feature_major(slot):
            return arena[:, slot * 4096:(slot + 1) * 4096].rearrange("p (q n) -> p q n", q=BP)

        ident = CN[:, C_ID:C_ID + P]
        ones = CN[:, C_ONE:C_ONE + P]

        def wt(at, n, rows=P):
            return WT[0:rows, at:at + n]

        def tile(t):
            return slice(t * P, (t + 1) * P)

        def groups(ap):
            return ap.rearrange("p (b f) -> p b f", f=F)

        def spread(ap, n=F):
            return ap.unsqueeze(2).broadcast_to([ap.shape[0], ap.shape[1], n])

        LN_ST = sb("LN_ST", [P, 64, 6])
        LN_A = sb("LN_A", [P, 64])
        LN_B = sb("LN_B", [P, 64])
        LN_V = sb("LN_V", [P, 64])
        LN_M = sb("LN_M", [P, 64])
        LN_Y = sb("LN_Y", [P, 64])
        ln_step = sem("ln_step")
        ln_count = [0]

        def layer_norm(dve, group, n, last):
            def link(ins):
                ln_count[0] += 1
                ins.then_inc(ln_step, 1)
                dve.wait_ge(ln_step, ln_count[0])

            for i in range(n):
                ins = dve.bn_stats(LN_ST[:, i, :], group(i)[0])
            link(ins)
            even, odd = LN_ST[:, 0:n, 1], LN_ST[:, 0:n, 4]
            a, b, v, m, y = (t[:, 0:n] for t in (LN_A, LN_B, LN_V, LN_M, LN_Y))
            dve.tensor_tensor(m, even, odd, ALU.add)
            dve.tensor_tensor(v, LN_ST[:, 0:n, 2], LN_ST[:, 0:n, 5], ALU.add)
            link(dve.tensor_tensor(a, even, odd, ALU.subtract))
            link(dve.scalar_tensor_tensor(b, a, 16.0, a, ALU.mult, ALU.mult))
            dve.tensor_scalar(m, m, 0.5, None, ALU.mult)
            link(dve.tensor_tensor(v, v, b, ALU.add))
            link(dve.tensor_scalar(v, v, 1.0 / F, EPS, ALU.mult, ALU.add))
            link(dve.tensor_scalar(a.bitcast(I32), v.bitcast(I32), 1, None, ALU.logical_shift_right))
            link(dve.tensor_scalar(y.bitcast(I32), a.bitcast(I32), -1.0, float(0x5F3759DF), ALU.mult, ALU.add))
            for _ in range(3):
                link(dve.scalar_tensor_tensor(a, v, -0.5, y, ALU.mult, ALU.mult))
                link(dve.tensor_tensor(b, a, y, ALU.mult))
                link(dve.scalar_tensor_tensor(y, b, 1.5, y, ALU.add, ALU.mult))
            for i in range(n):
                src, dst = group(i)
                ins = dve.tensor_scalar(dst, src, LN_M[:, i:i + 1], LN_Y[:, i:i + 1], ALU.subtract, ALU.mult)
            ins.then_inc(last, 1)

        XN = node_major(0)
        XT = feature_major(1)
        HP = node_major(2)
        XW = node_major(3)
        HT = feature_major(4)
        IND = node_major(5)
        EX = feature_major(6)
        ET = arena[:, 7 * 4096:8 * 4096].rearrange("p (t q c) -> p t q c", t=NT, q=BP)
        maskT = arena[:, 8 * 4096:8 * 4096 + N]
        limT = arena[:, 8 * 4096 + N:8 * 4096 + 2 * N]
        effT = arena[:, 8 * 4096 + 2 * N:8 * 4096 + 3 * N]
        rankT = sb("rankT", [P, N])
        hN = arena[:, 8 * 4096 + 3 * N:8 * 4096 + 3 * N + NT * E].rearrange("p (t e) -> p t e", e=E)
        limN = arena[:, 8 * 4096 + 3 * N + NT * E:9 * 4096].rearrange("p (t e) -> p t e", e=E)
        degH = sb("degH", [P, NT])
        none = sb("none", [P, NT])
        low = sb("low", [P, NT])
        degE = sb("degE", [P, NT])
        kmx = sb("kmx", [NT, 1])
        kst = sb("kst", [NT, QUADS])
        kq = sb("kq", [NT, 1])
        first_i = sb("first_i", [1, NT + 1], I32)
        nmx = sb("nmx", [P, BP])
        Zs = sb("Zs", [P, BP])
        rZ = sb("rZ", [P, BP])
        rdg = sb("rdg", [P, NT])
        HM = sb("HM", [P, NT, 17])
        AG = arena[:, 6144:6400].rearrange("p (q f) -> p q f", f=F)
        AGM = arena[:, 6400:6656].rearrange("p (q f) -> p q f", f=F)
        AEX = arena[:, 6656:6912].rearrange("p (q f) -> p q f", f=F)
        HE = arena[:, 6912:7168].rearrange("p (q f) -> p q f", f=F)
        HET = arena[:, 7168:7424].rearrange("p (a c) -> p a c", c=P)
        THE = arena[:, 7424:7936].rearrange("p (a c) -> p a c", c=P)
        ae = sb("ae", [P, BP])
        SM = sb("SM", [P, 17])
        AGBD = sb("AGBD", [P, B, F])
        DG = arena[:, 4096:4096 + B * E].rearrange("p (b e) -> p b e", e=E)
        SEB = arena[:, 4096 + B * E:4096 + 2 * B * E].rearrange("p (b e) -> p b e", e=E)
        LGM = arena[:, 4096 + 2 * B * E:4096 + 4 * B * E].rearrange("p (a b e) -> p a b e", a=2, e=E)
        zero16 = sb("zero16", [P, 512], BF16)

        consts_in, weights_in, xT_in, x_in, hT_in, hN_in, adj_in = (
            sem(s) for s in ("consts_in", "weights_in", "xT_in", "x_in", "hT_in", "hN_in", "adj_in"))
        h_ready, h_out, xw_ready, xw_out = sem("h_ready"), sem("h_out"), sem("xw_ready"), sem("xw_out")
        hT_ready, hT_outA, hT_outD = sem("hT_ready"), sem("hT_outA"), sem("hT_outD")
        mask_ready, degB_ready, eff_ready, rank_ready = sem("mask_ready"), sem("degB_ready"), sem("eff_ready"), sem("rank_ready")
        rank_done = sem("rank_done")
        s_ready, s_copied, s_out, ex_max, ex_done = sem("s_ready"), sem("s_copied"), sem("s_out"), sem("ex_max"), sem("ex_done")
        hg_ready, hg_out = sem("hg_ready"), sem("hg_out")
        ind_ready, ind_scale, ind_out = sem("ind_ready"), sem("ind_scale"), sem("ind_out")
        et_ready, et_outA, et_outD = sem("et_ready"), sem("et_outA"), sem("et_outD")
        rz_ready, agg_ready, agg_out, am_ready, aex_done, he_ready = (
            sem(s) for s in ("rz_ready", "agg_ready", "agg_out", "am_ready", "aex_done", "he_ready"))
        heT_ready, heT_out, fce_ready, the_done, se_ready, sm_ready, seB_ready, seB_out = (
            sem(s) for s in ("heT_ready", "heT_out", "fce_ready", "the_done", "se_ready", "sm_ready", "seB_ready", "seB_out"))
        zero_set, dstep, degT_ready, kq_ready, first_ready, sl = (
            sem(s) for s in ("zero_set", "dstep", "degT_ready", "kq_ready", "first_ready", "sl"))
        dn = [0]

        with nc.Block() as block:
            @block.sync
            def _(sp):
                for q in range(BP):
                    sp.dma_start(XT[:, q, :], x_tr[q * P:(q + 1) * P, :]).then_inc(xT_in, 16)
                for t in range(NT):
                    sp.dma_start(adjT[:, t, :], adj_tr[t * P:(t + 1) * P, :]).then_inc(adj_in, 16)
                sp.dma_start(XN.rearrange("p t (b f) -> p t b f", f=F),
                             x_nat.rearrange("(t p) b f -> p t b f", p=P)).then_inc(x_in, 16)
                sp.wait_ge(x_in, 16)

            @block.gpsimd
            def _(pool):
                pool.memset(SM[:, :], 0.0).then_inc(sl, 1)
                pool.memset(AGBD[:, :, :], 0.0).then_inc(zero_set, 1)
                pool.memset(HM[:, :, :], 0.0).then_inc(zero_set, 1)
                pool.memset(zero16[:, :], 0.0).then_inc(zero_set, 1)
                pool.wait_ge(sl, 1)
                pool.memset(SM[0:64, 16:17], 1.0).then_inc(zero_set, 1)

            @block.scalar
            def _(act):
                act.dma_start(CN[:, :], consts).then_inc(consts_in, 16)
                act.dma_start(WT[:, :], weights).then_inc(weights_in, 16)
                act.dma_start(maskT[0:64, :], h_tr).then_inc(hT_in, 16)
                act.dma_start(maskT[64:128, :], h_tr).then_inc(hT_in, 16)
                act.dma_start(hN, h_nat.rearrange("(t p) e -> p t e", p=P)).then_inc(hN_in, 16)
                for t in range(NT):
                    act.wait_ge(h_ready, t + 1)
                    act.activation(HP[:, t, :], PS[:, (2 * t) % 4, :], ACT.Copy, bias=1.0).then_inc(h_out, 1)
                for q in range(BP):
                    act.wait_ge(hT_ready, 2 * q + 1)
                    act.activation(HT[:, q, 0:HALF], PS[:, 4 + (2 * q) % 4, :], ACT.Copy).then_inc(hT_outA, 1)
                for q in range(BP):
                    for half in range(2):
                        u = 2 * q + half
                        act.wait_ge(s_ready, u + 1)
                        act.activation(EX[:, q, half * HALF:(half + 1) * HALF], PS[:, 4 + u % 4, :],
                                       ACT.Copy).then_inc(s_copied, 1)
                    if q >= 1:
                        act.wait_ge(ex_max, q)
                        act.activation(EX[:, q - 1, :], EX[:, q - 1, :], ACT.Exp, bias=nmx[:, q - 1:q],
                                       accum_out=Zs[:, q - 1:q]).then_inc(ex_done, 1)
                act.wait_ge(ex_max, BP)
                act.activation(EX[:, 3, :], EX[:, 3, :], ACT.Exp, bias=nmx[:, 3:4],
                               accum_out=Zs[:, 3:4]).then_inc(ex_done, 1)
                act.wait_ge(hg_ready, 1)
                act.wait_ge(zero_set, 2)
                act.activation(HM[:, :, 0:B], PS[:, 0, 0:NT * B].rearrange("p (t b) -> p t b", b=B),
                               ACT.Copy, scale=0.5).then_inc(hg_out, 1)

                def industry_out(t):
                    act.wait_ge(ind_scale, t + 1)
                    act.activation(IND[:, t, :], PS[:, 2 + t % 2, :], ACT.Copy,
                                   scale=rdg[:, t:t + 1]).then_inc(ind_out, 1)

                for t in range(3):
                    industry_out(t)
                for q in range(BP):
                    act.wait_ge(et_ready, q + 1)
                    act.activation(ET[:, 0:4, q, :], PS[:, 4 + 2 * (q % 2), :].rearrange("p (t c) -> p t c", c=P),
                                   ACT.Copy).then_inc(et_outA, 1)
                act.wait_ge(agg_ready, 1)
                act.wait_ge(rz_ready, 1)
                for q in range(BP):
                    for par in range(2):
                        r = slice(64 * par, 64 * par + 64)
                        ins = act.activation(AG[r, q, :], PS[r, 4, q * P + 64 * par:q * P + 64 * par + 64],
                                             ACT.Copy, scale=rZ[r, q:q + 1])
                ins.then_inc(agg_out, 1)
                act.wait_ge(agg_out, 1)
                act.activation(AEX[:, :, :], AG[:, :, :], ACT.Exp, bias=CN[:, C_M1:C_M1 + 1]).then_inc(aex_done, 1)
                industry_out(3)
                industry_out(4)
                act.wait_ge(heT_ready, 1)
                act.activation(HET[:, :, :], PS[:, 5, 0:2 * P].rearrange("p (a c) -> p a c", c=P),
                               ACT.Copy).then_inc(heT_out, 1)
                industry_out(5)
                act.wait_ge(fce_ready, 1)
                for par in range(2):
                    act.activation(THE[:, par:BP:2, :], PS[:, 6 + par, 0:2 * P].rearrange("p (a c) -> p a c", c=P), ACT.Tanh,
                                   bias=wt(W_FCB, 1)).then_inc(the_done, 1)
                industry_out(6)
                act.wait_ge(seB_ready, 1)
                act.activation(SEB[:, :, :], PS[:, 5, :].rearrange("p (b e) -> p b e", e=E), ACT.Copy).then_inc(seB_out, 1)
                industry_out(7)

            @block.vector
            def _(dve):
                def link(ins):
                    dn[0] += 1
                    ins.then_inc(dstep, 1)
                    dve.wait_ge(dstep, dn[0])

                dve.wait_ge(hT_in, 32)
                link(dve.tensor_scalar(maskT, maskT, 0.0, None, ALU.is_gt))
                dve.tensor_scalar(limT, maskT, BIG, NEG, ALU.mult, ALU.add).then_inc(mask_ready, 1)

                def xw_out_step(t):
                    dve.wait_ge(xw_ready, t + 1)
                    dve.tensor_copy(XW[:, t, :], PS[:, (2 * t + 1) % 4, :]).then_inc(xw_out, 1)

                for t in range(NT):
                    xw_out_step(t)
                for q in range(BP):
                    dve.wait_ge(hT_ready, 2 * q + 2)
                    dve.tensor_copy(HT[:, q, HALF:N], PS[:, 4 + (2 * q + 1) % 4, :]).then_inc(hT_outD, 1)
                dve.wait_ge(degB_ready, 1)
                for half in range(2):
                    s = slice(half * HALF, (half + 1) * HALF)
                    ins = dve.scalar_tensor_tensor(effT[:, s], PS[:, half, :], 0.0, maskT[:, s], ALU.is_equal, ALU.max)
                ins.then_inc(eff_ready, 1)
                for q in range(BP):
                    for half in range(2):
                        u = 2 * q + half
                        s = slice(half * HALF, (half + 1) * HALF)
                        dve.wait_ge(s_copied, u + 1)
                        ins = dve.scalar_tensor_tensor(EX[:, q, s], PS[:, 4 + u % 4, :], 0.2, EX[:, q, s],
                                                       ALU.mult, ALU.max).then_inc(s_out, 1)
                    dve.wait_ge(s_out, 2 * q + 2)
                    link(dve.tensor_tensor(EX[:, q, :], EX[:, q, :], limT, ALU.min))
                    dve.tensor_reduce(nmx[:, q:q + 1], EX[:, q, :], AX.X, ALU.max, negate=True).then_inc(ex_max, 1)
                    if q == 0:
                        dve.wait_ge(rank_ready, 1)
                        dve.wait_ge(eff_ready, 1)
                        for half in range(2):
                            s = slice(half * HALF, (half + 1) * HALF)
                            ins = dve.tensor_tensor(rankT[:, s], PS[:, 2 + half, :], effT[:, s], ALU.mult)
                        ins.then_inc(rank_done, 1)

                dve.wait_ge(hN_in, 16)
                link(dve.tensor_scalar(hN, hN, 0.0, None, ALU.is_gt))
                dve.tensor_scalar(limN, hN, BIG, NEG, ALU.mult, ALU.add)
                link(dve.tensor_reduce(degH[:, :], hN, AX.X, ALU.add))
                link(dve.tensor_scalar(none[:, :], degH[:, :], 0.0, None, ALU.is_equal))
                dve.tensor_scalar(low[:, :], none[:, :], BIG, -BIG, ALU.mult, ALU.add)
                dve.scalar_tensor_tensor(degE[:, :], none[:, :], float(E), degH[:, :], ALU.mult, ALU.add).then_inc(degT_ready, 1)

                def industry_scale(t):
                    dve.wait_ge(ind_ready, t + 1)
                    link(dve.tensor_scalar(rdg[:, t:t + 1], PS[:, t % 2, 0:1], 1.0, None, ALU.max))
                    dve.reciprocal(rdg[:, t:t + 1], rdg[:, t:t + 1]).then_inc(ind_scale, 1)

                dve.wait_ge(ex_done, BP)
                dve.reciprocal(rZ[:, :], Zs[:, :]).then_inc(rz_ready, 1)
                for t in range(3):
                    industry_scale(t)
                for q in range(BP):
                    dve.wait_ge(et_ready, q + 1)
                    dve.tensor_copy(ET[:, 4:8, q, :], PS[:, 5 + 2 * (q % 2), :].rearrange("p (t c) -> p t c", c=P)).then_inc(et_outD, 1)
                dve.wait_ge(kq_ready, 1)
                link(dve.tensor_reduce(kmx[:, :], PS[0:NT, 5, 0:P], AX.X, ALU.max))
                link(dve.tensor_scalar(kst[:, :], CN[0:NT, C_STEP:C_STEP + QUADS], kmx[:, 0:1], None, ALU.is_lt))
                dve.tensor_reduce(kq[:, :], kst[:, :], AX.X, ALU.add).then_inc(kq_ready, 1)
                dve.wait_ge(agg_out, 1)
                link(dve.tensor_scalar(AGM[:, :, :], AG[:, :, :], -1.0, None, ALU.add))
                dve.wait_ge(aex_done, 1)
                link(dve.tensor_scalar(AEX[:, :, :], AEX[:, :, :], 1.0, -1.0, ALU.min, ALU.add))
                dve.tensor_tensor(HE[:, :, :], AEX[:, :, :], AGM[:, :, :], ALU.max).then_inc(he_ready, 1)
                link(dve.tensor_tensor(AGM[:, :, :], AGM[:, :, :],
                                       wt(W_GE, F).unsqueeze(1).broadcast_to([P, BP, F]), ALU.mult))
                link(dve.tensor_reduce(ae[:, :], AGM[:, :, :], AX.X, ALU.add))
                dve.wait_ge(zero_set, 4)
                for par in range(2):
                    r = slice(64 * par, 64 * par + 64)
                    dve.tensor_scalar(SM[r, par:B:2], ae[r, :], 0.5, None, ALU.mult)
                    dve.tensor_copy(AGBD[r, par:B:2, :], AG[r, :, :])
                industry_scale(3)
                industry_scale(4)
                dve.wait_ge(kq_ready, 3)
                dve.tensor_copy(first_i[:, :], PS[0:1, 4, 0:NT + 1]).then_inc(first_ready, 1)
                industry_scale(5)
                dve.wait_ge(se_ready, 1)
                for par in range(2):
                    r = slice(64 * par, 64 * par + 64)
                    ins = dve.tensor_copy(SM[r, B + par:2 * B:2], PS[r, 5, 0:BP])
                link(ins)
                dve.tensor_tensor(DG[:, :, :], CN[:, C_ID2:C_ID2 + E].unsqueeze(1).broadcast_to([P, B, E]),
                                  spread(SM[:, B:2 * B], E), ALU.mult).then_inc(sm_ready, 1)
                industry_scale(6)
                dve.wait_ge(seB_out, 1)
                for t in range(NT):
                    link(dve.tensor_tensor(LGM[:, t % 2, :, :], SEB[:, :, :],
                                           limN[:, t:t + 1, :].broadcast_to([P, B, E]), ALU.min))
                    dve.tensor_reduce(HM[:, t, B:2 * B], LGM[:, t % 2, :, :], AX.X, ALU.max, negate=True)
                    if t == 0:
                        industry_scale(7)

            @block.tensor
            def _(pe):
                pe.wait_ge(weights_in, 16)
                pe.wait_ge(xT_in, 16 * BP)
                for t in range(NT):
                    for which, at in ((0, W_H), (1, W_IND)):
                        if t >= 2:
                            pe.wait_ge(xw_out if which else h_out, t - 1)
                        for q in range(BP):
                            ins = pe.matmul(PS[:, (2 * t + which) % 4, tile(q)], XT[:, q, tile(t)], wt(at, P),
                                            start=True, stop=True)
                        ins.then_inc(xw_ready if which else h_ready, 1)
                for q in range(BP):
                    for half in range(2):
                        u = 2 * q + half
                        if u >= 4:
                            pe.wait_ge(hT_outD if half else hT_outA, (u - 4) // 2 + 1)
                        pe.matmul(PS[:, 4 + u % 4, :], wt(W_H, P), XT[:, q, half * HALF:(half + 1) * HALF],
                                  start=True, stop=True).then_inc(hT_ready, 1)
                pe.wait_ge(consts_in, 16)
                pe.wait_ge(mask_ready, 1)
                pe.wait_ge(h_out, NT)
                for half in range(2):
                    ins = pe.matmul(PS[:, half, :], CN[0:64, C_ONE:C_ONE + P], maskT[0:64, half * HALF:(half + 1) * HALF],
                                    start=True, stop=True)
                ins.then_inc(degB_ready, 1)
                pe.wait_ge(hT_outA, BP)
                pe.wait_ge(hT_outD, BP)

                def node_scores(q):
                    for half in range(2):
                        u = 2 * q + half
                        if u >= 4:
                            pe.wait_ge(s_out, u - 3)
                        pe.matmul(PS[:, 4 + u % 4, :], wt(W_AN, P), HT[:, q, half * HALF:(half + 1) * HALF],
                                  start=True, stop=True).then_inc(s_ready, 1)

                node_scores(0)
                node_scores(1)
                pe.wait_ge(eff_ready, 1)
                pe.wait_ge(xw_out, NT)
                for half in range(2):
                    ins = pe.matmul(PS[:, 2 + half, :], CN[0:64, C_UP:C_UP + P], effT[0:64, half * HALF:(half + 1) * HALF],
                                    start=True, stop=True)
                ins.then_inc(rank_ready, 1)
                for t in range(NT):
                    for q in range(BP):
                        ins = pe.matmul(PS[:, 0, t * B + 2 * q:t * B + 2 * q + 2], HT[:, q, tile(t)], wt(W_GN, 2),
                                        start=True, stop=True)
                ins.then_inc(hg_ready, 1)
                node_scores(2)
                node_scores(3)

                def industry(t):
                    if t == 0:
                        pe.wait_ge(rank_done, 1)
                        pe.wait_ge(hg_out, 1)
                        pe.wait_ge(adj_in, 16 * NT)
                    if t >= 2:
                        pe.wait_ge(ind_out, t - 1)
                    for m in range(NT):
                        pe.matmul(PS[:, 2 + t % 2, :], adjT[:, m, tile(t)], XW[:, m, :], start=(m == 0), stop=(m == NT - 1))
                        ins = pe.matmul(PS[:, t % 2, 0:1], adjT[:, m, tile(t)], CN[:, C_ONE:C_ONE + 1],
                                        start=(m == 0), stop=(m == NT - 1))
                    ins.then_inc(ind_ready, 1)

                for t in range(3):
                    industry(t)
                pe.wait_ge(s_out, 2 * BP)
                for q in range(BP):
                    pe.wait_ge(ex_done, q + 1)
                    if q >= 2:
                        pe.wait_ge(et_outA, q - 1)
                        pe.wait_ge(et_outD, q - 1)
                    for t in range(NT):
                        ins = pe.transpose(PS[:, 4 + 2 * (q % 2) + t // 4, (t % 4) * P:(t % 4 + 1) * P],
                                           EX[:, q, tile(t)], ident)
                    ins.then_inc(et_ready, 1)
                pe.wait_ge(et_outA, BP)
                pe.wait_ge(et_outD, BP)
                for q in range(BP):
                    for t in range(NT):
                        ins = pe.matmul(PS[:, 4, tile(q)], ET[:, t, q, :], HP[:, t, tile(q)],
                                        start=(t == 0), stop=(t == NT - 1))
                ins.then_inc(agg_ready, 1)
                pe.wait_ge(degT_ready, 1)
                pe.transpose(PS[0:NT, 5, 0:P], degE[:, :], ident).then_inc(kq_ready, 1)
                industry(3)
                pe.wait_ge(kq_ready, 2)
                pe.wait_ge(agg_out, 1)
                pe.matmul(PS[0:1, 4, 0:NT + 1], kq[:, :], CN[0:NT, C_TRI:C_TRI + NT + 1], start=True, stop=True).then_inc(kq_ready, 1)
                industry(4)
                pe.wait_ge(he_ready, 1)
                for a in range(2):
                    ins = pe.transpose(PS[:, 5, tile(a)], HE[:, 2 * a:2 * a + 2, :].rearrange("p a f -> p (a f)"), ident)
                ins.then_inc(heT_ready, 1)
                industry(5)
                pe.wait_ge(heT_out, 1)
                for q in range(BP):
                    r = slice(64 * (q % 2), 64 * (q % 2) + 64)
                    ins = pe.matmul(PS[:, 6 + q % 2, tile(q // 2)], WT[r, W_FC:W_FC + P], HET[r, q // 2, :], start=True, stop=True)
                ins.then_inc(fce_ready, 1)
                pe.wait_ge(the_done, 2)
                for q in range(BP):
                    ins = pe.matmul(PS[:, 5, q:q + 1], THE[:, q, :], wt(W_AV, 1), start=True, stop=True)
                ins.then_inc(se_ready, 1)
                industry(6)
                pe.wait_ge(sm_ready, 1)
                pe.matmul(PS[:, 5, :], ones, DG[:, :, :].rearrange("p b e -> p (b e)"), start=True, stop=True).then_inc(seB_ready, 1)
                industry(7)

        GN = node_major(4)
        SEL = arena[:, 7 * 4096:7 * 4096 + SLOTS * P].rearrange("p (s c) -> p s c", c=P)
        TS = sb("TS", [P, SLOTS, 17])
        LG = sb("LG", [P, SLOTS, B])
        TH = sb("TH", [P, SLOTS, B])
        XC = sb("XC", [P, SLOTS, B])
        BE = sb("BE", [P, SLOTS, B])
        CC = sb("CC", [P, SLOTS, B])
        ZQ = sb("ZQ", [P, B])
        ZN = sb("ZN", [P, 2, B])
        S0 = arena[:, 6 * 4096:6 * 4096 + SLOTS * BF].rearrange("p (s c) -> p s c", c=BF)
        S1 = arena[:, 6 * 4096 + SLOTS * BF:7 * 4096].rearrange("p (s c) -> p s c", c=BF)
        POOLED = 2
        sel_ready, small_ready, gath_ready, ts_ready, lg_ready, th_ready, xc_ready, be_ready, cc_ready = (
            sem(s) for s in ("sel_ready", "small_ready", "gath_ready", "ts_ready", "lg_ready", "th_ready",
                             "xc_ready", "be_ready", "cc_ready"))
        d_ready, m_ready, z_ready, e_ready, t_ready, wp_ready, wd_ready, acc_done, g_done, zq_step, z_init = (
            sem(s) for s in ("d_ready", "m_ready", "z_ready", "e_ready", "t_ready", "wp_ready", "wd_ready",
                             "acc_done", "g_done", "zq_step", "z_init"))

        def first_turns(eng):
            return [eng.value_load(first_i[0:1, t:t + 1], min_val=0, max_val=NT * QUADS) for t in range(NT + 1)]

        with nc.Block() as block:
            @block.tensor
            def _(pe):
                first = first_turns(pe)
                for t in range(NT):
                    acc = PS[:, 5 + t % 2, :]
                    if t >= 2:
                        pe.wait_ge(g_done, t - 1)
                    pe.matmul(acc, zero16[:, 0:P], zero16[:, :], start=True, stop=False, skip_group_check=True)
                    if t == 0:
                        for s in range(SLOTS):
                            pe.matmul(PS[:, 7, 0:8], zero16[:, 0:P], zero16[:, 0:8], start=True, stop=True).then_inc(acc_done, 1)
                    with pe.Fori(first[t], first[t + 1]) as j:
                        for s in range(SLOTS):
                            pe.wait_ge(sel_ready, SLOTS * j + (s + 1))
                            ins = pe.matmul(PS[:, 4, s * 17:(s + 1) * 17], SEL[:, s, :], SM[:, :], start=True, stop=True)
                            if s == SLOTS - 1:
                                ins.then_inc(small_ready, 1)
                        for s in range(SLOTS):
                            pe.matmul(PS[:, s, :], SEL[:, s, :], AGBD[:, :, :].rearrange("p b f -> p (b f)"),
                                      start=True, stop=True).then_inc(gath_ready, 1)
                        for s in range(SLOTS):
                            if s < POOLED:
                                pe.wait_ge(wp_ready, POOLED * j + (s + 1))
                            else:
                                pe.wait_ge(wd_ready, (SLOTS - POOLED) * j + (s - POOLED + 1))
                            pe.matmul(acc, ident, S0[:, s, :], start=False, stop=True,
                                      skip_group_check=True).then_inc(acc_done, 1)

            @block.vector
            def _(dve):
                first = first_turns(dve)
                for t in range(NT):
                    dve.memset(ZN[:, t % 2, :], 0.0).then_inc(z_init, 1)
                    dve.wait_ge(z_init, t + 1)
                    with dve.Fori(first[t], first[t + 1]) as j:
                        k = nc.s_assert_within(SLOTS * (j - first[t]), 0, E - SLOTS, skip_runtime_bounds_check_because=
                                               "a tile takes at most E / SLOTS turns")
                        for s in range(SLOTS):
                            dve.tensor_scalar(SEL[:, s, :], rankT[:, tile(t)], CN[:, bass.ds(C_RANK + s + k, 1)],
                                              None, ALU.is_equal).then_inc(sel_ready, 1)
                        dve.wait_ge(small_ready, j + 1)
                        dve.tensor_tensor(TS[:, :, :], PS[:, 4, 0:SLOTS * 17].rearrange("p (s c) -> p s c", c=17),
                                          HM[:, t:t + 1, :].broadcast_to([P, SLOTS, 17]), ALU.add).then_inc(ts_ready, 1)

                        dve.wait_ge(ts_ready, j + 1)
                        dve.tensor_scalar(LG[:, :, :], TS[:, :, B:2 * B], low[:, t:t + 1], 0.0, ALU.max,
                                          ALU.min).then_inc(lg_ready, 1)

                        def diff(s):
                            dve.wait_ge(gath_ready, SLOTS * j + (s + 1))
                            dve.wait_ge(acc_done, SLOTS * j + (s + 1))
                            dve.tensor_tensor(S0[:, s, :], HP[:, t, :], PS[:, s, :], ALU.subtract).then_inc(d_ready, 1)

                        def mixed(s):
                            dve.wait_ge(m_ready, SLOTS * j + (s + 1))
                            dve.tensor_tensor(S0[:, s, :], S0[:, s, :], PS[:, s, :], ALU.add).then_inc(z_ready, 1)

                        def elu(s):
                            dve.wait_ge(e_ready, SLOTS * j + (s + 1))
                            dve.scalar_tensor_tensor(S0[:, s, :], S1[:, s, :], 1.0, S0[:, s, :], ALU.min,
                                                     ALU.max).then_inc(t_ready, 1)

                        def weigh(s):
                            dve.wait_ge(cc_ready, j + 1)
                            dve.wait_ge(t_ready, SLOTS * j + (s + 1))
                            dve.tensor_tensor(groups(S0[:, s, :]), groups(S0[:, s, :]), spread(CC[:, s, :]),
                                              ALU.mult).then_inc(wd_ready, 1)

                        diff(0)
                        diff(1)
                        diff(2)
                        mixed(0)
                        diff(3)
                        mixed(1)
                        elu(0)
                        mixed(2)
                        elu(1)
                        mixed(3)
                        elu(2)
                        weigh(2)
                        dve.tensor_reduce(ZQ[:, :], CC[:, :, :].rearrange("p s b -> p b s"), AX.X, ALU.add).then_inc(zq_step, 1)
                        elu(3)
                        dve.wait_ge(zq_step, 2 * j + 1)
                        dve.tensor_tensor(ZN[:, t % 2, :], ZN[:, t % 2, :], ZQ[:, :], ALU.add).then_inc(zq_step, 1)
                        weigh(3)
                    dve.wait_ge(zq_step, 2 * first[t + 1])
                    dve.reciprocal(ZN[:, t % 2, :], ZN[:, t % 2, :]).then_inc(rz_ready, 1)
                    dve.wait_ge(acc_done, SLOTS * first[t + 1] + SLOTS)
                    dve.wait_ge(rz_ready, 2 + t)
                    dve.tensor_tensor(groups(GN[:, t, :]), groups(PS[:, 5 + t % 2, :]), spread(ZN[:, t % 2, :]),
                                      ALU.mult).then_inc(g_done, 1)

            @block.scalar
            def _(act):
                first = first_turns(act)
                for t in range(NT):
                    with act.Fori(first[t], first[t + 1]) as j:
                        act.wait_ge(ts_ready, j + 1)
                        act.activation(TH[:, :, :], TS[:, :, 0:B], ACT.Tanh).then_inc(th_ready, 1)
                        act.wait_ge(lg_ready, j + 1)
                        act.activation(XC[:, :, :], LG[:, :, :], ACT.Exp).then_inc(xc_ready, 1)
                        act.wait_ge(th_ready, j + 1)
                        act.activation(BE[:, :, :], TH[:, :, :], ACT.Copy, scale=0.5, bias=0.5).then_inc(be_ready, 1)
                        for s in range(SLOTS):
                            act.wait_ge(z_ready, SLOTS * j + (s + 1))
                            act.activation(S1[:, s, :], S0[:, s, :], ACT.Exp, bias=CN[:, C_M1:C_M1 + 1]).then_inc(e_ready, 1)

            @block.gpsimd
            def _(pool):
                first = first_turns(pool)
                for t in range(NT):
                    with pool.Fori(first[t], first[t + 1]) as j:
                        pool.wait_ge(xc_ready, j + 1)
                        pool.tensor_tensor(CC[:, :, :], XC[:, :, :], TS[:, :, 16:17].broadcast_to([P, SLOTS, B]),
                                           ALU.mult).then_inc(cc_ready, 1)
                        pool.wait_ge(be_ready, j + 1)
                        for s in range(SLOTS):
                            pool.wait_ge(d_ready, SLOTS * j + (s + 1))
                            pool.tensor_tensor(groups(S0[:, s, :]), groups(S0[:, s, :]), spread(BE[:, s, :]),
                                               ALU.mult).then_inc(m_ready, 1)
                        pool.wait_ge(cc_ready, j + 1)
                        for s in range(POOLED):
                            pool.wait_ge(t_ready, SLOTS * j + (s + 1))
                            pool.tensor_tensor(groups(S0[:, s, :]), groups(S0[:, s, :]), spread(CC[:, s, :]),
                                               ALU.mult).then_inc(wp_ready, 1)

        GT = feature_major(6)
        INDT = feature_major(7)
        X1 = node_major(3)
        TNH = feature_major(2)
        KP = sb("KP", [P, NT, B])
        navc = sb("navc", [P, 1])
        c_in, tT_ready, tT_outA, tT_outD, fc_ready, tn_done, av_done, kap_ready, gx_ready, kk_step, x1_done, ig_ready, xr_ready, gm_done = (
            sem(s) for s in ("c_in", "tT_ready", "tT_outA", "tT_outD", "fc_ready", "tn_done", "av_done", "kap_ready",
                             "gx_ready", "kk_step", "x1_done", "ig_ready", "xr_ready", "gm_done"))

        with nc.Block() as block:
            @block.vector
            def _(dve):
                dve.tensor_scalar(navc[:, :], wt(W_AV, 1), -1.0, None, ALU.mult).then_inc(c_in, 1)
                for t in range(NT):
                    dve.tensor_scalar(GN[:, t, :], GN[:, t, :], -1.0, None, ALU.add).then_inc(gm_done, 1)
                for t in range(NT):
                    dve.wait_ge(tT_ready, 2 * t + 2)
                    dve.tensor_copy(INDT[:, :, tile(t)], PS[:, (2 * t + 1) % 4, :].rearrange("p (q c) -> p q c", c=P)).then_inc(tT_outD, 1)
                dve.wait_ge(kap_ready, 1)
                dve.tensor_scalar(KP[:, :, :], KP[:, :, :], 0.5, 0.5, ALU.mult, ALU.add).then_inc(kk_step, 1)
                dve.wait_ge(kk_step, 1)
                for t in range(NT):
                    dve.wait_ge(ig_ready, t + 1)
                    dve.tensor_tensor(groups(X1[:, t, :]), groups(X1[:, t, :]), spread(KP[:, t, :]), ALU.mult).then_inc(kk_step, 1)
                    dve.wait_ge(kk_step, t + 2)
                    dve.wait_ge(gx_ready, t + 1)
                    dve.tensor_tensor(X1[:, t, :], X1[:, t, :], GN[:, t, :], ALU.add).then_inc(xr_ready, 1)
                dve.wait_ge(xr_ready, NT)
                layer_norm(dve, lambda i: (X1[:, i // B, (i % B) * F:(i % B + 1) * F],) * 2, NT * B, x1_done)

            @block.gpsimd
            def _(pool):
                for t in range(NT):
                    pool.wait_ge(gm_done, t + 1)
                    pool.tensor_tensor(X1[:, t, :], IND[:, t, :], GN[:, t, :], ALU.subtract).then_inc(ig_ready, 1)
                for t in range(NT):
                    pool.wait_ge(tT_ready, 2 * t + 1)
                    pool.wait_ge(ig_ready, t + 1)
                    pool.tensor_tensor(GN[:, t, :], GN[:, t, :], XN[:, t, :], ALU.add).then_inc(gx_ready, 1)

            @block.scalar
            def _(act):
                for t in range(NT):
                    act.wait_ge(tT_ready, 2 * t + 1)
                    act.activation(GT[:, :, tile(t)], PS[:, (2 * t) % 4, :].rearrange("p (q c) -> p q c", c=P), ACT.Copy).then_inc(tT_outA, 1)
                for b in range(B):
                    for w in range(2):
                        u = 2 * b + w
                        act.wait_ge(fc_ready, u + 1)
                        if u >= 4:
                            act.wait_ge(av_done, u // 2 - 1)
                        bank = 2 * (u % 2)
                        act.activation(TNH[:, u % 4, :], PS[:, bank:bank + 2, :].rearrange("p a c -> p (a c)"), ACT.Tanh,
                                       bias=wt(W_FCB, 1)).then_inc(tn_done, 1)
                act.wait_ge(av_done, B)
                act.activation(KP[:, :, :], PS[:, 4, 0:NT * B].rearrange("p (t b) -> p t b", b=B), ACT.Tanh,
                               scale=0.5).then_inc(kap_ready, 1)

            @block.tensor
            def _(pe):
                for t in range(NT):
                    for w, src in ((0, GN), (1, IND)):
                        if w == 0:
                            pe.wait_ge(gm_done, t + 1)
                        if t >= 2:
                            pe.wait_ge(tT_outD if w else tT_outA, t - 1)
                        for q in range(BP):
                            ins = pe.transpose(PS[:, (2 * t + w) % 4, tile(q)], src[:, t, tile(q)], ident)
                        ins.then_inc(tT_ready, 1)
                pe.wait_ge(tT_outA, NT)
                pe.wait_ge(tT_outD, NT)
                pe.wait_ge(c_in, 1)

                def hidden(b):
                    r = slice(64 * (b % 2), 64 * (b % 2) + 64)
                    for w, src in ((0, INDT), (1, GT)):
                        u = 2 * b + w
                        if u >= 2:
                            pe.wait_ge(tn_done, u - 1)
                        for half in range(2):
                            ins = pe.matmul(PS[:, 2 * (u % 2) + half, :], WT[r, W_FC:W_FC + P],
                                            src[r, b // 2, half * HALF:(half + 1) * HALF], start=True, stop=True)
                        ins.then_inc(fc_ready, 1)

                def score(b):
                    pe.wait_ge(tn_done, 2 * b + 2)
                    for t in range(NT):
                        for w, a in ((0, wt(W_AV, 1)), (1, navc[:, :])):
                            ins = pe.matmul(PS[:, 4, t * B + b:t * B + b + 1], TNH[:, (2 * b + w) % 4, tile(t)], a,
                                            start=(w == 0), stop=(w == 1))
                    ins.then_inc(av_done, 1)

                hidden(0)
                for b in range(1, B):
                    hidden(b)
                    score(b - 1)
                score(B - 1)

        X1T = feature_major(1)
        QT = feature_major(2)
        KT = feature_major(4)
        V = node_major(5)
        AV = node_major(6)
        RING = 3
        PR = feature_major(0)
        XK = arena[:, 7 * 4096:9 * 4096].rearrange("p (t b k f) -> p t b k f", t=NT, b=B, k=2)
        NMX = sb("NMX", [P, B * NT])
        ZZ = sb("ZZ", [P, B * NT])
        RZ = sb("RZ", [P, B * NT])
        AVN = sb("AVN", [P, RING, F])
        xT1_ready, xT1_outA, xT1_outD, q_ready, q_out, k_ready, k_out, v_ready, v_outA, v_outD = (
            sem(s) for s in ("xT1_ready", "xT1_outA", "xT1_outD", "q_ready", "q_out", "k_ready", "k_out", "v_ready", "v_outA", "v_outD"))
        av1_ready, av1_outA, av1_outD, s1_ready, max_ready, p_ready, rz1_ready, avn_ready, pv_done, o_out, o_step, x2_done = (
            sem(s) for s in ("av1_ready", "av1_outA", "av1_outD", "s1_ready", "max_ready", "p_ready", "rz1_ready", "avn_ready",
                             "pv_done", "o_out", "o_step", "x2_done"))
        TURNS = B * NT

        with nc.Block() as block:
            @block.tensor
            def _(pe):
                for t in range(NT):
                    if t >= 4:
                        pe.wait_ge(xT1_outD if t % 2 else xT1_outA, (t - 4) // 2 + 1)
                    for q in range(BP):
                        ins = pe.transpose(PS[:, t % 4, tile(q)], X1[:, t, tile(q)], ident)
                    ins.then_inc(xT1_ready, 1)
                pe.wait_ge(xT1_outA, 4)
                pe.wait_ge(xT1_outD, 4)
                for t in range(NT):
                    if t >= 2:
                        pe.wait_ge(v_outD if t % 2 else v_outA, t // 2)
                    for q in range(BP):
                        ins = pe.matmul(PS[:, 4 + t % 2, tile(q)], X1T[:, q, tile(t)], wt(W_V, P), start=True, stop=True)
                    ins.then_inc(v_ready, 1)
                for q in range(BP):
                    for half in range(2):
                        u = 2 * q + half
                        s = slice(half * HALF, (half + 1) * HALF)
                        if u >= 2:
                            pe.wait_ge(q_out, u - 1)
                        pe.matmul(PS[:, u % 2, :], wt(W_Q, P), X1T[:, q, s], start=True, stop=True).then_inc(q_ready, 1)
                        if u >= 2:
                            pe.wait_ge(k_out, u - 1)
                        pe.matmul(PS[:, 2 + u % 2, :], wt(W_K, P), X1T[:, q, s], start=True, stop=True).then_inc(k_ready, 1)
                pe.wait_ge(v_outA, 4)
                pe.wait_ge(v_outD, 4)
                for t in range(NT):
                    if t >= 2:
                        pe.wait_ge(av1_outD if t % 2 else av1_outA, t // 2)
                    for m in range(NT):
                        ins = pe.matmul(PS[:, 4 + t % 2, :], adjT[:, m, tile(t)], V[:, m, :], start=(m == 0), stop=(m == NT - 1))
                    ins.then_inc(av1_ready, 1)
                pe.wait_ge(q_out, 2 * BP)
                pe.wait_ge(k_out, 2 * BP)
                pe.wait_ge(av1_outA, 4)
                pe.wait_ge(av1_outD, 4)

                def scores(i):
                    b, m = i // NT, i % NT
                    r = slice(64 * (b % 2), 64 * (b % 2) + 64)
                    if i >= RING:
                        pe.wait_ge(p_ready, i - RING + 1)
                    for half in range(2):
                        ins = pe.matmul(PS[:, 2 * (i % RING) + half, :], KT[r, b // 2, tile(m)],
                                        QT[r, b // 2, half * HALF:(half + 1) * HALF], start=True, stop=True)
                    ins.then_inc(s1_ready, 1)

                def values(i):
                    b, m = i // NT, i % NT
                    pe.wait_ge(avn_ready, i + 1)
                    if m == 0 and b >= 2:
                        pe.wait_ge(o_out, b - 1)
                    for t in range(NT):
                        ins = pe.matmul(PS[:, 6 + b % 2, t * F:(t + 1) * F], PR[:, i % RING, tile(t)], AVN[:, i % RING, :],
                                        start=(m == 0 and t == 0), stop=(m == NT - 1), skip_group_check=True)
                    ins.then_inc(pv_done, 1)

                for i in range(TURNS + 2):
                    if i < TURNS:
                        scores(i)
                    if i >= 2:
                        values(i - 2)

            @block.scalar
            def _(act):
                for t in range(0, NT, 2):
                    act.wait_ge(xT1_ready, t + 1)
                    act.activation(X1T[:, :, tile(t)], PS[:, t % 4, :].rearrange("p (q c) -> p q c", c=P), ACT.Copy).then_inc(xT1_outA, 1)
                for t in range(0, NT, 2):
                    act.wait_ge(v_ready, t + 1)
                    act.activation(V[:, t, :], PS[:, 4, :], ACT.Copy).then_inc(v_outA, 1)
                for u in range(2 * BP):
                    act.wait_ge(q_ready, u + 1)
                    act.activation(QT[:, u // 2, (u % 2) * HALF:(u % 2 + 1) * HALF], PS[:, u % 2, :], ACT.Identity,
                                   bias=wt(W_BQ, 1)).then_inc(q_out, 1)
                for t in range(0, NT, 2):
                    act.wait_ge(av1_ready, t + 1)
                    act.activation(AV[:, t, :], PS[:, 4, :], ACT.Copy).then_inc(av1_outA, 1)
                for i in range(TURNS):
                    act.wait_ge(max_ready, i + 1)
                    if i >= RING:
                        act.wait_ge(pv_done, i - RING + 1)
                    bank = 2 * (i % RING)
                    act.activation(PR[:, i % RING, :], PS[:, bank:bank + 2, :].rearrange("p a c -> p (a c)"), ACT.Exp,
                                   bias=NMX[:, i:i + 1], accum_out=ZZ[:, i:i + 1]).then_inc(p_ready, 1)

            @block.vector
            def _(dve):
                for t in range(1, NT, 2):
                    dve.wait_ge(xT1_ready, t + 1)
                    dve.tensor_copy(X1T[:, :, tile(t)], PS[:, t % 4, :].rearrange("p (q c) -> p q c", c=P)).then_inc(xT1_outD, 1)
                for t in range(1, NT, 2):
                    dve.wait_ge(v_ready, t + 1)
                    dve.tensor_copy(V[:, t, :], PS[:, 5, :]).then_inc(v_outD, 1)
                for u in range(2 * BP):
                    dve.wait_ge(k_ready, u + 1)
                    dve.tensor_scalar(KT[:, u // 2, (u % 2) * HALF:(u % 2 + 1) * HALF], PS[:, 2 + u % 2, :],
                                      wt(W_BK, 1), None, ALU.add).then_inc(k_out, 1)
                for t in range(1, NT, 2):
                    dve.wait_ge(av1_ready, t + 1)
                    dve.tensor_copy(AV[:, t, :], PS[:, 5, :]).then_inc(av1_outD, 1)
                dve.wait_ge(av1_outA, 4)

                def scaled_values(i):
                    b, m = i // NT, i % NT
                    dve.wait_ge(p_ready, i + 1)
                    dve.reciprocal(RZ[:, i:i + 1], ZZ[:, i:i + 1]).then_inc(rz1_ready, 1)
                    dve.wait_ge(rz1_ready, i + 1)
                    if i >= RING:
                        dve.wait_ge(pv_done, i - RING + 1)
                    dve.tensor_scalar(AVN[:, i % RING, :], AV[:, m, b * F:(b + 1) * F], RZ[:, i:i + 1], None,
                                      ALU.mult).then_inc(avn_ready, 1)

                def finish(b):
                    x2b = XK[:, :, b, 0, :]
                    dve.wait_ge(pv_done, NT * (b + 1))
                    dve.scalar_tensor_tensor(x2b, PS[:, 6 + b % 2, :].rearrange("p (t f) -> p t f", f=F), 0.0,
                                             X1[:, :, b * F:(b + 1) * F], ALU.max, ALU.add).then_inc(o_out, 1)
                    dve.wait_ge(o_out, b + 1)
                    layer_norm(dve, lambda i: (XK[:, i, b, 0, :],) * 2, NT, x2_done)

                for i in range(TURNS + 1):
                    if i < TURNS:
                        dve.wait_ge(s1_ready, i + 1)
                        bank = 2 * (i % RING)
                        dve.tensor_reduce(NMX[:, i:i + 1], PS[:, bank:bank + 2, :], AX.XY, ALU.max, negate=True).then_inc(max_ready, 1)
                    if i >= 1:
                        scaled_values(i - 1)
                    if i >= NT + 3 and (i - 3) % NT == 0:
                        finish((i - 3) // NT - 1)
                finish(B - 1)

        XKT = arena[:, 0:8192].rearrange("p (b n) -> p b n", b=B)
        XG2 = node_major(3)
        XG2T = feature_major(2)
        X3 = node_major(4)
        ACC = node_major(5)
        W01 = arena[:, 6 * 4096:6 * 4096 + D * F]
        W2 = arena[:, 6 * 4096 + D * F:6 * 4096 + 2 * D * F]
        BO = arena[:, 6 * 4096 + 2 * D * F:6 * 4096 + 2 * D * F + NT * F].rearrange("p (t f) -> p t f", f=F)
        w01_in, bo_ready, bo_out, init_done, a1_ready, a1_outA, a1_outD, a2_ready, a2_out = (
            sem(s) for s in ("w01_in", "bo_ready", "bo_out", "init_done", "a1_ready", "a1_outA", "a1_outD", "a2_ready", "a2_out"))
        kT_ready, kT_outA, kT_outD, gT_ready, gT_outA, gT_outD, y_ready, y_out, acc_step, x3_done = (
            sem(s) for s in ("kT_ready", "kT_outA", "kT_outD", "gT_ready", "gT_outA", "gT_outD", "y_ready", "y_out",
                             "acc_step", "x3_done"))
        DH = 8

        with nc.Block() as block:
            @block.sync
            def _(sp):
                sp.dma_start(W01, w01).then_inc(w01_in, 16)
                sp.dma_start(W2, w2).then_inc(w01_in, 16)
                sp.wait_ge(w01_in, 32)

            @block.gpsimd
            def _(pool):
                pool.wait_ge(bo_out, 1)
                for t in range(NT):
                    pool.tensor_tensor(groups(ACC[:, t, :]), XK[:, t, :, 0, :],
                                       BO[:, t:t + 1, :].broadcast_to([P, B, F]), ALU.add).then_inc(init_done, 1)

            @block.scalar
            def _(act):
                act.wait_ge(bo_ready, 1)
                act.activation(BO, PS[:, 7, :].rearrange("p (t f) -> p t f", f=F), ACT.Copy).then_inc(bo_out, 1)
                for t in range(0, NT, 2):
                    act.wait_ge(a1_ready, t + 1)
                    act.activation(XK[:, t, :, 1, :], groups(PS[:, t % 2, :]), ACT.Copy).then_inc(a1_outA, 1)
                for u in range(0, 16, 2):
                    act.wait_ge(kT_ready, u + 1)
                    t, h = u // 2, u % 2
                    act.activation(XKT[:, 4 * h:4 * h + 4, tile(t)], PS[:, 4 + u % 4, :].rearrange("p (b c) -> p b c", c=P),
                                   ACT.Copy).then_inc(kT_outA, 1)
                for t in range(0, NT, 2):
                    act.wait_ge(gT_ready, t + 1)
                    act.activation(XG2T[:, :, tile(t)], PS[:, 4 + t % 4, :].rearrange("p (q c) -> p q c", c=P), ACT.Copy).then_inc(gT_outA, 1)

            @block.vector
            def _(dve):
                for t in range(1, NT, 2):
                    dve.wait_ge(a1_ready, t + 1)
                    dve.tensor_copy(XK[:, t, :, 1, :], groups(PS[:, t % 2, :])).then_inc(a1_outD, 1)
                for t in range(NT):
                    dve.wait_ge(a2_ready, t + 1)
                    dve.scalar_tensor_tensor(groups(XG2[:, t, :]), groups(PS[:, 2 + t % 2, :]), 2.0, XK[:, t, :, 0, :],
                                             ALU.mult, ALU.subtract).then_inc(a2_out, 1)
                    u = 2 * t + 1
                    dve.wait_ge(kT_ready, u + 1)
                    dve.tensor_copy(XKT[:, 4:8, tile(t)], PS[:, 4 + u % 4, :].rearrange("p (b c) -> p b c", c=P)).then_inc(kT_outD, 1)
                for t in range(1, NT, 2):
                    dve.wait_ge(gT_ready, t + 1)
                    dve.tensor_copy(XG2T[:, :, tile(t)], PS[:, 4 + t % 4, :].rearrange("p (q c) -> p q c", c=P)).then_inc(gT_outD, 1)
                steps = 0
                for t in range(NT):
                    dve.wait_ge(init_done, t + 1)
                    for g in range(2):
                        acc = groups(ACC[:, t, g * 4 * F:(g + 1) * 4 * F])
                        for dh in range(D // DH):
                            r = (t * 2 + g) * 2 + dh
                            dve.wait_ge(y_ready, r + 1)
                            for d in range(DH):
                                e = dh * DH + d
                                if steps:
                                    dve.wait_ge(acc_step, steps)
                                ins = dve.scalar_tensor_tensor(acc, PS[:, 4 * (r % 2):4 * (r % 2) + 4, d * F:(d + 1) * F],
                                                               WT[:, W_EMB + t * D + e:W_EMB + t * D + e + 1], acc,
                                                               ALU.mult, ALU.add).then_inc(acc_step, 1)
                                steps += 1
                    dve.wait_ge(acc_step, steps)
                    layer_norm(dve, lambda i: (ACC[:, t, i * F:(i + 1) * F], X3[:, t, i * F:(i + 1) * F]), B, x3_done)

            @block.tensor
            def _(pe):
                for t in range(NT):
                    ins = pe.matmul(PS[:, 7, t * F:(t + 1) * F], WT[0:D, W_EMBT + t * P:W_EMBT + (t + 1) * P], wt(W_BIAS, F, D),
                                    start=True, stop=True)
                ins.then_inc(bo_ready, 1)
                for t in range(NT):
                    if t >= 2:
                        pe.wait_ge(a1_outD if t % 2 else a1_outA, t // 2)
                    for m in range(NT):
                        ins = pe.matmul(PS[:, t % 2, :], adjT[:, m, tile(t)], XK[:, m, :, 0, :], start=(m == 0), stop=(m == NT - 1))
                    ins.then_inc(a1_ready, 1)
                pe.wait_ge(a1_outA, 4)
                pe.wait_ge(a1_outD, 4)
                pe.wait_ge(bo_out, 1)
                for t in range(NT):
                    if t >= 2:
                        pe.wait_ge(a2_out, t - 1)
                    for m in range(NT):
                        ins = pe.matmul(PS[:, 2 + t % 2, :], adjT[:, m, tile(t)], XK[:, m, :, 1, :], start=(m == 0), stop=(m == NT - 1))
                    ins.then_inc(a2_ready, 1)
                    for h in range(2):
                        u = 2 * t + h
                        if u >= 4:
                            pe.wait_ge(kT_outD if h else kT_outA, (u - 4) // 2 + 1)
                        for i in range(4):
                            ins = pe.transpose(PS[:, 4 + u % 4, tile(i)],
                                               XK[:, t, 4 * h + i, :, :].rearrange("p k f -> p (k f)"), ident)
                        ins.then_inc(kT_ready, 1)
                pe.wait_ge(a2_out, NT)
                pe.wait_ge(kT_outA, NT)
                pe.wait_ge(kT_outD, NT)
                for t in range(NT):
                    if t >= 4:
                        pe.wait_ge(gT_outD if t % 2 else gT_outA, (t - 4) // 2 + 1)
                    for q in range(BP):
                        ins = pe.transpose(PS[:, 4 + t % 4, tile(q)], XG2[:, t, tile(q)], ident)
                    ins.then_inc(gT_ready, 1)
                pe.wait_ge(gT_outA, 4)
                pe.wait_ge(gT_outD, 4)
                pe.wait_ge(w01_in, 32)
                for t in range(NT):
                    for g in range(2):
                        for dh in range(D // DH):
                            r = (t * 2 + g) * 2 + dh
                            if r >= 2:
                                pe.wait_ge(acc_step, DH * (r - 1))
                            c = slice(dh * DH * F, (dh + 1) * DH * F)
                            for i in range(4):
                                b = 4 * g + i
                                rows = slice(64 * (b % 2), 64 * (b % 2) + 64)
                                bank = PS[:, 4 * (r % 2) + i, :]
                                pe.matmul(bank, XKT[:, b, tile(t)], W01[:, c], start=True, stop=False)
                                ins = pe.matmul(bank, XG2T[rows, b // 2, tile(t)], W2[rows, c], start=False, stop=True)
                            ins.then_inc(y_ready, 1)

        LT = feature_major(5)
        Z1 = node_major(6)
        X4 = node_major(0)
        lt_ready, lt_outA, lt_outD, z_r, z1_out, z2_out, x4_done, stored = (
            sem(s) for s in ("lt_ready", "lt_outA", "lt_outD", "z_r", "z1_out", "z2_out", "x4_done", "stored"))
        NB = 2 * BP

        with nc.Block() as block:
            @block.sync
            def _(sp):
                for q in range(BP):
                    for par in range(2):
                        b = 2 * q + par
                        sp.wait_ge(x4_done, b + 1)
                        sp.dma_start(out[b].rearrange("(t p) f -> p t f", p=P), X4[:, :, b * F:(b + 1) * F]).then_inc(stored, 16)
                sp.wait_ge(stored, 16 * B)

            @block.tensor
            def _(pe):
                def spread_nodes(u):
                    layer, q = u // BP, u % BP
                    src = Z1 if layer else X3
                    if layer:
                        pe.wait_ge(z1_out, q + 1)
                    for half in range(2):
                        if u >= 2:
                            pe.wait_ge(lt_outD if half else lt_outA, u - 1)
                        for m in range(NT):
                            ins = pe.matmul(PS[:, 2 * (u % 2) + half, :], src[:, m, tile(q)], adjT[:, m, half * HALF:(half + 1) * HALF],
                                            start=(m == 0), stop=(m == NT - 1))
                        ins.then_inc(lt_ready, 1)

                def features(u):
                    layer, q = u // BP, u % BP
                    pe.wait_ge(lt_outA, u + 1)
                    pe.wait_ge(lt_outD, u + 1)
                    if 2 <= u < BP + 2:
                        pe.wait_ge(z1_out, u - 1)
                    elif u >= BP + 2:
                        pe.wait_ge(z2_out, u - 1 - BP)
                    for t in range(NT):
                        ins = pe.matmul(PS[:, 4 + 2 * (u % 2) + t // 4, (t % 4) * P:(t % 4 + 1) * P], LT[:, u % 4, tile(t)],
                                        wt(W_L3 + layer * P, P), start=True, stop=True)
                    ins.then_inc(z_r, 1)

                spread_nodes(0)
                for u in range(1, NB):
                    spread_nodes(u)
                    features(u - 1)
                features(NB - 1)

            @block.scalar
            def _(act):
                def lt_copy(u):
                    act.wait_ge(lt_ready, 2 * u + 1)
                    act.activation(LT[:, u % 4, 0:HALF], PS[:, 2 * (u % 2), :], ACT.Copy).then_inc(lt_outA, 1)

                lt_copy(0)
                for u in range(NB):
                    if u + 1 < NB:
                        lt_copy(u + 1)
                    if u < BP:
                        act.wait_ge(z_r, u + 1)
                        act.activation(Z1[:, :, tile(u)], PS[:, 4 + 2 * (u % 2):6 + 2 * (u % 2), :].rearrange("p a (t c) -> p (a t) c", c=P),
                                       ACT.Relu).then_inc(z1_out, 1)

            @block.vector
            def _(dve):
                def lt_copy(u):
                    dve.wait_ge(lt_ready, 2 * u + 2)
                    dve.tensor_copy(LT[:, u % 4, HALF:N], PS[:, 2 * (u % 2) + 1, :]).then_inc(lt_outD, 1)

                lt_copy(0)
                for u in range(NB):
                    if u + 1 < NB:
                        lt_copy(u + 1)
                    if u >= BP:
                        q = u - BP
                        dve.wait_ge(z_r, u + 1)
                        dve.scalar_tensor_tensor(X4[:, :, tile(q)], PS[:, 4 + 2 * (u % 2):6 + 2 * (u % 2), :].rearrange("p a (t c) -> p (a t) c", c=P),
                                                 0.0, X3[:, :, tile(q)], ALU.max, ALU.add).then_inc(z2_out, 1)
                        dve.wait_ge(z2_out, q + 1)
                        for par in range(2):
                            b = 2 * q + par
                            layer_norm(dve, lambda i: (X4[:, i, b * F:(b + 1) * F],) * 2, NT, x4_done)


def kernel(**inputs):
    import numpy as np
    import concourse.bacc as bacc
    from concourse.bass_utils import run_bass_kernel_spmd

    a = {k: np.asarray(v) for k, v in inputs.items()}

    consts = np.zeros((P, CW), np.float32)
    consts[:, C_ID:C_ID + P] = np.eye(P)
    consts[:, C_ID2:C_ID2 + F] = np.concatenate([np.eye(F)] * 2)
    consts[:, C_ONE:C_ONE + P] = 1
    consts[0:64, C_UP:C_UP + P] = np.concatenate([np.triu(np.ones((E, E)))] * 2, 1)
    consts[0:NT, C_TRI:C_TRI + NT + 1] = np.triu(np.ones((NT, NT + 1)), 1)
    consts[:, C_STEP:C_STEP + QUADS] = SLOTS * np.arange(QUADS)
    consts[:, C_RANK:C_RANK + E + SLOTS] = 1 + np.arange(E + SLOTS)
    consts[:, C_M1] = -1

    weights = np.zeros((P, WW), np.float32)

    def diagonal(at, w):
        n = w.shape[1]
        weights[0:64, at:at + n] = w
        weights[64:128, at + n:at + 2 * n] = w

    def twice(at, w):
        weights[0:64, at:at + w.shape[1]] = w
        weights[64:128, at:at + w.shape[1]] = w

    diagonal(W_H, a["L0_gnn_W"])
    diagonal(W_IND, a["L0_gnn_W_ind"])
    diagonal(W_AN, np.repeat(a["L0_gnn_a_node"][:, None], E, 1))
    diagonal(W_GN, a["L0_gnn_a_gn"][:, None])
    twice(W_FC, a["L0_gnn_fcW"])
    weights[:, W_FCB] = a["L0_gnn_fcb"]
    weights[:, W_AV] = a["L0_gnn_av"]
    weights[:, W_GE:W_GE + F] = a["L0_gnn_a_ge"][None, :]
    diagonal(W_Q, a["L1_gnn_Wq"])
    diagonal(W_K, a["L1_gnn_Wk"])
    diagonal(W_V, a["L1_gnn_Wv"])
    twice(W_BQ, a["L1_gnn_bq"][:, None])
    twice(W_BK, a["L1_gnn_bk"][:, None])
    weights[:, W_EMB:W_EMB + NT * D] = a["L2_gnn_embedding"].reshape(NT, P, D).transpose(1, 0, 2).reshape(P, NT * D)
    weights[0:D, W_EMBT:W_EMBT + N] = a["L2_gnn_embedding"].T
    weights[0:D, W_BIAS:W_BIAS + F] = a["L2_gnn_bias"]
    l3 = a["L3_gnn_net_params"].reshape(2, F, F)
    diagonal(W_L3, l3[0])
    diagonal(W_L3 + P, l3[1])

    w = a["L2_gnn_weight"].transpose(1, 2, 0, 3).reshape(3, F, D * F)
    arrays = {
        "in_x_nat": np.ascontiguousarray(a["x"].transpose(1, 0, 2)),
        "in_x_tr": np.ascontiguousarray(a["x"].transpose(0, 2, 1)).reshape(B * F, N),
        "in_adj_tr": np.ascontiguousarray(a["adj"].T),
        "in_h_nat": np.ascontiguousarray(a["L0_gnn_H"]),
        "in_h_tr": np.ascontiguousarray(a["L0_gnn_H"].T),
        "in_consts": consts,
        "in_weights": weights,
        "in_w01": np.ascontiguousarray(w[0:2].reshape(2 * F, D * F)),
        "in_w2": np.ascontiguousarray(np.concatenate([w[2], w[2]])),
    }
    nc = bacc.Bacc("TRN2", target_bir_lowering=False, num_devices=1)
    args = [nc.dram_tensor(n, v.shape, mybir.dt.from_np(v.dtype), kind="ExternalInput").ap() for n, v in arrays.items()]
    out = nc.dram_tensor("out_0", (B, N, F), F32, kind="ExternalOutput").ap()
    program(nc, *args, out)
    r = run_bass_kernel_spmd(nc, [arrays], core_ids=[0])
    return r.results[0]["out_0"]
```

```python
from contextlib import ExitStack

import concourse.bass as bass
from concourse import mybir

F32 = mybir.dt.float32
F32R = mybir.dt.float32r
BF16 = mybir.dt.bfloat16
I32 = mybir.dt.int32
ALU = mybir.AluOpType
ACT = mybir.ActivationFunctionType
AX = mybir.AxisListType

P = 128
B = 8
N = 1024
F = 64
E = 64
NT = N // P
BP = B // 2
BF = B * F
HALF = N // 2
D = 16
SLOTS = 4
QUADS = E // SLOTS
NEG = -1e9
BIG = 3e38
EPS = 1e-5

C_ID = 0
C_ID2 = C_ID + P
C_ONE = C_ID2 + F
C_UP = C_ONE + P
C_TRI = C_UP + P
C_STEP = C_TRI + NT + 1
C_RANK = C_STEP + QUADS
C_M1 = C_RANK + E + SLOTS
CW = C_M1 + 1

W_H = 0
W_IND = W_H + P
W_AN = W_IND + P
W_GN = W_AN + P
W_FC = W_GN + 2
W_FCB = W_FC + 2 * P
W_AV = W_FCB + 1
W_GE = W_AV + 1
W_Q = W_GE + F
W_K = W_Q + 2 * P
W_V = W_K + 2 * P
W_BQ = W_V + P
W_BK = W_BQ + 1
W_EMB = W_BK + 1
W_L3 = W_EMB + NT * D
WW = W_L3 + 2 * P


def program(nc, x_nat, x_tr, adj_tr, h_nat, h_tr, consts, weights, w01, w2, emb_bias, out):
    ctx = ExitStack()
    with ctx:
        def sb(name, shape, dt=F32):
            return ctx.enter_context(nc.sbuf_tensor(name, shape, dt))

        stage_sems = []

        def sem(name):
            stage_sems.append(nc.alloc_semaphore(name))
            return stage_sems[-1]

        def free_semaphores():
            nc.clear_and_free_semaphores(stage_sems)
            nc.all_engine_barrier()
            stage_sems.clear()

        PS = ctx.enter_context(nc.psum_tensor("PS", [P, 8, 512], F32))

        ADJH = sb("ADJH", [P, NT, N], F32R)
        ADJL = sb("ADJL", [P, NT, N], F32R)
        CN = sb("CN", [P, CW])
        WT = sb("WT", [P, WW])
        SLOT = NT * BF
        SLOTS_IN_ARENA = 7
        arena_at = -(-nc.sbuf_base // 32) * 32
        arena = sb("arena", [P, SLOTS_IN_ARENA * SLOT])

        def rounded(name, column, shape):
            n = 1
            for k in shape[1:]:
                n *= k
            assert column + n <= SLOTS_IN_ARENA * SLOT
            return nc.alloc_sbuf_tensor_at(name, shape, F32R, offset=arena_at + 4 * column)

        def node_major(slot):
            return arena[:, slot * 4096:(slot + 1) * 4096].rearrange("p (t c) -> p t c", t=NT)

        def feature_major(slot):
            return arena[:, slot * 4096:(slot + 1) * 4096].rearrange("p (q n) -> p q n", q=BP)

        ident = CN[:, C_ID:C_ID + P]
        ones = CN[:, C_ONE:C_ONE + P]

        def bits(ap):
            return ap.bitcast(F32)

        def wt(at, n, rows=P):
            return WT[0:rows, at:at + n]

        def tile(t):
            return slice(t * P, (t + 1) * P)

        def groups(ap):
            return ap.rearrange("p (b f) -> p b f", f=F)

        def spread(ap, n=F):
            return ap.unsqueeze(2).broadcast_to([ap.shape[0], ap.shape[1], n])

        LN_ST = sb("LN_ST", [P, 64, 6])
        LN_A = sb("LN_A", [P, 64])
        LN_B = sb("LN_B", [P, 64])
        LN_V = sb("LN_V", [P, 64])
        LN_M = sb("LN_M", [P, 64])
        LN_Y = sb("LN_Y", [P, 64])
        ln_step = ctx.enter_context(nc.semaphore("ln_step"))
        ln_count = [0]

        def link(dve, ins):
            ln_count[0] += 1
            ins.then_inc(ln_step, 1)
            dve.wait_ge(ln_step, ln_count[0])

        def norm_stats(dve, source, groups):
            for i in groups:
                ins = dve.bn_stats(LN_ST[:, i, :], source(i))
            link(dve, ins)

        def norm_scales(dve, n, at=0):
            g = slice(at, at + n)
            even, odd = LN_ST[:, g, 1], LN_ST[:, g, 4]
            a, b, v, m, y = (t[:, g] for t in (LN_A, LN_B, LN_V, LN_M, LN_Y))
            dve.tensor_tensor(m, even, odd, ALU.add)
            dve.tensor_tensor(v, LN_ST[:, g, 2], LN_ST[:, g, 5], ALU.add)
            link(dve, dve.tensor_tensor(a, even, odd, ALU.subtract))
            link(dve, dve.scalar_tensor_tensor(b, a, 16.0, a, ALU.mult, ALU.mult))
            dve.tensor_scalar(m, m, 0.5, None, ALU.mult)
            link(dve, dve.tensor_tensor(v, v, b, ALU.add))
            link(dve, dve.tensor_scalar(v, v, 1.0 / F, EPS, ALU.mult, ALU.add))
            link(dve, dve.tensor_scalar(a.bitcast(I32), v.bitcast(I32), 1, None, ALU.logical_shift_right))
            link(dve, dve.tensor_scalar(y.bitcast(I32), a.bitcast(I32), -1.0, float(0x5F3759DF), ALU.mult, ALU.add))
            for _ in range(3):
                link(dve, dve.scalar_tensor_tensor(a, v, -0.5, y, ALU.mult, ALU.mult))
                link(dve, dve.tensor_tensor(b, a, y, ALU.mult))
                link(dve, dve.scalar_tensor_tensor(y, b, 1.5, y, ALU.add, ALU.mult))
        def spread_feature(ap):
            return ap.unsqueeze(3).broadcast_to([ap.shape[0], ap.shape[1], ap.shape[2], F])

        def norm_apply(engine, x, n_at, tiles, graphs):
            def scale(t):
                return spread_feature(t[:, n_at:n_at + tiles * graphs].rearrange("p (t b) -> p t b", b=graphs))
            v = x.rearrange("p t (b f) -> p t b f", f=F)
            return (lambda: engine.tensor_tensor(v, v, scale(LN_M), ALU.subtract),
                    lambda: engine.tensor_tensor(v, v, scale(LN_Y), ALU.mult))

        def layer_norm(dve, group, n, last):
            norm_stats(dve, lambda i: group(i)[0], range(n))
            norm_scales(dve, n)
            for i in range(n):
                src, dst = group(i)
                ins = dve.tensor_scalar(dst, src, LN_M[:, i:i + 1], LN_Y[:, i:i + 1], ALU.subtract, ALU.mult)
            ins.then_inc(last, 1)

        def adjacent(pe, rest, t, acc, high, low):
            for m in range(NT):
                pe.matmul(acc, ADJH[:, m, tile(t)], high(m), start=(m == 0), stop=False, skip_group_check=True)
            with pe.If(rest > 0):
                for m in range(NT):
                    pe.matmul(acc, ADJL[:, m, tile(t)], high(m), start=False, stop=False, skip_group_check=True)
            for m in range(NT):
                ins = pe.matmul(acc, ADJH[:, m, tile(t)], low(m), start=False, stop=(m == NT - 1), skip_group_check=True)
            return ins

        XN = node_major(5)
        XT = feature_major(0)
        HP = node_major(2)
        XWH = rounded("XWH", 5 * SLOT, [P, NT, BF])
        XWL = rounded("XWL", 6 * SLOT, [P, NT, BF])
        HT = feature_major(1)
        IND = node_major(3)
        RAW = arena[:, 3 * SLOT:4 * SLOT].rearrange("p (r n) -> p r n", n=N)
        EX = feature_major(0)
        ET = arena[:, SLOT:2 * SLOT].rearrange("p (t q c) -> p t q c", t=NT, q=BP)
        maskT = arena[:, 4 * SLOT:4 * SLOT + N]
        limT = arena[:, 4 * SLOT + N:4 * SLOT + 2 * N]
        effT = arena[:, 4 * SLOT + 2 * N:4 * SLOT + 3 * N]
        rankT = effT
        hN = arena[:, 4 * SLOT + 3 * N:4 * SLOT + 3 * N + NT * E].rearrange("p (t e) -> p t e", e=E)
        limN = arena[:, 4 * SLOT + 3 * N + NT * E:5 * SLOT].rearrange("p (t e) -> p t e", e=E)
        degH = sb("degH", [P, NT])
        none = sb("none", [P, NT])
        low = sb("low", [P, NT])
        degE = sb("degE", [P, NT])
        kmx = sb("kmx", [NT, 1])
        kst = sb("kst", [NT, QUADS])
        kq = sb("kq", [NT, 1])
        first_i = sb("first_i", [1, NT + 1], I32)
        nmx = sb("nmx", [P, BP])
        Zs = sb("Zs", [P, BP])
        rZ = sb("rZ", [P, BP])
        rdg = sb("rdg", [P, NT])
        HM = sb("HM", [P, NT, 17])
        AG = arena[:, 2048:2304].rearrange("p (q f) -> p q f", f=F)
        AGM = arena[:, 2304:2560].rearrange("p (q f) -> p q f", f=F)
        AEX = arena[:, 2560:2816].rearrange("p (q f) -> p q f", f=F)
        HE = arena[:, 2816:3072].rearrange("p (q f) -> p q f", f=F)
        HET = arena[:, 3072:3328].rearrange("p (a c) -> p a c", c=P)
        THE = arena[:, 3328:3840].rearrange("p (a c) -> p a c", c=P)
        ae = sb("ae", [P, BP])
        SM = sb("SM", [P, 17])
        AGBD = sb("AGBD", [P, B, F])
        DG = arena[:, 0:B * E].rearrange("p (b e) -> p b e", e=E)
        SEB = arena[:, B * E:2 * B * E].rearrange("p (b e) -> p b e", e=E)
        LGM = arena[:, 2 * B * E:4 * B * E].rearrange("p (a b e) -> p a b e", a=2, e=E)
        zero16 = sb("zero16", [P, 512], BF16)
        ONR = sb("ONR", [P, 2], F32R)
        rest_max = sb("rest_max", [P, NT + 1])
        has_rest = sb("has_rest", [1, 1], I32)

        consts_in, weights_in, xT_in, x_in, hT_in, hN_in, one_ready = (
            sem(s) for s in ("consts_in", "weights_in", "xT_in", "x_in", "hT_in", "hN_in", "one_ready"))
        adj_in = [sem(f"adj_in{i}") for i in range(4)]
        adjh_ready, adjl_ready, rest_seen, rest_ready, xwh_ready = (
            sem(s) for s in ("adjh_ready", "adjl_ready", "rest_seen", "rest_ready", "xwh_ready"))
        h_ready, h_out, xw_ready, xw_out = sem("h_ready"), sem("h_out"), sem("xw_ready"), sem("xw_out")
        hT_ready, hT_outA, hT_outD = sem("hT_ready"), sem("hT_outA"), sem("hT_outD")
        mask_ready, degB_ready, eff_ready, rank_ready = sem("mask_ready"), sem("degB_ready"), sem("eff_ready"), sem("rank_ready")
        rank_done = sem("rank_done")
        s_ready, s_copied, s_out, ex_max, ex_done = sem("s_ready"), sem("s_copied"), sem("s_out"), sem("ex_max"), sem("ex_done")
        hg_ready, hg_out = sem("hg_ready"), sem("hg_out")
        ind_ready, ind_scale, ind_out = sem("ind_ready"), sem("ind_scale"), sem("ind_out")
        et_ready, et_outA, et_outD = sem("et_ready"), sem("et_outA"), sem("et_outD")
        rz_ready, agg_ready, agg_out, am_ready, aex_done, he_ready = (
            sem(s) for s in ("rz_ready", "agg_ready", "agg_out", "am_ready", "aex_done", "he_ready"))
        heT_ready, heT_out, fce_ready, the_done, se_ready, sm_ready, seB_ready, seB_out = (
            sem(s) for s in ("heT_ready", "heT_out", "fce_ready", "the_done", "se_ready", "sm_ready", "seB_ready", "seB_out"))
        zero_set, dstep, degT_ready, kq_ready, first_ready, sl = (
            sem(s) for s in ("zero_set", "dstep", "degT_ready", "kq_ready", "first_ready", "sl"))
        dn = [0]

        with nc.Block() as block:
            @block.sync
            def _(sp):
                for q in range(BP):
                    sp.dma_start(XT[:, q, :], x_tr[q * P:(q + 1) * P, :]).then_inc(xT_in, 16)
                for t in range(NT):
                    if t >= 4:
                        sp.wait_ge(adjl_ready, t - 3)
                    sp.dma_start(RAW[:, t % 4, :], adj_tr[t * P:(t + 1) * P, :]).then_inc(adj_in[t % 4], 16)

            @block.gpsimd
            def _(pool):
                pool.memset(SM[:, :], 0.0).then_inc(sl, 1)
                pool.memset(AGBD[:, :, :], 0.0).then_inc(zero_set, 1)
                pool.memset(HM[:, :, :], 0.0).then_inc(zero_set, 1)
                pool.memset(zero16[:, :], 0.0).then_inc(zero_set, 1)
                pool.wait_ge(sl, 1)
                pool.memset(SM[0:64, 16:17], 1.0).then_inc(zero_set, 1)
                for t in range(NT):
                    pool.wait_ge(adj_in[t % 4], 16 * (t // 4 + 1))
                    pool.wait_ge(adjh_ready, t + 1)
                    pool.tensor_tensor(ADJL[:, t, :], RAW[:, t % 4, :], bits(ADJH[:, t, :]), ALU.subtract).then_inc(adjl_ready, 1)

            @block.scalar
            def _(act):
                act.dma_start(CN[:, :], consts).then_inc(consts_in, 16)
                act.dma_start(WT[:, :], weights).then_inc(weights_in, 16)
                act.dma_start(maskT[0:64, :], h_tr).then_inc(hT_in, 16)
                act.dma_start(maskT[64:128, :], h_tr).then_inc(hT_in, 16)
                act.dma_start(hN, h_nat.rearrange("(t p) e -> p t e", p=P)).then_inc(hN_in, 16)

                def split_adj(t):
                    act.wait_ge(adj_in[t % 4], 16 * (t // 4 + 1))
                    act.activation(ADJH[:, t, :], RAW[:, t % 4, :], ACT.Copy).then_inc(adjh_ready, 1)

                for t in range(NT):
                    act.wait_ge(h_ready, t + 1)
                    act.activation(HP[:, t, :], PS[:, (2 * t) % 4, :], ACT.Copy, bias=1.0).then_inc(h_out, 1)
                    act.wait_ge(xw_ready, t + 1)
                    act.activation(XWH[:, t, :], PS[:, (2 * t + 1) % 4, :], ACT.Copy).then_inc(xwh_ready, 1)
                for q in range(BP):
                    act.wait_ge(hT_ready, 2 * q + 1)
                    act.activation(HT[:, q, 0:HALF], PS[:, 4 + (2 * q) % 4, :], ACT.Copy).then_inc(hT_outA, 1)
                    split_adj(q)
                for q in range(BP):
                    for half in range(2):
                        u = 2 * q + half
                        act.wait_ge(s_ready, u + 1)
                        act.activation(EX[:, q, half * HALF:(half + 1) * HALF], PS[:, 4 + u % 4, :],
                                       ACT.Copy).then_inc(s_copied, 1)
                    if q >= 1:
                        act.wait_ge(ex_max, q)
                        act.activation(EX[:, q - 1, :], EX[:, q - 1, :], ACT.Exp, bias=nmx[:, q - 1:q],
                                       accum_out=Zs[:, q - 1:q]).then_inc(ex_done, 1)
                    split_adj(4 + q)
                act.wait_ge(ex_max, BP)
                act.activation(EX[:, 3, :], EX[:, 3, :], ACT.Exp, bias=nmx[:, 3:4],
                               accum_out=Zs[:, 3:4]).then_inc(ex_done, 1)
                act.wait_ge(hg_ready, 1)
                act.wait_ge(zero_set, 2)
                act.activation(HM[:, :, 0:B], PS[:, 0, 0:NT * B].rearrange("p (t b) -> p t b", b=B),
                               ACT.Copy, scale=0.5).then_inc(hg_out, 1)

                def industry_out(t):
                    act.wait_ge(ind_scale, t + 1)
                    act.activation(IND[:, t, :], PS[:, 2 + t % 2, :], ACT.Copy,
                                   scale=rdg[:, t:t + 1]).then_inc(ind_out, 1)

                for t in range(3):
                    industry_out(t)
                for q in range(BP):
                    act.wait_ge(et_ready, q + 1)
                    act.activation(ET[:, 0:4, q, :], PS[:, 4 + 2 * (q % 2), :].rearrange("p (t c) -> p t c", c=P),
                                   ACT.Copy).then_inc(et_outA, 1)
                act.wait_ge(agg_ready, 1)
                act.wait_ge(rz_ready, 1)
                for q in range(BP):
                    for par in range(2):
                        r = slice(64 * par, 64 * par + 64)
                        ins = act.activation(AG[r, q, :], PS[r, 4, q * P + 64 * par:q * P + 64 * par + 64],
                                             ACT.Copy, scale=rZ[r, q:q + 1])
                ins.then_inc(agg_out, 1)
                act.wait_ge(agg_out, 1)
                act.activation(AEX[:, :, :], AG[:, :, :], ACT.Exp, bias=CN[:, C_M1:C_M1 + 1]).then_inc(aex_done, 1)
                industry_out(3)
                industry_out(4)
                act.wait_ge(heT_ready, 1)
                act.activation(HET[:, :, :], PS[:, 5, 0:2 * P].rearrange("p (a c) -> p a c", c=P),
                               ACT.Copy).then_inc(heT_out, 1)
                industry_out(5)
                act.wait_ge(fce_ready, 1)
                for par in range(2):
                    act.activation(THE[:, par:BP:2, :], PS[:, 6 + par, 0:2 * P].rearrange("p (a c) -> p a c", c=P), ACT.Tanh,
                                   bias=wt(W_FCB, 1)).then_inc(the_done, 1)
                industry_out(6)
                act.wait_ge(seB_ready, 1)
                act.activation(SEB[:, :, :], PS[:, 5, :].rearrange("p (b e) -> p b e", e=E), ACT.Copy).then_inc(seB_out, 1)
                industry_out(7)

            @block.vector
            def _(dve):
                def link(ins):
                    dn[0] += 1
                    ins.then_inc(dstep, 1)
                    dve.wait_ge(dstep, dn[0])

                def rest_seen_in(t):
                    dve.wait_ge(adjl_ready, t + 1)
                    dve.tensor_reduce(rest_max[:, t:t + 1], bits(ADJL[:, t, :]), AX.X, ALU.max,
                                      apply_absolute_value=True).then_inc(rest_seen, 1)

                dve.wait_ge(hT_in, 32)
                link(dve.tensor_scalar(maskT, maskT, 0.0, None, ALU.is_gt))
                dve.tensor_scalar(limT, maskT, BIG, NEG, ALU.mult, ALU.add).then_inc(mask_ready, 1)

                def xw_out_step(t):
                    dve.wait_ge(xwh_ready, t + 1)
                    dve.tensor_tensor(XWL[:, t, :], PS[:, (2 * t + 1) % 4, :], bits(XWH[:, t, :]), ALU.subtract).then_inc(xw_out, 1)

                for t in range(NT):
                    xw_out_step(t)
                for q in range(BP):
                    dve.wait_ge(hT_ready, 2 * q + 2)
                    dve.tensor_copy(HT[:, q, HALF:N], PS[:, 4 + (2 * q + 1) % 4, :]).then_inc(hT_outD, 1)
                dve.wait_ge(degB_ready, 1)
                for half in range(2):
                    s = slice(half * HALF, (half + 1) * HALF)
                    ins = dve.scalar_tensor_tensor(effT[:, s], PS[:, half, :], 0.0, maskT[:, s], ALU.is_equal, ALU.max)
                ins.then_inc(eff_ready, 1)
                for q in range(BP):
                    for half in range(2):
                        u = 2 * q + half
                        s = slice(half * HALF, (half + 1) * HALF)
                        dve.wait_ge(s_copied, u + 1)
                        ins = dve.scalar_tensor_tensor(EX[:, q, s], PS[:, 4 + u % 4, :], 0.2, EX[:, q, s],
                                                       ALU.mult, ALU.max).then_inc(s_out, 1)
                    dve.wait_ge(s_out, 2 * q + 2)
                    link(dve.tensor_tensor(EX[:, q, :], EX[:, q, :], limT, ALU.min))
                    dve.tensor_reduce(nmx[:, q:q + 1], EX[:, q, :], AX.X, ALU.max, negate=True).then_inc(ex_max, 1)
                    if q == 0:
                        dve.wait_ge(rank_ready, 1)
                        dve.wait_ge(eff_ready, 1)
                        for half in range(2):
                            s = slice(half * HALF, (half + 1) * HALF)
                            ins = dve.tensor_tensor(rankT[:, s], PS[:, 2 + half, :], effT[:, s], ALU.mult)
                        ins.then_inc(rank_done, 1)

                dve.wait_ge(hN_in, 16)
                link(dve.tensor_scalar(hN, hN, 0.0, None, ALU.is_gt))
                dve.tensor_scalar(limN, hN, BIG, NEG, ALU.mult, ALU.add)
                link(dve.tensor_reduce(degH[:, :], hN, AX.X, ALU.add))
                link(dve.tensor_scalar(none[:, :], degH[:, :], 0.0, None, ALU.is_equal))
                dve.tensor_scalar(low[:, :], none[:, :], BIG, -BIG, ALU.mult, ALU.add)
                dve.scalar_tensor_tensor(degE[:, :], none[:, :], float(E), degH[:, :], ALU.mult, ALU.add).then_inc(degT_ready, 1)

                dve.wait_ge(consts_in, 16)
                dve.tensor_copy(ONR[:, :], CN[:, C_ONE:C_ONE + 2]).then_inc(one_ready, 1)
                for t in range(NT):
                    rest_seen_in(t)
                dve.wait_ge(rest_seen, NT)
                dve.tensor_reduce(rest_max[:, NT:NT + 1], rest_max[:, 0:NT], AX.X, ALU.max).then_inc(rest_ready, 1)
                dve.wait_ge(rest_ready, 2)
                dve.tensor_scalar(has_rest[:, :], PS[0:1, 1, 0:1], 0.0, None, ALU.is_gt).then_inc(rest_ready, 1)

                def industry_scale(t):
                    dve.wait_ge(ind_ready, t + 1)
                    link(dve.tensor_scalar(rdg[:, t:t + 1], PS[:, t % 2, 0:1], 1.0, None, ALU.max))
                    dve.reciprocal(rdg[:, t:t + 1], rdg[:, t:t + 1]).then_inc(ind_scale, 1)

                dve.wait_ge(ex_done, BP)
                dve.reciprocal(rZ[:, :], Zs[:, :]).then_inc(rz_ready, 1)
                for t in range(3):
                    industry_scale(t)
                for q in range(BP):
                    dve.wait_ge(et_ready, q + 1)
                    dve.tensor_copy(ET[:, 4:8, q, :], PS[:, 5 + 2 * (q % 2), :].rearrange("p (t c) -> p t c", c=P)).then_inc(et_outD, 1)
                dve.wait_ge(kq_ready, 1)
                link(dve.tensor_reduce(kmx[:, :], PS[0:NT, 5, 0:P], AX.X, ALU.max))
                link(dve.tensor_scalar(kst[:, :], CN[0:NT, C_STEP:C_STEP + QUADS], kmx[:, 0:1], None, ALU.is_lt))
                dve.tensor_reduce(kq[:, :], kst[:, :], AX.X, ALU.add).then_inc(kq_ready, 1)
                dve.wait_ge(agg_out, 1)
                link(dve.tensor_scalar(AGM[:, :, :], AG[:, :, :], -1.0, None, ALU.add))
                dve.wait_ge(aex_done, 1)
                link(dve.tensor_scalar(AEX[:, :, :], AEX[:, :, :], 1.0, -1.0, ALU.min, ALU.add))
                dve.tensor_tensor(HE[:, :, :], AEX[:, :, :], AGM[:, :, :], ALU.max).then_inc(he_ready, 1)
                link(dve.tensor_tensor(AGM[:, :, :], AGM[:, :, :],
                                       wt(W_GE, F).unsqueeze(1).broadcast_to([P, BP, F]), ALU.mult))
                link(dve.tensor_reduce(ae[:, :], AGM[:, :, :], AX.X, ALU.add))
                dve.wait_ge(zero_set, 4)
                for par in range(2):
                    r = slice(64 * par, 64 * par + 64)
                    dve.tensor_scalar(SM[r, par:B:2], ae[r, :], 0.5, None, ALU.mult)
                    dve.tensor_copy(AGBD[r, par:B:2, :], AG[r, :, :])
                industry_scale(3)
                industry_scale(4)
                dve.wait_ge(kq_ready, 3)
                dve.tensor_copy(first_i[:, :], PS[0:1, 4, 0:NT + 1]).then_inc(first_ready, 1)
                industry_scale(5)
                dve.wait_ge(se_ready, 1)
                for par in range(2):
                    r = slice(64 * par, 64 * par + 64)
                    ins = dve.tensor_copy(SM[r, B + par:2 * B:2], PS[r, 5, 0:BP])
                link(ins)
                dve.tensor_tensor(DG[:, :, :], CN[:, C_ID2:C_ID2 + E].unsqueeze(1).broadcast_to([P, B, E]),
                                  spread(SM[:, B:2 * B], E), ALU.mult).then_inc(sm_ready, 1)
                industry_scale(6)
                dve.wait_ge(seB_out, 1)
                for t in range(NT):
                    link(dve.tensor_tensor(LGM[:, t % 2, :, :], SEB[:, :, :],
                                           limN[:, t:t + 1, :].broadcast_to([P, B, E]), ALU.min))
                    dve.tensor_reduce(HM[:, t, B:2 * B], LGM[:, t % 2, :, :], AX.X, ALU.max, negate=True)
                    if t == 0:
                        industry_scale(7)

            @block.tensor
            def _(pe):
                pe.wait_ge(weights_in, 16)
                pe.wait_ge(xT_in, 16 * BP)
                for t in range(NT):
                    for which, at in ((0, W_H), (1, W_IND)):
                        if t >= 2:
                            pe.wait_ge(xw_out if which else h_out, t - 1)
                        for q in range(BP):
                            ins = pe.matmul(PS[:, (2 * t + which) % 4, tile(q)], XT[:, q, tile(t)], wt(at, P),
                                            start=True, stop=True)
                        ins.then_inc(xw_ready if which else h_ready, 1)
                for q in range(BP):
                    for half in range(2):
                        u = 2 * q + half
                        if u >= 4:
                            pe.wait_ge(hT_outD if half else hT_outA, (u - 4) // 2 + 1)
                        pe.matmul(PS[:, 4 + u % 4, :], wt(W_H, P), XT[:, q, half * HALF:(half + 1) * HALF],
                                  start=True, stop=True).then_inc(hT_ready, 1)
                pe.wait_ge(consts_in, 16)
                pe.wait_ge(mask_ready, 1)
                pe.wait_ge(h_out, NT)
                for half in range(2):
                    ins = pe.matmul(PS[:, half, :], CN[0:64, C_ONE:C_ONE + P], maskT[0:64, half * HALF:(half + 1) * HALF],
                                    start=True, stop=True)
                ins.then_inc(degB_ready, 1)
                pe.wait_ge(hT_outA, BP)
                pe.wait_ge(hT_outD, BP)

                def node_scores(q):
                    for half in range(2):
                        u = 2 * q + half
                        if u >= 4:
                            pe.wait_ge(s_out, u - 3)
                        pe.matmul(PS[:, 4 + u % 4, :], wt(W_AN, P), HT[:, q, half * HALF:(half + 1) * HALF],
                                  start=True, stop=True).then_inc(s_ready, 1)

                node_scores(0)
                node_scores(1)
                pe.wait_ge(eff_ready, 1)
                pe.wait_ge(xw_out, NT)
                for half in range(2):
                    ins = pe.matmul(PS[:, 2 + half, :], CN[0:64, C_UP:C_UP + P], effT[0:64, half * HALF:(half + 1) * HALF],
                                    start=True, stop=True)
                ins.then_inc(rank_ready, 1)
                for t in range(NT):
                    for q in range(BP):
                        ins = pe.matmul(PS[:, 0, t * B + 2 * q:t * B + 2 * q + 2], HT[:, q, tile(t)], wt(W_GN, 2),
                                        start=True, stop=True)
                ins.then_inc(hg_ready, 1)
                node_scores(2)
                node_scores(3)

                pe.wait_ge(rest_ready, 1)
                pe.matmul(PS[0:1, 1, 0:1], rest_max[:, NT:NT + 1], CN[:, C_ONE:C_ONE + 1], start=True, stop=True).then_inc(rest_ready, 1)
                pe.wait_ge(rest_ready, 3)
                rest = pe.value_load(has_rest[0:1, 0:1], min_val=0, max_val=1)

                def industry(t):
                    if t == 0:
                        pe.wait_ge(rank_done, 1)
                        pe.wait_ge(hg_out, 1)
                        pe.wait_ge(one_ready, 1)
                    if t >= 2:
                        pe.wait_ge(ind_out, t - 1)
                    deg = PS[:, t % 2, 0:2]
                    for m in range(NT):
                        pe.matmul(deg, ADJH[:, m, tile(t)], ONR[:, :], start=(m == 0), stop=False, skip_group_check=True)
                    with pe.If(rest > 0):
                        for m in range(NT):
                            pe.matmul(deg, ADJL[:, m, tile(t)], ONR[:, :], start=False, stop=False, skip_group_check=True)
                    adjacent(pe, rest, t, PS[:, 2 + t % 2, :], lambda m: XWH[:, m, :],
                             lambda m: XWL[:, m, :]).then_inc(ind_ready, 1)

                for t in range(3):
                    industry(t)
                pe.wait_ge(s_out, 2 * BP)
                for q in range(BP):
                    pe.wait_ge(ex_done, q + 1)
                    if q >= 2:
                        pe.wait_ge(et_outA, q - 1)
                        pe.wait_ge(et_outD, q - 1)
                    for t in range(NT):
                        ins = pe.transpose(PS[:, 4 + 2 * (q % 2) + t // 4, (t % 4) * P:(t % 4 + 1) * P],
                                           EX[:, q, tile(t)], ident)
                    ins.then_inc(et_ready, 1)
                pe.wait_ge(et_outA, BP)
                pe.wait_ge(et_outD, BP)
                for q in range(BP):
                    for t in range(NT):
                        ins = pe.matmul(PS[:, 4, tile(q)], ET[:, t, q, :], HP[:, t, tile(q)],
                                        start=(t == 0), stop=(t == NT - 1))
                ins.then_inc(agg_ready, 1)
                pe.wait_ge(degT_ready, 1)
                pe.transpose(PS[0:NT, 5, 0:P], degE[:, :], ident).then_inc(kq_ready, 1)
                industry(3)
                pe.wait_ge(kq_ready, 2)
                pe.wait_ge(agg_out, 1)
                pe.matmul(PS[0:1, 4, 0:NT + 1], kq[:, :], CN[0:NT, C_TRI:C_TRI + NT + 1], start=True, stop=True).then_inc(kq_ready, 1)
                industry(4)
                pe.wait_ge(he_ready, 1)
                for a in range(2):
                    ins = pe.transpose(PS[:, 5, tile(a)], HE[:, 2 * a:2 * a + 2, :].rearrange("p a f -> p (a f)"), ident)
                ins.then_inc(heT_ready, 1)
                industry(5)
                pe.wait_ge(heT_out, 1)
                for q in range(BP):
                    ins = pe.matmul(PS[:, 6 + q % 2, tile(q // 2)], wt(W_FC + (q % 2) * P, P), HET[:, q // 2, :], start=True, stop=True)
                ins.then_inc(fce_ready, 1)
                pe.wait_ge(the_done, 2)
                for q in range(BP):
                    ins = pe.matmul(PS[:, 5, q:q + 1], THE[:, q, :], wt(W_AV, 1), start=True, stop=True)
                ins.then_inc(se_ready, 1)
                industry(6)
                pe.wait_ge(sm_ready, 1)
                pe.matmul(PS[:, 5, :], ones, DG[:, :, :].rearrange("p b e -> p (b e)"), start=True, stop=True).then_inc(seB_ready, 1)
                industry(7)

        GN = node_major(1)
        SEL = rounded("SEL", 6 * SLOT, [P, SLOTS, P])
        AGH = rounded("AGH", 6 * SLOT + SLOTS * P, [P, BF])
        AGL = rounded("AGL", 6 * SLOT + SLOTS * P + BF, [P, BF])
        TS = sb("TS", [P, SLOTS, 17])
        LG = sb("LG", [P, SLOTS, B])
        TH = sb("TH", [P, SLOTS, B])
        XC = sb("XC", [P, SLOTS, B])
        BE = sb("BE", [P, SLOTS, B])
        CC = sb("CC", [P, SLOTS, B])
        ZQ = sb("ZQ", [P, B])
        ZN = sb("ZN", [P, 2, B])
        S0 = arena[:, 0:SLOTS * BF].rearrange("p (s c) -> p s c", c=BF)
        S1 = arena[:, SLOTS * BF:SLOT].rearrange("p (s c) -> p s c", c=BF)
        POOLED = 2
        PE_MIXED = 3
        sel_ready, small_ready, gath_ready, ts_ready, lg_ready, th_ready, xc_ready, be_ready, cc_ready = (
            sem(s) for s in ("sel_ready", "small_ready", "gath_ready", "ts_ready", "lg_ready", "th_ready",
                             "xc_ready", "be_ready", "cc_ready"))
        d_ready, m_ready, z_ready, e_ready, t_ready, wp_ready, wd_ready, zd_ready, acc_done, g_done, zq_step, z_init, agh_ready, agl_ready = (
            sem(s) for s in ("d_ready", "m_ready", "z_ready", "e_ready", "t_ready", "wp_ready", "wd_ready",
                             "zd_ready", "acc_done", "g_done", "zq_step", "z_init", "agh_ready", "agl_ready"))

        def first_turns(eng):
            return [eng.value_load(first_i[0:1, t:t + 1], min_val=0, max_val=NT * QUADS) for t in range(NT + 1)]

        with nc.Block() as block:
            @block.sync
            def _(sp):
                sp.dma_start(XN.rearrange("p t (b f) -> p t b f", f=F),
                             x_nat.rearrange("(t p) b f -> p t b f", p=P)).then_inc(x_in, 16)
                sp.wait_ge(x_in, 16)

            @block.tensor
            def _(pe):
                first = first_turns(pe)

                def small(j):
                    pe.wait_ge(sel_ready, SLOTS * j + SLOTS)
                    for s in range(SLOTS):
                        ins = pe.matmul(PS[:, 4, s * 17:(s + 1) * 17], bits(SEL[:, s, :]), SM[:, :], start=True, stop=True)
                    ins.then_inc(small_ready, 1)

                def gather(s):
                    pe.matmul(PS[:, s, :], SEL[:, s, :], AGH[:, :], start=True, stop=False, skip_group_check=True)
                    pe.matmul(PS[:, s, :], SEL[:, s, :], AGL[:, :], start=False, stop=True,
                              skip_group_check=True).then_inc(gath_ready, 1)

                pe.wait_ge(agl_ready, 1)
                small(0)
                for s in range(SLOTS):
                    gather(s)
                for t in range(NT):
                    acc = PS[:, 5 + t % 2, :]
                    if t >= 2:
                        pe.wait_ge(g_done, t - 1)
                    pe.matmul(acc, zero16[:, 0:P], zero16[:, :], start=True, stop=False, skip_group_check=True)
                    with pe.Fori(first[t], first[t + 1]) as j:
                        for s in range(PE_MIXED):
                            pe.wait_ge(m_ready, SLOTS * j + (s + 1))
                            pe.matmul(PS[:, s, :], ident, S0[:, s, :], start=False, stop=True,
                                      skip_group_check=True).then_inc(z_ready, 1)
                        pe.wait_ge(ts_ready, j + 1)
                        small(j + 1)
                        for s in range(SLOTS):
                            if s < POOLED:
                                pe.wait_ge(wp_ready, POOLED * j + (s + 1))
                            else:
                                pe.wait_ge(wd_ready, (SLOTS - POOLED) * j + (s - POOLED + 1))
                            pe.matmul(acc, ident, S0[:, s, :], start=False, stop=True,
                                      skip_group_check=True).then_inc(acc_done, 1)
                            gather(s)

            @block.vector
            def _(dve):
                first = first_turns(dve)

                def one_hot(k, rank):
                    for s in range(SLOTS):
                        dve.tensor_scalar(SEL[:, s, :], rank, CN[:, bass.ds(C_RANK + s + k, 1)],
                                          None, ALU.is_equal).then_inc(sel_ready, 1)

                def small(j, tile_at):
                    dve.wait_ge(small_ready, j + 1)
                    dve.tensor_tensor(TS[:, :, :], PS[:, 4, 0:SLOTS * 17].rearrange("p (s c) -> p s c", c=17),
                                      HM[:, bass.ds(tile_at, 1), :].broadcast_to([P, SLOTS, 17]), ALU.add).then_inc(ts_ready, 1)
                    dve.wait_ge(ts_ready, j + 1)
                    dve.tensor_scalar(LG[:, :, :], TS[:, :, B:2 * B], low[:, bass.ds(tile_at, 1)], 0.0, ALU.max,
                                      ALU.min).then_inc(lg_ready, 1)

                dve.wait_ge(agh_ready, 1)
                dve.tensor_tensor(AGL[:, :], AGBD[:, :, :].rearrange("p b f -> p (b f)"), bits(AGH[:, :]),
                                  ALU.subtract).then_inc(agl_ready, 1)
                one_hot(0, rankT[:, tile(0)])
                small(0, 0)
                for t in range(NT):
                    if t >= 2:
                        dve.wait_ge(g_done, t - 1)
                    dve.memset(ZN[:, t % 2, :], 0.0).then_inc(z_init, 1)
                    dve.wait_ge(z_init, t + 1)
                    with dve.Fori(first[t], first[t + 1]) as j:
                        k = nc.s_assert_within(SLOTS * (j - first[t]), 0, E - SLOTS, skip_runtime_bounds_check_because=
                                               "a tile takes at most E / SLOTS turns")
                        if t + 1 < NT:
                            more = nc.s_assert_within(j + 1 < first[t + 1], 0, 1, skip_runtime_bounds_check_because="a comparison")
                            k_next = nc.s_assert_within((k + SLOTS) * more, 0, E, skip_runtime_bounds_check_because=
                                                        "k is at most E - SLOTS")
                            t_next = nc.s_assert_within(t + 1 - more, t, t + 1, skip_runtime_bounds_check_because="more is 0 or 1")
                        else:
                            k_next, t_next = k + SLOTS, t

                        for s in range(SLOTS):
                            dve.wait_ge(gath_ready, SLOTS * j + (s + 1))
                            dve.tensor_tensor(S0[:, s, :], HP[:, t, :], PS[:, s, :], ALU.subtract).then_inc(d_ready, 1)
                        one_hot(k_next, rankT[:, bass.ds(t_next * P, P)])
                        def mixed(s):
                            dve.wait_ge(m_ready, SLOTS * j + (s + 1))
                            dve.tensor_tensor(S0[:, s, :], S0[:, s, :], PS[:, s, :], ALU.add).then_inc(zd_ready, 1)

                        def elu(s):
                            dve.wait_ge(e_ready, SLOTS * j + (s + 1))
                            z = PS if s < PE_MIXED else S0
                            dve.scalar_tensor_tensor(S0[:, s, :], S1[:, s, :], 1.0, z[:, s, :], ALU.min,
                                                     ALU.max).then_inc(t_ready, 1)

                        def weigh(s):
                            dve.wait_ge(t_ready, SLOTS * j + (s + 1))
                            dve.tensor_tensor(groups(S0[:, s, :]), groups(S0[:, s, :]), spread(CC[:, s, :]),
                                              ALU.mult).then_inc(wd_ready, 1)

                        elu(0)
                        dve.wait_ge(cc_ready, j + 1)
                        dve.tensor_reduce(ZQ[:, :], CC[:, :, :].rearrange("p s b -> p b s"), AX.X, ALU.add).then_inc(zq_step, 1)
                        elu(1)
                        dve.wait_ge(zq_step, 2 * j + 1)
                        dve.tensor_tensor(ZN[:, t % 2, :], ZN[:, t % 2, :], ZQ[:, :], ALU.add).then_inc(zq_step, 1)
                        mixed(3)
                        elu(2)
                        dve.wait_ge(th_ready, j + 1)
                        small(j + 1, t_next)
                        weigh(2)
                        elu(3)
                        weigh(3)
                    dve.wait_ge(zq_step, 2 * first[t + 1])
                    dve.reciprocal(ZN[:, t % 2, :], ZN[:, t % 2, :]).then_inc(rz_ready, 1)

            @block.scalar
            def _(act):
                first = first_turns(act)
                act.activation(AGH[:, :], AGBD[:, :, :].rearrange("p b f -> p (b f)"), ACT.Copy).then_inc(agh_ready, 1)

                def small(j):
                    act.wait_ge(ts_ready, j + 1)
                    act.activation(TH[:, :, :], TS[:, :, 0:B], ACT.Tanh).then_inc(th_ready, 1)
                    act.wait_ge(lg_ready, j + 1)
                    act.activation(XC[:, :, :], LG[:, :, :], ACT.Exp).then_inc(xc_ready, 1)
                    act.wait_ge(th_ready, j + 1)
                    act.activation(BE[:, :, :], TH[:, :, :], ACT.Copy, scale=0.5, bias=0.5).then_inc(be_ready, 1)

                small(0)
                for t in range(NT):
                    with act.Fori(first[t], first[t + 1]) as j:
                        for s in range(SLOTS):
                            if s < PE_MIXED:
                                act.wait_ge(z_ready, PE_MIXED * j + (s + 1))
                            else:
                                act.wait_ge(zd_ready, (SLOTS - PE_MIXED) * j + (s - PE_MIXED + 1))
                            act.activation(S1[:, s, :], (PS if s < PE_MIXED else S0)[:, s, :], ACT.Exp, bias=CN[:, C_M1:C_M1 + 1]).then_inc(e_ready, 1)
                        small(j + 1)
                    act.wait_ge(rz_ready, 2 + t)
                    act.wait_ge(acc_done, SLOTS * first[t + 1])
                    for b in range(B):
                        c = slice(b * F, (b + 1) * F)
                        ins = act.activation(GN[:, t, c], PS[:, 5 + t % 2, c], ACT.Copy, bias=-1.0, scale=ZN[:, t % 2, b:b + 1])
                    ins.then_inc(g_done, 1)

            @block.gpsimd
            def _(pool):
                first = first_turns(pool)
                for t in range(NT):
                    with pool.Fori(first[t], first[t + 1]) as j:
                        pool.wait_ge(be_ready, j + 1)
                        for s in range(SLOTS):
                            pool.wait_ge(d_ready, SLOTS * j + (s + 1))
                            if s == 1:
                                pool.wait_ge(xc_ready, j + 1)
                                pool.tensor_tensor(CC[:, :, :], XC[:, :, :], TS[:, :, 16:17].broadcast_to([P, SLOTS, B]),
                                                   ALU.mult).then_inc(cc_ready, 1)
                            pool.tensor_tensor(groups(S0[:, s, :]), groups(S0[:, s, :]), spread(BE[:, s, :]),
                                               ALU.mult).then_inc(m_ready, 1)
                        pool.wait_ge(cc_ready, j + 1)
                        for s in range(POOLED):
                            pool.wait_ge(t_ready, SLOTS * j + (s + 1))
                            pool.tensor_tensor(groups(S0[:, s, :]), groups(S0[:, s, :]), spread(CC[:, s, :]),
                                               ALU.mult).then_inc(wp_ready, 1)

        FT = feature_major(0)
        X1 = node_major(3)
        TNH = feature_major(2)
        HRING = 3
        KP = sb("KP", [P, BP, NT, 2])
        navc = sb("navc", [P, 1])
        c_in, gT_r, iT_r, gT_o, iT_o, fc_ready, tn_done, av_done, kap_ready, gx_ready, kap_scaled, ig_scaled, ig_ready = (
            sem(s) for s in ("c_in", "gT_r", "iT_r", "gT_o", "iT_o", "fc_ready", "tn_done", "av_done", "kap_ready",
                             "gx_ready", "kap_scaled", "ig_scaled", "ig_ready"))
        xr_ready, x1_scales, x1_centredP, x1_centredD, x1_doneP, x1_doneD = (
            sem(s) for s in ("xr_ready", "x1_scales", "x1_centredP", "x1_centredD", "x1_doneP", "x1_doneD"))

        def x1_norm(engine, q, half):
            c = slice(4 * half, 4 * half + 4)
            return norm_apply(engine, X1[:, c, tile(q)], 2 * NT * q + 8 * half, 4, 2)

        with nc.Block() as block:
            @block.vector
            def _(dve):
                dve.tensor_scalar(navc[:, :], wt(W_AV, 1), -1.0, None, ALU.mult).then_inc(c_in, 1)
                for q in range(BP):
                    x = X1[:, :, tile(q)]
                    dve.wait_ge(kap_ready, q + 1)
                    dve.tensor_scalar(KP[:, q, :, :], KP[:, q, :, :], 0.5, 0.5, ALU.mult, ALU.add).then_inc(kap_scaled, 1)
                    dve.wait_ge(kap_scaled, q + 1)
                    dve.wait_ge(ig_ready, q + 1)
                    v = x.rearrange("p t (b f) -> p t b f", f=F)
                    dve.tensor_tensor(v, v, spread_feature(KP[:, q, :, :]), ALU.mult).then_inc(ig_scaled, 1)
                    dve.wait_ge(ig_scaled, q + 1)
                    dve.wait_ge(gx_ready, q + 1)
                    dve.tensor_tensor(x, x, GN[:, :, tile(q)], ALU.add).then_inc(xr_ready, 1)
                    dve.wait_ge(xr_ready, q + 1)
                    first = 2 * NT * q
                    norm_stats(dve, lambda i: X1[:, (i - first) // 2, (2 * q + i % 2) * F:(2 * q + i % 2 + 1) * F],
                               range(first, first + 2 * NT))
                    norm_scales(dve, 2 * NT, first)
                    dve.nop().then_inc(x1_scales, 1)
                    centre, scale = x1_norm(dve, q, 1)
                    centre().then_inc(x1_centredD, 1)
                    dve.wait_ge(x1_centredD, q + 1)
                    scale().then_inc(x1_doneD, 1)

            @block.gpsimd
            def _(pool):
                def apply_norm(q):
                    centre, scale = x1_norm(pool, q, 0)
                    pool.wait_ge(x1_scales, q + 1)
                    centre().then_inc(x1_centredP, 1)
                    pool.wait_ge(x1_centredP, q + 1)
                    scale().then_inc(x1_doneP, 1)

                for q in range(BP):
                    pool.wait_ge(iT_r, q + 1)
                    pool.tensor_tensor(X1[:, :, tile(q)], IND[:, :, tile(q)], GN[:, :, tile(q)], ALU.subtract).then_inc(ig_ready, 1)
                    pool.wait_ge(gT_r, q + 1)
                    pool.wait_ge(ig_ready, q + 1)
                    pool.tensor_tensor(GN[:, :, tile(q)], GN[:, :, tile(q)], XN[:, :, tile(q)], ALU.add).then_inc(gx_ready, 1)
                    if q >= 2:
                        apply_norm(q - 2)
                apply_norm(BP - 2)
                apply_norm(BP - 1)

            @block.scalar
            def _(act):
                def features_out(q):
                    for ready, dst, bank, done in ((gT_r, q % 2, 0, gT_o), (iT_r, 2 + q % 2, 2, iT_o)):
                        act.wait_ge(ready, q + 1)
                        if q >= 2:
                            act.wait_ge(fc_ready, 8 * (q - 1))
                        act.activation(FT[:, dst, :], PS[:, bank:bank + 2, :].rearrange("p a c -> p (a c)"), ACT.Copy).then_inc(done, 1)

                def kappa(q):
                    act.wait_ge(av_done, 2 * q + 2)
                    act.activation(KP[:, q, :, :], PS[:, 7, q * 2 * NT:(q + 1) * 2 * NT].rearrange("p (t b) -> p t b", b=2), ACT.Tanh,
                                   scale=0.5).then_inc(kap_ready, 1)

                features_out(0)
                for b in range(B):
                    if b >= 2:
                        act.wait_ge(av_done, b - 1)
                    for v in range(4 * b, 4 * b + 4):
                        act.wait_ge(fc_ready, v + 1)
                        half = v % 2
                        act.activation(TNH[:, (v // 2) % 4, half * HALF:(half + 1) * HALF], PS[:, 4 + v % HRING, :], ACT.Tanh,
                                       bias=wt(W_FCB, 1)).then_inc(tn_done, 1)
                    if b % 2 == 0 and b // 2 + 1 < BP:
                        features_out(b // 2 + 1)
                    if b % 2 == 0 and b >= 2:
                        kappa(b // 2 - 1)
                kappa(BP - 1)

            @block.tensor
            def _(pe):
                def turn(q):
                    if q >= 1:
                        pe.wait_ge(gT_o, q)
                    for t in range(NT):
                        ins = pe.transpose(PS[:, t // 4, (t % 4) * P:(t % 4 + 1) * P], GN[:, t, tile(q)], ident)
                    ins.then_inc(gT_r, 1)
                    if q >= 1:
                        pe.wait_ge(iT_o, q)
                    for t in range(NT):
                        ins = pe.transpose(PS[:, 2 + t // 4, (t % 4) * P:(t % 4 + 1) * P], IND[:, t, tile(q)], ident)
                    ins.then_inc(iT_r, 1)

                def hidden(b):
                    q = b // 2
                    for v in range(4 * b, 4 * b + 4):
                        w, half = (v // 2) % 2, v % 2
                        pe.wait_ge(iT_o if w else gT_o, q + 1)
                        if v >= HRING:
                            pe.wait_ge(tn_done, v - HRING + 1)
                        pe.matmul(PS[:, 4 + v % HRING, :], wt(W_FC + (b % 2) * P, P),
                                  FT[:, (2 if w else 0) + q % 2, half * HALF:(half + 1) * HALF],
                                  start=True, stop=True).then_inc(fc_ready, 1)

                def score(b):
                    if b == 0:
                        pe.wait_ge(c_in, 1)
                    pe.wait_ge(tn_done, 4 * b + 4)
                    for t in range(NT):
                        at = b // 2 * 2 * NT + 2 * t + b % 2
                        for w, a in ((0, navc[:, :]), (1, wt(W_AV, 1))):
                            ins = pe.matmul(PS[:, 7, at:at + 1], TNH[:, (2 * b + w) % 4, tile(t)], a,
                                            start=(w == 0), stop=(w == 1))
                    ins.then_inc(av_done, 1)

                turn(0)
                for b in range(B):
                    hidden(b)
                    if b % 2 == 0 and b // 2 + 1 < BP:
                        turn(b // 2 + 1)
                    if b >= 1:
                        score(b - 1)
                score(B - 1)

        free_semaphores()

        X1T = feature_major(0)
        VH = rounded("VH", 5 * SLOT, [P, NT, BF])
        VL = rounded("VL", 6 * SLOT, [P, NT, BF])
        AV = node_major(1)
        EF = feature_major(2)
        RING = 3
        KS = [rounded(f"KS{i}", (4 + i) * SLOT, [P, N]) for i in range(2)]
        QH = [rounded(f"QH{i}", (4 + i) * SLOT + N, [P, N]) for i in range(2)]
        QL = [rounded(f"QL{i}", (4 + i) * SLOT + 2 * N, [P, N]) for i in range(2)]
        EHL = rounded("EHL", 6 * SLOT, [P, 4, N])
        EHM = [rounded(f"EHM{i}", (4 + i) * SLOT + 3 * N, [P, N]) for i in range(2)]
        EH = [EHL[:, 0, :], EHL[:, 1, :], EHM[0][:, :]]
        EL = [EHL[:, 2, :], EHL[:, 3, :], EHM[1][:, :]]
        NMX = sb("NMX", [P, B * NT])
        ZZ = sb("ZZ", [P, B * NT])
        RZ = sb("RZ", [P, B * NT])
        AVN = sb("AVN", [P, RING, 2 * F], F32R)
        SUMT = sb("SUMT", [P, NT, F])
        xT1_ready, xT1_outA, xT1_outD, v_ready, v_h, v_out, av1_ready, av1_outA, av1_outD = (
            sem(s) for s in ("xT1_ready", "xT1_outA", "xT1_outD", "v_ready", "v_h", "v_out", "av1_ready", "av1_outA", "av1_outD"))
        k_ready, k_h, k_out, q_ready, q_h, q_out, s1_ready, max_ready, p_ready, eh_ready, el_ready = (
            sem(s) for s in ("k_ready", "k_h", "k_out", "q_ready", "q_h", "q_out", "s1_ready", "max_ready", "p_ready",
                             "eh_ready", "el_ready"))
        rz1_ready, avn_h, avn_ready, pv_done, o_copied, oT_ready, o_sum, o_out, norm_ready, centred, x2_done = (
            sem(s) for s in ("rz1_ready", "avn_h", "avn_ready", "pv_done", "o_copied", "oT_ready", "o_sum", "o_out",
                             "norm_ready", "centred", "x2_done"))
        TURNS = B * NT
        LAG = RING

        with nc.Block() as block:
            @block.tensor
            def _(pe):
                rest = pe.value_load(has_rest[0:1, 0:1], min_val=0, max_val=1)
                for t in range(NT):
                    if t >= 4:
                        pe.wait_ge(xT1_outD if t % 2 else xT1_outA, (t - 4) // 2 + 1)
                    for q in range(BP):
                        ins = pe.transpose(PS[:, t % 4, tile(q)], X1[:, t, tile(q)], ident)
                    ins.then_inc(xT1_ready, 1)
                pe.wait_ge(xT1_outA, 4)
                pe.wait_ge(xT1_outD, 4)
                for t in range(NT):
                    if t >= 2:
                        pe.wait_ge(v_out, t - 1)
                    for q in range(BP):
                        ins = pe.matmul(PS[:, 4 + t % 2, tile(q)], X1T[:, q, tile(t)], wt(W_V, P), start=True, stop=True)
                    ins.then_inc(v_ready, 1)
                pe.wait_ge(v_out, NT)
                for t in range(NT):
                    if t >= 2:
                        pe.wait_ge(av1_outD if t % 2 else av1_outA, t // 2)
                    adjacent(pe, rest, t, PS[:, 4 + t % 2, :], lambda m: VH[:, m, :], lambda m: VL[:, m, :]).then_inc(av1_ready, 1)

                def project(b, at, ready, freed, n):
                    if n:
                        pe.wait_ge(freed, n)
                    for half in range(2):
                        ins = pe.matmul(PS[:, 4 + half, :], wt(at + (b % 2) * P, P), X1T[:, b // 2, half * HALF:(half + 1) * HALF],
                                        start=True, stop=True)
                    ins.then_inc(ready, 1)

                def scores(i):
                    b, m = i // NT, i % NT
                    if m == 0:
                        pe.wait_ge(k_out, b + 1)
                        pe.wait_ge(q_out, b + 1)
                    if i >= 2:
                        pe.wait_ge(p_ready, i - 1)
                    for half in range(2):
                        c = slice(half * HALF, (half + 1) * HALF)
                        acc = PS[:, 2 * (i % 2) + half, :]
                        pe.matmul(acc, KS[b % 2][:, tile(m)], QH[b % 2][:, c], start=True, stop=False)
                        ins = pe.matmul(acc, KS[b % 2][:, tile(m)], QL[b % 2][:, c], start=False, stop=True)
                    ins.then_inc(s1_ready, 1)

                def values(i):
                    b, m = i // NT, i % NT
                    pe.wait_ge(avn_ready, i + 1)
                    pe.wait_ge(eh_ready, i + 1)
                    pe.wait_ge(el_ready, i + 1)
                    if m == 0 and b >= 1:
                        pe.wait_ge(o_copied, b)
                    for half in range(2):
                        c = slice(half * HALF, (half + 1) * HALF)
                        acc = PS[:, 6 + half, :]
                        pe.matmul(acc, AVN[:, i % RING, :], EH[i % RING][:, c], start=(m == 0), stop=False)
                        ins = pe.matmul(acc, AVN[:, i % RING, :], EL[i % RING][:, c], start=False, stop=(m == NT - 1))
                    ins.then_inc(pv_done, 1)

                def turn_back(b):
                    pe.wait_ge(o_copied, b + 1)
                    pe.wait_ge(q_out, min(b + 3, B))
                    for t in range(NT):
                        ins = pe.transpose(PS[:, 4 + t // 4, (t % 4) * P:(t % 4 + 1) * P], EF[:, RING, tile(t)], ident)
                    ins.then_inc(oT_ready, 1)

                pe.wait_ge(av1_outA, 4)
                pe.wait_ge(av1_outD, 4)
                project(0, W_K, k_ready, k_out, 0)
                project(0, W_Q, q_ready, k_out, 1)
                for i in range(TURNS + LAG):
                    b, m = i // NT, i % NT
                    if i < TURNS:
                        scores(i)
                    if m == 0 and b + 1 < B:
                        if b >= 2:
                            pe.wait_ge(o_sum, b - 1)
                        project(b + 1, W_K, k_ready, q_out, b + 1)
                    if m == 2 and b + 1 < B:
                        project(b + 1, W_Q, q_ready, k_out, b + 2)
                    if i >= LAG:
                        values(i - LAG)
                    if m == 4 and 1 <= b < B:
                        turn_back(b - 1)
                turn_back(B - 1)

            @block.scalar
            def _(act):
                for t in range(0, NT, 2):
                    act.wait_ge(xT1_ready, t + 1)
                    act.activation(X1T[:, :, tile(t)], PS[:, t % 4, :].rearrange("p (q c) -> p q c", c=P), ACT.Copy).then_inc(xT1_outA, 1)
                for t in range(NT):
                    act.wait_ge(v_ready, t + 1)
                    act.activation(VH[:, t, :], PS[:, 4 + t % 2, :], ACT.Copy).then_inc(v_h, 1)
                for t in range(0, NT, 2):
                    act.wait_ge(av1_ready, t + 1)
                    act.activation(AV[:, t, :], PS[:, 4, :], ACT.Copy).then_inc(av1_outA, 1)

                def high(b, ready, dst, at, done):
                    act.wait_ge(ready, b + 1)
                    if b >= 2:
                        act.wait_ge(s1_ready, NT * (b - 1))
                    act.activation(dst[b % 2][:, :], PS[:, 4:6, :].rearrange("p a c -> p (a c)"), ACT.Identity,
                                   bias=wt(at, 1)).then_inc(done, 1)

                def sums_out(act, b):
                    act.wait_ge(pv_done, NT * (b + 1))
                    if b >= 1:
                        act.wait_ge(oT_ready, b)
                    act.activation(EF[:, RING, :], PS[:, 6:8, :].rearrange("p a c -> p (a c)"), ACT.Copy).then_inc(o_copied, 1)

                act.wait_ge(av1_ready, NT)
                high(0, k_ready, KS, W_BK, k_h)
                high(0, q_ready, QH, W_BQ, q_h)
                for i in range(TURNS):
                    b, m = i // NT, i % NT
                    act.wait_ge(max_ready, i + 1)
                    if i >= RING:
                        act.wait_ge(el_ready, i - RING + 1)
                    bank = 2 * (i % 2)
                    act.activation(EF[:, i % RING, :], PS[:, bank:bank + 2, :].rearrange("p a c -> p (a c)"), ACT.Exp,
                                   bias=NMX[:, i:i + 1], accum_out=ZZ[:, i:i + 1]).then_inc(p_ready, 1)
                    if i >= RING:
                        act.wait_ge(pv_done, i - RING + 1)
                    act.wait_ge(p_ready, i + 1)
                    act.activation(EH[i % RING], EF[:, i % RING, :], ACT.Copy).then_inc(eh_ready, 1)
                    if m == 0 and b + 1 < B:
                        high(b + 1, k_ready, KS, W_BK, k_h)
                    if m == 2 and b >= 1:
                        sums_out(act, b - 1)
                    if m == 2 and b + 1 < B:
                        high(b + 1, q_ready, QH, W_BQ, q_h)
                sums_out(act, B - 1)

            @block.gpsimd
            def _(pool):
                def apply_norm(q, k):
                    half, x = k % 2, X1[:, (k % 2) * 4:(k % 2) * 4 + 4, tile(q)]
                    centre, scale = norm_apply(pool, x, 2 * NT * q + 8 * half, 4, 2)
                    if k < 2:
                        pool.wait_ge(norm_ready, q + 1)
                        centre().then_inc(centred, 1)
                    else:
                        pool.wait_ge(centred, 2 * q + half + 1)
                        scale().then_inc(x2_done, 1)

                for i in range(TURNS):
                    pool.wait_ge(eh_ready, i + 1)
                    if i >= RING:
                        pool.wait_ge(pv_done, i - RING + 1)
                    pool.tensor_tensor(EL[i % RING], EF[:, i % RING, :], bits(EH[i % RING]), ALU.subtract).then_inc(el_ready, 1)
                    b, m = i // NT, i % NT
                    if b % 2 == 1 and b >= 3 and m < 4:
                        apply_norm(b // 2 - 1, m)
                for k in range(4):
                    apply_norm(BP - 1, k)

            @block.vector
            def _(dve):
                for t in range(1, NT, 2):
                    dve.wait_ge(xT1_ready, t + 1)
                    dve.tensor_copy(X1T[:, :, tile(t)], PS[:, t % 4, :].rearrange("p (q c) -> p q c", c=P)).then_inc(xT1_outD, 1)
                for t in range(NT):
                    dve.wait_ge(v_h, t + 1)
                    dve.tensor_tensor(VL[:, t, :], PS[:, 4 + t % 2, :], bits(VH[:, t, :]), ALU.subtract).then_inc(v_out, 1)
                for t in range(1, NT, 2):
                    dve.wait_ge(av1_ready, t + 1)
                    dve.tensor_copy(AV[:, t, :], PS[:, 5, :]).then_inc(av1_outD, 1)
                dve.wait_ge(av1_outA, 4)
                dve.wait_ge(av1_outD, 4)

                def low(b, w):
                    if w == 0:
                        dve.wait_ge(k_h, b + 1)
                        r, dst, src, at, done = slice(64, 128), KS[b % 2], KS[b % 2], W_BK, k_out
                    else:
                        dve.wait_ge(q_h, b + 1)
                        r, dst, src, at, done = slice(0, 128), QL[b % 2], QH[b % 2], W_BQ, q_out
                    dve.scalar_tensor_tensor(dst[r, :], PS[r, 4:6, :].rearrange("p a c -> p (a c)"), WT[r, at:at + 1],
                                             bits(src[r, :]), ALU.add, ALU.subtract).then_inc(done, 1)

                def scaled_values(i):
                    b, m = i // NT, i % NT
                    dve.wait_ge(p_ready, i + 1)
                    dve.reciprocal(RZ[:, i:i + 1], ZZ[:, i:i + 1]).then_inc(rz1_ready, 1)
                    dve.wait_ge(rz1_ready, i + 1)
                    if i >= RING:
                        dve.wait_ge(pv_done, i - RING + 1)
                    av = AV[:, m, b * F:(b + 1) * F]
                    dve.tensor_scalar(AVN[:, i % RING, 0:F], av, RZ[:, i:i + 1], None, ALU.mult).then_inc(avn_h, 1)
                    dve.wait_ge(avn_h, i + 1)
                    dve.scalar_tensor_tensor(AVN[:, i % RING, F:2 * F], av, RZ[:, i:i + 1], bits(AVN[:, i % RING, 0:F]),
                                             ALU.mult, ALU.subtract).then_inc(avn_ready, 1)

                def residual(b):
                    dve.wait_ge(oT_ready, b + 1)
                    dve.tensor_reduce(SUMT[:, :, :], PS[:, 4:6, :].rearrange("p a (t k f) -> p (a t) f k", k=2, f=F), AX.X,
                                      ALU.add).then_inc(o_sum, 1)

                def statistics(b):
                    x2b = X1[:, :, b * F:(b + 1) * F]
                    dve.wait_ge(o_sum, b + 1)
                    dve.scalar_tensor_tensor(x2b, SUMT[:, :, :], 0.0, x2b, ALU.max, ALU.add).then_inc(o_out, 1)
                    dve.wait_ge(o_out, b + 1)
                    norm_stats(dve, lambda i: X1[:, i // 2 % NT, b * F:(b + 1) * F], range(NT * (b - b % 2) + b % 2, NT * (b - b % 2) + 2 * NT, 2))

                def norm_pair(q):
                    norm_scales(dve, 2 * NT, 2 * NT * q)
                    dve.nop().then_inc(norm_ready, 1)

                low(0, 0)
                low(0, 1)
                for i in range(TURNS + 1):
                    if i < TURNS:
                        dve.wait_ge(s1_ready, i + 1)
                        bank = 2 * (i % 2)
                        dve.tensor_reduce(NMX[:, i:i + 1], PS[:, bank:bank + 2, :], AX.XY, ALU.max, negate=True).then_inc(max_ready, 1)
                    if i >= 1:
                        scaled_values(i - 1)
                    b, m = i // NT, i % NT
                    if m == 1 and b + 1 < B:
                        low(b + 1, 0)
                    if m == 3 and b + 1 < B:
                        low(b + 1, 1)
                    if m == 5 and 1 <= b < B:
                        residual(b - 1)
                    if m == 6 and 1 <= b < B:
                        statistics(b - 1)
                    if m == 7 and b % 2 == 0 and 2 <= b < B:
                        norm_pair(b // 2 - 1)
                residual(B - 1)
                statistics(B - 1)
                norm_pair(BP - 1)

        X2 = node_major(3)
        XA = node_major(4)
        XX = sb("XX", [P, B, 2, F])
        ZH = rounded("ZH", 5 * SLOT, [P, NT, BF])
        ZL = rounded("ZL", 6 * SLOT, [P, NT, BF])
        XG = node_major(1)
        X3 = node_major(0)
        W01F = arena[:, 0:D * F]
        W2F = arena[:, D * F:2 * D * F]
        EB = arena[0:D, 2 * D * F:2 * D * F + N + F]
        WH = rounded("WH", 2 * SLOT, [P, 2, D * F])
        WL = rounded("WL", 2 * SLOT + 2 * D * F, [P, 2, D * F])
        KH = rounded("KH", 5 * SLOT, [P, 2, B, P])
        KL = rounded("KL", 5 * SLOT + 2 * B * P, [P, 2, B, P])
        GK = rounded("GK", 6 * SLOT, [P, 2, B, P])
        GS = arena[:, 6 * SLOT + 2 * B * P:7 * SLOT].rearrange("p (r b k f) -> p r b k f", r=2, k=2, f=F)
        BO = SUMT[:, :, :]
        w_in, wh_ready, wl_ready, eb_ready, bo_ready, bo_out, init_done = (
            sem(s) for s in ("w_in", "wh_ready", "wl_ready", "eb_ready", "bo_ready", "bo_out", "init_done"))
        z_h, z_l, a1_ready, a1_outA, a1_outD, a2_ready, a2_out = (
            sem(s) for s in ("z_h", "z_l", "a1_ready", "a1_outA", "a1_outD", "a2_ready", "a2_out"))
        kT_ready, k2_h, k2_l, gs_h, gs_l, gT_ready, g2_out, y_ready, acc_step, x3_done = (
            sem(s) for s in ("kT_ready", "k2_h", "k2_l", "gs_h", "gs_l", "gT_ready", "g2_out", "y_ready", "acc_step", "x3_done"))
        xx_ready = sem("xx_ready")
        DH = 8

        rounds = [(0, None)]
        for t in range(NT):
            rounds += [(t, 0), (t, 1)] + ([(t + 1, None)] if t + 1 < NT else []) + [(t, 2), (t, 3)]

        def turn_round(t):
            return rounds.index((t, None))

        def product_round(t, j):
            return rounds.index((t, j))

        with nc.Block() as block:
            @block.sync
            def _(sp):
                sp.dma_start(W01F, w01).then_inc(w_in, 16)
                sp.dma_start(W2F, w2).then_inc(w_in, 16)
                sp.dma_start(EB, emb_bias).then_inc(w_in, 16)

            @block.gpsimd
            def _(pool):
                pool.wait_ge(w_in, 48)
                for k, w in ((0, W01F), (1, W2F)):
                    pool.tensor_copy(WH[:, k, :], w).then_inc(wh_ready, 1)
                pool.wait_ge(wh_ready, 2)
                for k, w in ((0, W01F), (1, W2F)):
                    pool.tensor_tensor(WL[:, k, :], w, bits(WH[:, k, :]), ALU.subtract).then_inc(wl_ready, 1)
                pool.wait_ge(bo_out, 1)
                pool.wait_ge(wl_ready, 2)
                for t in range(NT):
                    pool.tensor_tensor(groups(X3[:, t, :]), groups(X2[:, t, :]),
                                       BO[:, t:t + 1, :].broadcast_to([P, B, F]), ALU.add).then_inc(init_done, 1)
                pool.wait_ge(a1_outA, 4)
                pool.wait_ge(a1_outD, 4)
                for t in range(NT):
                    if t >= 1:
                        pool.wait_ge(kT_ready, t)
                    pool.tensor_copy(XX[:, :, 0, :], groups(X2[:, t, :])).then_inc(xx_ready, 1)
                    pool.tensor_copy(XX[:, :, 1, :], groups(XA[:, t, :])).then_inc(xx_ready, 1)
                    pool.wait_ge(gs_h, t + 1)
                    pool.tensor_tensor(GS[:, t % 2, :, 1, :], groups(XG[:, t, :]), GS[:, t % 2, :, 0, :], ALU.subtract).then_inc(gs_l, 1)

            @block.scalar
            def _(act):
                for t in range(NT):
                    act.activation(ZH[:, t, :], X2[:, t, :], ACT.Copy).then_inc(z_h, 1)
                act.wait_ge(bo_ready, 1)
                act.activation(BO[:, :, :], PS[:, 7, :].rearrange("p (t f) -> p t f", f=F), ACT.Copy).then_inc(bo_out, 1)
                for t in range(0, NT, 2):
                    act.wait_ge(a1_ready, t + 1)
                    act.activation(XA[:, t, :], PS[:, t % 2, :], ACT.Copy).then_inc(a1_outA, 1)
                act.wait_ge(a1_ready, NT)
                act.wait_ge(a1_outA, 4)
                act.wait_ge(a1_outD, 4)
                for t in range(NT):
                    act.activation(ZH[:, t, :], XA[:, t, :], ACT.Copy).then_inc(z_h, 1)
                act.wait_ge(a2_ready, NT)

                def high_parts(t):
                    if t >= 2:
                        act.wait_ge(gT_ready, t - 1)
                    act.wait_ge(a2_out, t + 1)
                    act.activation(GS[:, t % 2, :, 0, :].bitcast(F32R), groups(XG[:, t, :]), ACT.Copy).then_inc(gs_h, 1)

                high_parts(0)
                for t in range(NT):
                    at = 4 * (turn_round(t) % 2)
                    for h in range(2):
                        act.wait_ge(kT_ready, t + 1)
                        if t >= 2:
                            act.wait_ge(y_ready, 4 * (t - 1))
                        act.activation(KH[:, t % 2, 4 * h:4 * h + 4, :], PS[:, at + h, :].rearrange("p (b c) -> p b c", c=P),
                                       ACT.Copy).then_inc(k2_h, 1)
                    if t + 1 < NT:
                        high_parts(t + 1)
                    for h in range(2):
                        act.wait_ge(gT_ready, t + 1)
                        act.activation(GK[:, t % 2, 4 * h:4 * h + 4, :], PS[:, at + 2 + h, :].rearrange("p (b c) -> p b c", c=P),
                                       ACT.Copy).then_inc(g2_out, 1)

            @block.vector
            def _(dve):
                for t in range(NT):
                    dve.wait_ge(z_h, t + 1)
                    dve.tensor_tensor(ZL[:, t, :], X2[:, t, :], bits(ZH[:, t, :]), ALU.subtract).then_inc(z_l, 1)
                for t in range(1, NT, 2):
                    dve.wait_ge(a1_ready, t + 1)
                    dve.tensor_copy(XA[:, t, :], PS[:, t % 2, :]).then_inc(a1_outD, 1)
                dve.wait_ge(a1_outA, 4)
                for t in range(NT):
                    dve.wait_ge(z_h, NT + t + 1)
                    dve.tensor_tensor(ZL[:, t, :], XA[:, t, :], bits(ZH[:, t, :]), ALU.subtract).then_inc(z_l, 1)
                for t in range(NT):
                    dve.wait_ge(a2_ready, t + 1)
                    dve.scalar_tensor_tensor(XG[:, t, :], PS[:, 2 + t % 2, :], 2.0, X2[:, t, :],
                                             ALU.mult, ALU.subtract).then_inc(a2_out, 1)

                def low_parts(t):
                    at = 4 * (turn_round(t) % 2)
                    for h in range(2):
                        dve.wait_ge(k2_h, 2 * t + h + 1)
                        dve.tensor_tensor(KL[:, t % 2, 4 * h:4 * h + 4, :], PS[:, at + h, :].rearrange("p (b c) -> p b c", c=P),
                                          bits(KH[:, t % 2, 4 * h:4 * h + 4, :]), ALU.subtract).then_inc(k2_l, 1)

                low_parts(0)
                steps = 0
                for t in range(NT):
                    dve.wait_ge(init_done, t + 1)
                    for j in range(4):
                        if j == 2 and t + 1 < NT:
                            low_parts(t + 1)
                        g, dh = j // 2, j % 2
                        acc = groups(X3[:, t, g * 4 * F:(g + 1) * 4 * F])
                        at = 4 * (product_round(t, j) % 2)
                        dve.wait_ge(y_ready, 4 * t + j + 1)
                        for d in range(DH):
                            e = W_EMB + t * D + dh * DH + d
                            if steps:
                                dve.wait_ge(acc_step, steps)
                            dve.scalar_tensor_tensor(acc, PS[:, at:at + 4, d * F:(d + 1) * F], WT[:, e:e + 1], acc,
                                                     ALU.mult, ALU.add).then_inc(acc_step, 1)
                            steps += 1
                    dve.wait_ge(acc_step, steps)
                    layer_norm(dve, lambda i: (X3[:, t, i * F:(i + 1) * F],) * 2, B, x3_done)

            @block.tensor
            def _(pe):
                rest = pe.value_load(has_rest[0:1, 0:1], min_val=0, max_val=1)
                pe.wait_ge(w_in, 48)
                for t in range(NT):
                    ins = pe.matmul(PS[:, 7, t * F:(t + 1) * F], EB[:, tile(t)], EB[:, N:N + F], start=True, stop=True)
                ins.then_inc(bo_ready, 1)
                pe.wait_ge(z_l, NT)
                for t in range(NT):
                    if t >= 2:
                        pe.wait_ge(a1_outD if t % 2 else a1_outA, t // 2)
                    adjacent(pe, rest, t, PS[:, t % 2, :], lambda m: ZH[:, m, :], lambda m: ZL[:, m, :]).then_inc(a1_ready, 1)
                pe.wait_ge(z_l, 2 * NT)
                for t in range(NT):
                    if t >= 2:
                        pe.wait_ge(a2_out, t - 1)
                    adjacent(pe, rest, t, PS[:, 2 + t % 2, :], lambda m: ZH[:, m, :], lambda m: ZL[:, m, :]).then_inc(a2_ready, 1)
                pe.wait_ge(a2_out, NT)
                pe.wait_ge(bo_out, 1)

                def banks_free(rnd):
                    if rnd < 2:
                        return
                    t, j = rounds[rnd - 2]
                    if j is None:
                        pe.wait_ge(k2_l, 2 * t + 2)
                        pe.wait_ge(g2_out, 2 * t + 2)
                    else:
                        pe.wait_ge(acc_step, DH * (4 * t + j + 1))

                def turn(t):
                    at = 4 * (turn_round(t) % 2)
                    banks_free(turn_round(t))
                    pe.wait_ge(xx_ready, 2 * t + 2)
                    for b in range(B):
                        ins = pe.transpose(PS[:, at + b // 4, tile(b % 4)], XX[:, b, :, :].rearrange("p k f -> p (k f)"), ident)
                    ins.then_inc(kT_ready, 1)
                    pe.wait_ge(gs_l, t + 1)
                    for b in range(B):
                        ins = pe.transpose(PS[:, at + 2 + b // 4, tile(b % 4)], GS[:, t % 2, b, :, :].rearrange("p k f -> p (k f)"), ident)
                    ins.then_inc(gT_ready, 1)

                def products(t, j):
                    g, dh = j // 2, j % 2
                    at = 4 * (product_round(t, j) % 2)
                    banks_free(product_round(t, j))
                    pe.wait_ge(k2_l, 2 * t + g + 1)
                    pe.wait_ge(g2_out, 2 * t + g + 1)
                    c = slice(dh * DH * F, (dh + 1) * DH * F)
                    r = t % 2
                    for i in range(4):
                        b, acc = 4 * g + i, PS[:, at + i, :]
                        pe.matmul(acc, KH[:, r, b, :], WH[:, 0, c], start=True, stop=False)
                        pe.matmul(acc, KH[:, r, b, :], WL[:, 0, c], start=False, stop=False)
                        pe.matmul(acc, KL[:, r, b, :], WH[:, 0, c], start=False, stop=False)
                        pe.matmul(acc, GK[:, r, b, :], WH[:, 1, c], start=False, stop=False)
                        ins = pe.matmul(acc, GK[:, r, b, :], WL[:, 1, c], start=False, stop=True)
                    ins.then_inc(y_ready, 1)

                pe.wait_ge(wl_ready, 2)
                for t, j in rounds:
                    if j is None:
                        turn(t)
                    else:
                        products(t, j)

        NH = rounded("NH", 5 * SLOT, [P, NT, BF])
        NL = rounded("NL", 6 * SLOT, [P, NT, BF])
        LT = feature_major(1)
        X4 = node_major(2)
        n_h, n_l, lt_ready, lt_outA, lt_outD, z_r, z1_h, z1_l, z2_out, x4_done, stored = (
            sem(s) for s in ("n_h", "n_l", "lt_ready", "lt_outA", "lt_outD", "z_r", "z1_h", "z1_l", "z2_out", "x4_done", "stored"))
        NB = 2 * BP

        with nc.Block() as block:
            @block.sync
            def _(sp):
                for b in range(B):
                    sp.wait_ge(x4_done, b + 1)
                    sp.dma_start(out[b].rearrange("(t p) f -> p t f", p=P), X4[:, :, b * F:(b + 1) * F]).then_inc(stored, 16)
                sp.wait_ge(stored, 16 * B)

            @block.tensor
            def _(pe):
                rest = pe.value_load(has_rest[0:1, 0:1], min_val=0, max_val=1)

                def spread_nodes(u):
                    layer, q = u // BP, u % BP
                    if layer:
                        pe.wait_ge(z1_l, q + 1)
                    for half in range(2):
                        c = slice(half * HALF, (half + 1) * HALF)
                        acc = PS[:, 2 * (u % 2) + half, :]
                        if u >= 2:
                            pe.wait_ge(lt_outD if half else lt_outA, u - 1)
                        for m in range(NT):
                            if u == 0:
                                pe.wait_ge(n_h, m + 1)
                            pe.matmul(acc, NH[:, m, tile(q)], ADJH[:, m, c], start=(m == 0), stop=False, skip_group_check=True)
                        with pe.If(rest > 0):
                            for m in range(NT):
                                pe.matmul(acc, NH[:, m, tile(q)], ADJL[:, m, c], start=False, stop=False, skip_group_check=True)
                        for m in range(NT):
                            if u == 0:
                                pe.wait_ge(n_l, m + 1)
                            ins = pe.matmul(acc, NL[:, m, tile(q)], ADJH[:, m, c], start=False, stop=(m == NT - 1), skip_group_check=True)
                        ins.then_inc(lt_ready, 1)

                def features(u):
                    layer, q = u // BP, u % BP
                    pe.wait_ge(lt_outA, u + 1)
                    pe.wait_ge(lt_outD, u + 1)
                    if 2 <= u < BP + 2:
                        pe.wait_ge(z1_l, u - 1)
                    elif u >= BP + 2:
                        pe.wait_ge(z2_out, u - 1 - BP)
                    for t in range(NT):
                        ins = pe.matmul(PS[:, 4 + 2 * (u % 2) + t // 4, (t % 4) * P:(t % 4 + 1) * P], LT[:, u % 4, tile(t)],
                                        wt(W_L3 + layer * P, P), start=True, stop=True)
                    ins.then_inc(z_r, 1)

                spread_nodes(0)
                for u in range(1, NB):
                    spread_nodes(u)
                    features(u - 1)
                features(NB - 1)

            def product(u):
                return PS[:, 4 + 2 * (u % 2):6 + 2 * (u % 2), :].rearrange("p a (t c) -> p (a t) c", c=P)

            @block.scalar
            def _(act):
                for t in range(NT):
                    act.activation(NH[:, t, :], X3[:, t, :], ACT.Copy).then_inc(n_h, 1)

                def lt_copy(u):
                    act.wait_ge(lt_ready, 2 * u + 1)
                    act.activation(LT[:, u % 4, 0:HALF], PS[:, 2 * (u % 2), :], ACT.Copy).then_inc(lt_outA, 1)

                lt_copy(0)
                for u in range(NB):
                    if u + 1 < NB:
                        lt_copy(u + 1)
                    if u < BP:
                        act.wait_ge(z_r, u + 1)
                        act.activation(NH[:, :, tile(u)], product(u), ACT.Relu).then_inc(z1_h, 1)

            @block.vector
            def _(dve):
                for t in range(NT):
                    dve.wait_ge(n_h, t + 1)
                    dve.tensor_tensor(NL[:, t, :], X3[:, t, :], bits(NH[:, t, :]), ALU.subtract).then_inc(n_l, 1)

                def lt_copy(u):
                    dve.wait_ge(lt_ready, 2 * u + 2)
                    dve.tensor_copy(LT[:, u % 4, HALF:N], PS[:, 2 * (u % 2) + 1, :]).then_inc(lt_outD, 1)

                lt_copy(0)
                for u in range(NB):
                    if u + 1 < NB:
                        lt_copy(u + 1)
                    if u < BP:
                        dve.wait_ge(z1_h, u + 1)
                        dve.scalar_tensor_tensor(NL[:, :, tile(u)], product(u), 0.0, bits(NH[:, :, tile(u)]),
                                                 ALU.max, ALU.subtract).then_inc(z1_l, 1)
                    else:
                        q = u - BP
                        dve.wait_ge(z_r, u + 1)
                        dve.scalar_tensor_tensor(X4[:, :, tile(q)], product(u), 0.0, X3[:, :, tile(q)],
                                                 ALU.max, ALU.add).then_inc(z2_out, 1)
                        dve.wait_ge(z2_out, q + 1)
                        for par in range(2):
                            b = 2 * q + par
                            layer_norm(dve, lambda i: (X4[:, i, b * F:(b + 1) * F],) * 2, NT, x4_done)


def kernel(**inputs):
    import numpy as np
    import concourse.bacc as bacc
    from concourse.bass_utils import run_bass_kernel_spmd

    a = {k: np.asarray(v) for k, v in inputs.items()}

    consts = np.zeros((P, CW), np.float32)
    consts[:, C_ID:C_ID + P] = np.eye(P)
    consts[:, C_ID2:C_ID2 + F] = np.concatenate([np.eye(F)] * 2)
    consts[:, C_ONE:C_ONE + P] = 1
    consts[0:64, C_UP:C_UP + P] = np.concatenate([np.triu(np.ones((E, E)))] * 2, 1)
    consts[0:NT, C_TRI:C_TRI + NT + 1] = np.triu(np.ones((NT, NT + 1)), 1)
    consts[:, C_STEP:C_STEP + QUADS] = SLOTS * np.arange(QUADS)
    consts[:, C_RANK:C_RANK + E + SLOTS] = 1 + np.arange(E + SLOTS)
    consts[:, C_M1] = -1

    weights = np.zeros((P, WW), np.float32)

    def diagonal(at, w):
        n = w.shape[1]
        weights[0:64, at:at + n] = w
        weights[64:128, at + n:at + 2 * n] = w

    def twice(at, w):
        weights[0:64, at:at + w.shape[1]] = w
        weights[64:128, at:at + w.shape[1]] = w

    diagonal(W_H, a["L0_gnn_W"])
    diagonal(W_IND, a["L0_gnn_W_ind"])
    diagonal(W_AN, np.repeat(a["L0_gnn_a_node"][:, None], E, 1))
    diagonal(W_GN, a["L0_gnn_a_gn"][:, None])
    weights[0:64, W_FC:W_FC + P] = a["L0_gnn_fcW"]
    weights[64:128, W_FC + P:W_FC + 2 * P] = a["L0_gnn_fcW"]
    weights[:, W_FCB] = a["L0_gnn_fcb"]
    weights[:, W_AV] = a["L0_gnn_av"]
    weights[:, W_GE:W_GE + F] = a["L0_gnn_a_ge"][None, :]
    for at, w in ((W_Q, a["L1_gnn_Wq"]), (W_K, a["L1_gnn_Wk"])):
        weights[0:64, at:at + P] = np.concatenate([w, w], 1)
        weights[64:128, at + P:at + 2 * P] = np.concatenate([w, w], 1)
    diagonal(W_V, a["L1_gnn_Wv"])
    twice(W_BQ, a["L1_gnn_bq"][:, None])
    twice(W_BK, a["L1_gnn_bk"][:, None])
    weights[:, W_EMB:W_EMB + NT * D] = a["L2_gnn_embedding"].reshape(NT, P, D).transpose(1, 0, 2).reshape(P, NT * D)
    l3 = a["L3_gnn_net_params"].reshape(2, F, F)
    diagonal(W_L3, l3[0])
    diagonal(W_L3 + P, l3[1])

    w = a["L2_gnn_weight"].transpose(1, 2, 0, 3).reshape(3, F, D * F)
    arrays = {
        "in_x_nat": np.ascontiguousarray(a["x"].transpose(1, 0, 2)),
        "in_x_tr": np.ascontiguousarray(a["x"].transpose(0, 2, 1)).reshape(B * F, N),
        "in_adj_tr": np.ascontiguousarray(a["adj"].T),
        "in_h_nat": np.ascontiguousarray(a["L0_gnn_H"]),
        "in_h_tr": np.ascontiguousarray(a["L0_gnn_H"].T),
        "in_consts": consts,
        "in_weights": weights,
        "in_w01": np.ascontiguousarray(w[0:2].reshape(2 * F, D * F)),
        "in_w2": np.ascontiguousarray(np.concatenate([w[2], w[2]])),
        "in_emb_bias": np.ascontiguousarray(np.concatenate([a["L2_gnn_embedding"].T, a["L2_gnn_bias"]], 1)),
    }
    nc = bacc.Bacc("TRN2", target_bir_lowering=False, num_devices=1)
    args = [nc.dram_tensor(n, v.shape, mybir.dt.from_np(v.dtype), kind="ExternalInput").ap() for n, v in arrays.items()]
    out = nc.dram_tensor("out_0", (B, N, F), F32, kind="ExternalOutput").ap()
    program(nc, *args, out)
    r = run_bass_kernel_spmd(nc, [arrays], core_ids=[0])
    return r.results[0]["out_0"]
```

```python
from contextlib import ExitStack

import concourse.bass as bass
from concourse import mybir

F32 = mybir.dt.float32
F32R = mybir.dt.float32r
BF16 = mybir.dt.bfloat16
I32 = mybir.dt.int32
ALU = mybir.AluOpType
ACT = mybir.ActivationFunctionType
AX = mybir.AxisListType

P = 128
B = 8
N = 1024
F = 64
E = 64
NT = N // P
BP = B // 2
BF = B * F
HALF = N // 2
D = 16
SLOTS = 4
QUADS = E // SLOTS
NEG = -1e9
BIG = 3e38
EPS = 1e-5

C_ID = 0
C_ID2 = C_ID + P
C_ONE = C_ID2 + F
C_UP = C_ONE + P
C_TRI = C_UP + P
C_STEP = C_TRI + NT + 1
C_RANK = C_STEP + QUADS
C_M1 = C_RANK + E + SLOTS
CW = C_M1 + 1

W_H = 0
W_IND = W_H + P
W_AN = W_IND + P
W_GN = W_AN + P
W_FC = W_GN + 2
W_FCB = W_FC + 2 * P
W_AV = W_FCB + 1
W_GE = W_AV + 1
W_Q = W_GE + F
W_K = W_Q + 2 * P
W_V = W_K + 2 * P
W_BQ = W_V + P
W_BK = W_BQ + 1
W_EMB = W_BK + 1
W_L3 = W_EMB + NT * D
WW = W_L3 + 2 * P


def program(nc, x_nat, x_tr, adj_tr, h_nat, h_tr, consts, weights, w01, w2, emb_bias, out):
    ctx = ExitStack()
    with ctx:
        def sb(name, shape, dt=F32):
            return ctx.enter_context(nc.sbuf_tensor(name, shape, dt))

        stage_sems = []

        def sem(name):
            stage_sems.append(nc.alloc_semaphore(name))
            return stage_sems[-1]

        def free_semaphores():
            nc.clear_and_free_semaphores(stage_sems)
            nc.all_engine_barrier()
            stage_sems.clear()

        PS = ctx.enter_context(nc.psum_tensor("PS", [P, 8, 512], F32))

        ADJH = sb("ADJH", [P, NT, N], F32R)
        ADJL = sb("ADJL", [P, NT, N], F32R)
        CN = sb("CN", [P, CW])
        WT = sb("WT", [P, WW])
        SLOT = NT * BF
        SLOTS_IN_ARENA = 7
        arena_at = -(-nc.sbuf_base // 32) * 32
        arena = sb("arena", [P, SLOTS_IN_ARENA * SLOT])

        def rounded(name, column, shape):
            n = 1
            for k in shape[1:]:
                n *= k
            assert column + n <= SLOTS_IN_ARENA * SLOT
            return nc.alloc_sbuf_tensor_at(name, shape, F32R, offset=arena_at + 4 * column)

        def node_major(slot):
            return arena[:, slot * SLOT:(slot + 1) * SLOT].rearrange("p (t c) -> p t c", t=NT)

        def feature_major(slot):
            return arena[:, slot * SLOT:(slot + 1) * SLOT].rearrange("p (q n) -> p q n", q=BP)

        ident = CN[:, C_ID:C_ID + P]
        ones = CN[:, C_ONE:C_ONE + P]

        def bits(ap):
            return ap.bitcast(F32)

        def wt(at, n, rows=P):
            return WT[0:rows, at:at + n]

        def tile(t):
            return slice(t * P, (t + 1) * P)

        def groups(ap):
            return ap.rearrange("p (b f) -> p b f", f=F)

        def spread(ap, n=F):
            return ap.unsqueeze(2).broadcast_to([ap.shape[0], ap.shape[1], n])

        LN_ST = sb("LN_ST", [P, 64, 6])
        LN_A = sb("LN_A", [P, 64])
        LN_B = sb("LN_B", [P, 64])
        LN_V = sb("LN_V", [P, 64])
        LN_M = sb("LN_M", [P, 64])
        LN_Y = sb("LN_Y", [P, 64])
        ln_step = ctx.enter_context(nc.semaphore("ln_step"))
        ln_count = [0]

        def link(dve, ins):
            ln_count[0] += 1
            ins.then_inc(ln_step, 1)
            dve.wait_ge(ln_step, ln_count[0])

        def norm_stats(dve, source, groups):
            for i in groups:
                ins = dve.bn_stats(LN_ST[:, i, :], source(i))
            link(dve, ins)

        def norm_scales(dve, n, at=0):
            g = slice(at, at + n)
            even, odd = LN_ST[:, g, 1], LN_ST[:, g, 4]
            a, b, v, m, y = (t[:, g] for t in (LN_A, LN_B, LN_V, LN_M, LN_Y))
            dve.tensor_tensor(m, even, odd, ALU.add)
            dve.tensor_tensor(v, LN_ST[:, g, 2], LN_ST[:, g, 5], ALU.add)
            link(dve, dve.tensor_tensor(a, even, odd, ALU.subtract))
            link(dve, dve.scalar_tensor_tensor(b, a, 16.0, a, ALU.mult, ALU.mult))
            dve.tensor_scalar(m, m, 0.5, None, ALU.mult)
            link(dve, dve.tensor_tensor(v, v, b, ALU.add))
            link(dve, dve.tensor_scalar(v, v, 1.0 / F, EPS, ALU.mult, ALU.add))
            link(dve, dve.tensor_scalar(a.bitcast(I32), v.bitcast(I32), 1, None, ALU.logical_shift_right))
            link(dve, dve.tensor_scalar(y.bitcast(I32), a.bitcast(I32), -1.0, float(0x5F3759DF), ALU.mult, ALU.add))
            for _ in range(3):
                link(dve, dve.scalar_tensor_tensor(a, v, -0.5, y, ALU.mult, ALU.mult))
                link(dve, dve.tensor_tensor(b, a, y, ALU.mult))
                link(dve, dve.scalar_tensor_tensor(y, b, 1.5, y, ALU.add, ALU.mult))
        def spread_feature(ap):
            return ap.unsqueeze(3).broadcast_to([ap.shape[0], ap.shape[1], ap.shape[2], F])

        def norm_apply(engine, x, n_at, tiles, graphs):
            def scale(t):
                return spread_feature(t[:, n_at:n_at + tiles * graphs].rearrange("p (t b) -> p t b", b=graphs))
            v = x.rearrange("p t (b f) -> p t b f", f=F)
            return (lambda: engine.tensor_tensor(v, v, scale(LN_M), ALU.subtract),
                    lambda: engine.tensor_tensor(v, v, scale(LN_Y), ALU.mult))

        def adjacent(pe, rest, t, acc, high, low, parts=None):
            for m in range(NT):
                if parts:
                    pe.wait_ge(parts[0], parts[2] + m + 1)
                pe.matmul(acc, ADJH[:, m, tile(t)], high(m), start=(m == 0), stop=False, skip_group_check=True)
            with pe.If(rest > 0):
                for m in range(NT):
                    pe.matmul(acc, ADJL[:, m, tile(t)], high(m), start=False, stop=False, skip_group_check=True)
            for m in range(NT):
                if parts:
                    pe.wait_ge(parts[1], parts[2] + m + 1)
                ins = pe.matmul(acc, ADJH[:, m, tile(t)], low(m), start=False, stop=(m == NT - 1), skip_group_check=True)
            return ins

        XN = node_major(5)
        XT = feature_major(0)
        HP = node_major(2)
        XWH = rounded("XWH", 5 * SLOT, [P, NT, BF])
        XWL = rounded("XWL", 6 * SLOT, [P, NT, BF])
        HT = feature_major(1)
        IND = node_major(3)
        RAW = arena[:, 3 * SLOT:4 * SLOT].rearrange("p (r n) -> p r n", n=N)
        EX = feature_major(0)
        ET = arena[:, SLOT:2 * SLOT].rearrange("p (t q c) -> p t q c", t=NT, q=BP)
        maskT = arena[:, 4 * SLOT:4 * SLOT + N]
        limT = arena[:, 4 * SLOT + N:4 * SLOT + 2 * N]
        effT = arena[:, 4 * SLOT + 2 * N:4 * SLOT + 3 * N]
        rankT = effT
        hN = arena[:, 4 * SLOT + 3 * N:4 * SLOT + 3 * N + NT * E].rearrange("p (t e) -> p t e", e=E)
        limN = arena[:, 4 * SLOT + 3 * N + NT * E:5 * SLOT].rearrange("p (t e) -> p t e", e=E)
        degH = sb("degH", [P, NT])
        none = sb("none", [P, NT])
        low = sb("low", [P, NT])
        degE = sb("degE", [P, NT])
        kmx = sb("kmx", [NT, 1])
        kst = sb("kst", [NT, QUADS])
        kq = sb("kq", [NT, 1])
        first_i = sb("first_i", [1, NT + 1], I32)
        nmx = sb("nmx", [P, BP])
        Zs = sb("Zs", [P, BP])
        rZ = sb("rZ", [P, BP])
        rdg = sb("rdg", [P, NT])
        HM = sb("HM", [P, NT, 17])
        edges_at, edge_cols = SLOT // 2, BP * F
        AG, AGM, AEX, HE = (arena[:, edges_at + i * edge_cols:edges_at + (i + 1) * edge_cols].rearrange("p (q f) -> p q f", f=F)
                            for i in range(4))
        HET = arena[:, edges_at + 4 * edge_cols:edges_at + 5 * edge_cols].rearrange("p (a c) -> p a c", c=P)
        THE = arena[:, edges_at + 5 * edge_cols:edges_at + 7 * edge_cols].rearrange("p (a c) -> p a c", c=P)
        ae = sb("ae", [P, BP])
        SM = sb("SM", [P, 17])
        AGBD = sb("AGBD", [P, B, F])
        DG = arena[:, 0:B * E].rearrange("p (b e) -> p b e", e=E)
        SEB = arena[:, B * E:2 * B * E].rearrange("p (b e) -> p b e", e=E)
        LGM = arena[:, 2 * B * E:4 * B * E].rearrange("p (a b e) -> p a b e", a=2, e=E)
        zero16 = sb("zero16", [P, 512], BF16)
        ONR = sb("ONR", [P, 2], F32R)
        rest_max = sb("rest_max", [P, NT + 1])
        has_rest = sb("has_rest", [1, 1], I32)

        consts_in, weights_in, xT_in, x_in, hT_in, hN_in, one_ready = (
            sem(s) for s in ("consts_in", "weights_in", "xT_in", "x_in", "hT_in", "hN_in", "one_ready"))
        adj_in = [sem(f"adj_in{i}") for i in range(4)]
        adjh_ready, adjl_ready, rest_seen, rest_ready, xwh_ready = (
            sem(s) for s in ("adjh_ready", "adjl_ready", "rest_seen", "rest_ready", "xwh_ready"))
        h_ready, h_out, xw_ready, xw_out = sem("h_ready"), sem("h_out"), sem("xw_ready"), sem("xw_out")
        hT_ready, hT_outA, hT_outD = sem("hT_ready"), sem("hT_outA"), sem("hT_outD")
        mask_ready, degB_ready, eff_ready, rank_ready = sem("mask_ready"), sem("degB_ready"), sem("eff_ready"), sem("rank_ready")
        rank_done = sem("rank_done")
        s_ready, s_copied, s_out, ex_max, ex_done = sem("s_ready"), sem("s_copied"), sem("s_out"), sem("ex_max"), sem("ex_done")
        hg_ready, hg_out = sem("hg_ready"), sem("hg_out")
        ind_ready, ind_scale, ind_out = sem("ind_ready"), sem("ind_scale"), sem("ind_out")
        et_ready, et_outA, et_outD = sem("et_ready"), sem("et_outA"), sem("et_outD")
        rz_ready, agg_ready, agg_out, aex_done, he_ready = (
            sem(s) for s in ("rz_ready", "agg_ready", "agg_out", "aex_done", "he_ready"))
        heT_ready, heT_out, fce_ready, the_done, se_ready, sm_ready, seB_ready, seB_out = (
            sem(s) for s in ("heT_ready", "heT_out", "fce_ready", "the_done", "se_ready", "sm_ready", "seB_ready", "seB_out"))
        zero_set, dstep, degT_ready, kq_ready, first_ready, sl = (
            sem(s) for s in ("zero_set", "dstep", "degT_ready", "kq_ready", "first_ready", "sl"))
        dn = [0]

        with nc.Block() as block:
            @block.sync
            def _(sp):
                for q in range(BP):
                    sp.dma_start(XT[:, q, :], x_tr[q * P:(q + 1) * P, :]).then_inc(xT_in, 16)
                for t in range(NT):
                    if t >= 4:
                        sp.wait_ge(adjl_ready, t - 3)
                    sp.dma_start(RAW[:, t % 4, :], adj_tr[t * P:(t + 1) * P, :]).then_inc(adj_in[t % 4], 16)

            @block.gpsimd
            def _(pool):
                pool.memset(SM[:, :], 0.0).then_inc(sl, 1)
                pool.memset(AGBD[:, :, :], 0.0).then_inc(zero_set, 1)
                pool.memset(HM[:, :, :], 0.0).then_inc(zero_set, 1)
                pool.memset(zero16[:, :], 0.0).then_inc(zero_set, 1)
                pool.wait_ge(sl, 1)
                pool.memset(SM[0:64, 16:17], 1.0).then_inc(zero_set, 1)
                for t in range(NT):
                    pool.wait_ge(adj_in[t % 4], 16 * (t // 4 + 1))
                    pool.wait_ge(adjh_ready, t + 1)
                    pool.tensor_tensor(ADJL[:, t, :], RAW[:, t % 4, :], bits(ADJH[:, t, :]), ALU.subtract).then_inc(adjl_ready, 1)

            @block.scalar
            def _(act):
                act.dma_start(CN[:, :], consts).then_inc(consts_in, 16)
                act.dma_start(WT[:, :], weights).then_inc(weights_in, 16)
                act.dma_start(maskT[0:64, :], h_tr).then_inc(hT_in, 16)
                act.dma_start(maskT[64:128, :], h_tr).then_inc(hT_in, 16)
                act.dma_start(hN, h_nat.rearrange("(t p) e -> p t e", p=P)).then_inc(hN_in, 16)

                def split_adj(t):
                    act.wait_ge(adj_in[t % 4], 16 * (t // 4 + 1))
                    act.activation(ADJH[:, t, :], RAW[:, t % 4, :], ACT.Copy).then_inc(adjh_ready, 1)

                for t in range(NT):
                    act.wait_ge(h_ready, t + 1)
                    act.activation(HP[:, t, :], PS[:, (2 * t) % 4, :], ACT.Copy, bias=1.0).then_inc(h_out, 1)
                    act.wait_ge(xw_ready, t + 1)
                    act.activation(XWH[:, t, :], PS[:, (2 * t + 1) % 4, :], ACT.Copy).then_inc(xwh_ready, 1)
                for q in range(BP):
                    act.wait_ge(hT_ready, 2 * q + 1)
                    act.activation(HT[:, q, 0:HALF], PS[:, 4 + (2 * q) % 4, :], ACT.Copy).then_inc(hT_outA, 1)
                    split_adj(q)
                for q in range(BP):
                    for half in range(2):
                        u = 2 * q + half
                        act.wait_ge(s_ready, u + 1)
                        act.activation(EX[:, q, half * HALF:(half + 1) * HALF], PS[:, 4 + u % 4, :],
                                       ACT.Copy).then_inc(s_copied, 1)
                    if q >= 1:
                        act.wait_ge(ex_max, q)
                        act.activation(EX[:, q - 1, :], EX[:, q - 1, :], ACT.Exp, bias=nmx[:, q - 1:q],
                                       accum_out=Zs[:, q - 1:q]).then_inc(ex_done, 1)
                    split_adj(4 + q)
                act.wait_ge(ex_max, BP)
                act.activation(EX[:, 3, :], EX[:, 3, :], ACT.Exp, bias=nmx[:, 3:4],
                               accum_out=Zs[:, 3:4]).then_inc(ex_done, 1)
                act.wait_ge(hg_ready, 1)
                act.wait_ge(zero_set, 2)
                act.activation(HM[:, :, 0:B], PS[:, 0, 0:NT * B].rearrange("p (t b) -> p t b", b=B),
                               ACT.Copy, scale=0.5).then_inc(hg_out, 1)

                def industry_out(t):
                    act.wait_ge(ind_scale, t + 1)
                    act.activation(IND[:, t, :], PS[:, 2 + t % 2, :], ACT.Copy,
                                   scale=rdg[:, t:t + 1]).then_inc(ind_out, 1)

                for q in range(BP):
                    act.wait_ge(et_ready, q + 1)
                    act.activation(ET[:, 0:4, q, :], PS[:, 4 + 2 * (q % 2), :].rearrange("p (t c) -> p t c", c=P),
                                   ACT.Copy).then_inc(et_outA, 1)
                act.wait_ge(agg_ready, 1)
                act.wait_ge(rz_ready, 1)
                for q in range(BP):
                    for par in range(2):
                        r = slice(64 * par, 64 * par + 64)
                        ins = act.activation(AG[r, q, :], PS[r, 4, q * P + 64 * par:q * P + 64 * par + 64],
                                             ACT.Copy, scale=rZ[r, q:q + 1])
                ins.then_inc(agg_out, 1)
                act.wait_ge(agg_out, 1)
                act.activation(AEX[:, :, :], AG[:, :, :], ACT.Exp, bias=CN[:, C_M1:C_M1 + 1]).then_inc(aex_done, 1)
                industry_out(0)
                industry_out(1)
                act.wait_ge(heT_ready, 1)
                act.activation(HET[:, :, :], PS[:, 5, 0:2 * P].rearrange("p (a c) -> p a c", c=P),
                               ACT.Copy).then_inc(heT_out, 1)
                industry_out(2)
                act.wait_ge(fce_ready, 1)
                for par in range(2):
                    act.activation(THE[:, par:BP:2, :], PS[:, 6 + par, 0:2 * P].rearrange("p (a c) -> p a c", c=P), ACT.Tanh,
                                   bias=wt(W_FCB, 1)).then_inc(the_done, 1)
                industry_out(3)
                act.wait_ge(seB_ready, 1)
                act.activation(SEB[:, :, :], PS[:, 5, :].rearrange("p (b e) -> p b e", e=E), ACT.Copy).then_inc(seB_out, 1)
                for t in range(4, NT):
                    industry_out(t)

            @block.vector
            def _(dve):
                def link(ins):
                    dn[0] += 1
                    ins.then_inc(dstep, 1)
                    dve.wait_ge(dstep, dn[0])

                def rest_seen_in(t):
                    dve.wait_ge(adjl_ready, t + 1)
                    dve.tensor_reduce(rest_max[:, t:t + 1], bits(ADJL[:, t, :]), AX.X, ALU.max,
                                      apply_absolute_value=True).then_inc(rest_seen, 1)

                dve.wait_ge(hT_in, 32)
                link(dve.tensor_scalar(maskT, maskT, 0.0, None, ALU.is_gt))
                dve.tensor_scalar(limT, maskT, BIG, NEG, ALU.mult, ALU.add).then_inc(mask_ready, 1)

                def xw_out_step(t):
                    dve.wait_ge(xwh_ready, t + 1)
                    dve.tensor_tensor(XWL[:, t, :], PS[:, (2 * t + 1) % 4, :], bits(XWH[:, t, :]), ALU.subtract).then_inc(xw_out, 1)

                for t in range(NT):
                    xw_out_step(t)
                for q in range(BP):
                    dve.wait_ge(hT_ready, 2 * q + 2)
                    dve.tensor_copy(HT[:, q, HALF:N], PS[:, 4 + (2 * q + 1) % 4, :]).then_inc(hT_outD, 1)
                dve.wait_ge(degB_ready, 1)
                for half in range(2):
                    s = slice(half * HALF, (half + 1) * HALF)
                    ins = dve.scalar_tensor_tensor(effT[:, s], PS[:, half, :], 0.0, maskT[:, s], ALU.is_equal, ALU.max)
                ins.then_inc(eff_ready, 1)
                for q in range(BP):
                    for half in range(2):
                        u = 2 * q + half
                        s = slice(half * HALF, (half + 1) * HALF)
                        dve.wait_ge(s_copied, u + 1)
                        ins = dve.scalar_tensor_tensor(EX[:, q, s], PS[:, 4 + u % 4, :], 0.2, EX[:, q, s],
                                                       ALU.mult, ALU.max).then_inc(s_out, 1)
                    dve.wait_ge(s_out, 2 * q + 2)
                    link(dve.tensor_tensor(EX[:, q, :], EX[:, q, :], limT, ALU.min))
                    dve.tensor_reduce(nmx[:, q:q + 1], EX[:, q, :], AX.X, ALU.max, negate=True).then_inc(ex_max, 1)
                    if q == 0:
                        dve.wait_ge(rank_ready, 1)
                        dve.wait_ge(eff_ready, 1)
                        for half in range(2):
                            s = slice(half * HALF, (half + 1) * HALF)
                            ins = dve.tensor_tensor(rankT[:, s], PS[:, 2 + half, :], effT[:, s], ALU.mult)
                        ins.then_inc(rank_done, 1)
                        for t in range(NT // 2):
                            rest_seen_in(t)

                dve.wait_ge(hN_in, 16)
                link(dve.tensor_scalar(hN, hN, 0.0, None, ALU.is_gt))
                dve.tensor_scalar(limN, hN, BIG, NEG, ALU.mult, ALU.add)
                link(dve.tensor_reduce(degH[:, :], hN, AX.X, ALU.add))
                link(dve.tensor_scalar(none[:, :], degH[:, :], 0.0, None, ALU.is_equal))
                dve.tensor_scalar(low[:, :], none[:, :], BIG, -BIG, ALU.mult, ALU.add)
                dve.scalar_tensor_tensor(degE[:, :], none[:, :], float(E), degH[:, :], ALU.mult, ALU.add).then_inc(degT_ready, 1)

                dve.wait_ge(consts_in, 16)
                dve.tensor_copy(ONR[:, :], CN[:, C_ONE:C_ONE + 2]).then_inc(one_ready, 1)
                for t in range(NT // 2, NT):
                    rest_seen_in(t)
                dve.wait_ge(rest_seen, NT)
                dve.tensor_reduce(rest_max[:, NT:NT + 1], rest_max[:, 0:NT], AX.X, ALU.max).then_inc(rest_ready, 1)
                dve.wait_ge(rest_ready, 2)
                dve.tensor_scalar(has_rest[:, :], PS[0:1, 1, 0:1], 0.0, None, ALU.is_gt).then_inc(rest_ready, 1)

                def industry_scale(t):
                    dve.wait_ge(ind_ready, t + 1)
                    link(dve.tensor_scalar(rdg[:, t:t + 1], PS[:, t % 2, 0:1], 1.0, None, ALU.max))
                    dve.reciprocal(rdg[:, t:t + 1], rdg[:, t:t + 1]).then_inc(ind_scale, 1)

                dve.wait_ge(ex_done, BP)
                dve.reciprocal(rZ[:, :], Zs[:, :]).then_inc(rz_ready, 1)
                for q in range(BP):
                    dve.wait_ge(et_ready, q + 1)
                    dve.tensor_copy(ET[:, 4:8, q, :], PS[:, 5 + 2 * (q % 2), :].rearrange("p (t c) -> p t c", c=P)).then_inc(et_outD, 1)
                dve.wait_ge(kq_ready, 1)
                link(dve.tensor_reduce(kmx[:, :], PS[0:NT, 5, 0:P], AX.X, ALU.max))
                link(dve.tensor_scalar(kst[:, :], CN[0:NT, C_STEP:C_STEP + QUADS], kmx[:, 0:1], None, ALU.is_lt))
                dve.tensor_reduce(kq[:, :], kst[:, :], AX.X, ALU.add).then_inc(kq_ready, 1)
                dve.wait_ge(agg_out, 1)
                link(dve.tensor_scalar(AGM[:, :, :], AG[:, :, :], -1.0, None, ALU.add))
                dve.wait_ge(aex_done, 1)
                link(dve.tensor_scalar(AEX[:, :, :], AEX[:, :, :], 1.0, -1.0, ALU.min, ALU.add))
                dve.tensor_tensor(HE[:, :, :], AEX[:, :, :], AGM[:, :, :], ALU.max).then_inc(he_ready, 1)
                link(dve.tensor_tensor(AGM[:, :, :], AGM[:, :, :],
                                       wt(W_GE, F).unsqueeze(1).broadcast_to([P, BP, F]), ALU.mult))
                link(dve.tensor_reduce(ae[:, :], AGM[:, :, :], AX.X, ALU.add))
                dve.wait_ge(zero_set, 4)
                for par in range(2):
                    r = slice(64 * par, 64 * par + 64)
                    dve.tensor_scalar(SM[r, par:B:2], ae[r, :], 0.5, None, ALU.mult)
                    dve.tensor_copy(AGBD[r, par:B:2, :], AG[r, :, :])
                industry_scale(0)
                industry_scale(1)
                dve.wait_ge(kq_ready, 3)
                dve.tensor_copy(first_i[:, :], PS[0:1, 4, 0:NT + 1]).then_inc(first_ready, 1)
                industry_scale(2)
                dve.wait_ge(se_ready, 1)
                for par in range(2):
                    r = slice(64 * par, 64 * par + 64)
                    ins = dve.tensor_copy(SM[r, B + par:2 * B:2], PS[r, 5, 0:BP])
                link(ins)
                dve.tensor_tensor(DG[:, :, :], CN[:, C_ID2:C_ID2 + E].unsqueeze(1).broadcast_to([P, B, E]),
                                  spread(SM[:, B:2 * B], E), ALU.mult).then_inc(sm_ready, 1)
                industry_scale(3)
                dve.wait_ge(seB_out, 1)
                for t in range(NT):
                    link(dve.tensor_tensor(LGM[:, t % 2, :, :], SEB[:, :, :],
                                           limN[:, t:t + 1, :].broadcast_to([P, B, E]), ALU.min))
                    dve.tensor_reduce(HM[:, t, B:2 * B], LGM[:, t % 2, :, :], AX.X, ALU.max, negate=True)
                    if t % 2 == 1:
                        industry_scale(4 + t // 2)

            @block.tensor
            def _(pe):
                pe.wait_ge(weights_in, 16)
                pe.wait_ge(xT_in, 16 * BP)
                for t in range(NT):
                    for which, at in ((0, W_H), (1, W_IND)):
                        if t >= 2:
                            pe.wait_ge(xw_out if which else h_out, t - 1)
                        for q in range(BP):
                            ins = pe.matmul(PS[:, (2 * t + which) % 4, tile(q)], XT[:, q, tile(t)], wt(at, P),
                                            start=True, stop=True)
                        ins.then_inc(xw_ready if which else h_ready, 1)
                for q in range(BP):
                    for half in range(2):
                        u = 2 * q + half
                        if u >= 4:
                            pe.wait_ge(hT_outD if half else hT_outA, (u - 4) // 2 + 1)
                        pe.matmul(PS[:, 4 + u % 4, :], wt(W_H, P), XT[:, q, half * HALF:(half + 1) * HALF],
                                  start=True, stop=True).then_inc(hT_ready, 1)
                pe.wait_ge(consts_in, 16)
                pe.wait_ge(mask_ready, 1)
                pe.wait_ge(h_out, NT)
                for half in range(2):
                    ins = pe.matmul(PS[:, half, :], CN[0:64, C_ONE:C_ONE + P], maskT[0:64, half * HALF:(half + 1) * HALF],
                                    start=True, stop=True)
                ins.then_inc(degB_ready, 1)
                pe.wait_ge(hT_outA, BP)
                pe.wait_ge(hT_outD, BP)

                def node_scores(q):
                    for half in range(2):
                        u = 2 * q + half
                        if u >= 4:
                            pe.wait_ge(s_out, u - 3)
                        pe.matmul(PS[:, 4 + u % 4, :], wt(W_AN, P), HT[:, q, half * HALF:(half + 1) * HALF],
                                  start=True, stop=True).then_inc(s_ready, 1)

                node_scores(0)
                node_scores(1)
                pe.wait_ge(eff_ready, 1)
                pe.wait_ge(xw_out, NT)
                for half in range(2):
                    ins = pe.matmul(PS[:, 2 + half, :], CN[0:64, C_UP:C_UP + P], effT[0:64, half * HALF:(half + 1) * HALF],
                                    start=True, stop=True)
                ins.then_inc(rank_ready, 1)
                for t in range(NT):
                    for q in range(BP):
                        ins = pe.matmul(PS[:, 0, t * B + 2 * q:t * B + 2 * q + 2], HT[:, q, tile(t)], wt(W_GN, 2),
                                        start=True, stop=True)
                ins.then_inc(hg_ready, 1)
                node_scores(2)
                node_scores(3)

                pe.wait_ge(rest_ready, 1)
                pe.matmul(PS[0:1, 1, 0:1], rest_max[:, NT:NT + 1], CN[:, C_ONE:C_ONE + 1], start=True, stop=True).then_inc(rest_ready, 1)
                pe.wait_ge(rest_ready, 3)
                rest = pe.value_load(has_rest[0:1, 0:1], min_val=0, max_val=1)

                def industry(t):
                    if t == 0:
                        pe.wait_ge(rank_done, 1)
                        pe.wait_ge(hg_out, 1)
                        pe.wait_ge(one_ready, 1)
                    if t >= 2:
                        pe.wait_ge(ind_out, t - 1)
                    deg = PS[:, t % 2, 0:2]
                    for m in range(NT):
                        pe.matmul(deg, ADJH[:, m, tile(t)], ONR[:, :], start=(m == 0), stop=False, skip_group_check=True)
                    with pe.If(rest > 0):
                        for m in range(NT):
                            pe.matmul(deg, ADJL[:, m, tile(t)], ONR[:, :], start=False, stop=False, skip_group_check=True)
                    adjacent(pe, rest, t, PS[:, 2 + t % 2, :], lambda m: XWH[:, m, :],
                             lambda m: XWL[:, m, :]).then_inc(ind_ready, 1)

                pe.wait_ge(s_out, 2 * BP)
                for q in range(BP):
                    pe.wait_ge(ex_done, q + 1)
                    if q >= 2:
                        pe.wait_ge(et_outA, q - 1)
                        pe.wait_ge(et_outD, q - 1)
                    for t in range(NT):
                        ins = pe.transpose(PS[:, 4 + 2 * (q % 2) + t // 4, (t % 4) * P:(t % 4 + 1) * P],
                                           EX[:, q, tile(t)], ident)
                    ins.then_inc(et_ready, 1)
                pe.wait_ge(et_outA, BP)
                pe.wait_ge(et_outD, BP)
                for q in range(BP):
                    for t in range(NT):
                        ins = pe.matmul(PS[:, 4, tile(q)], ET[:, t, q, :], HP[:, t, tile(q)],
                                        start=(t == 0), stop=(t == NT - 1))
                ins.then_inc(agg_ready, 1)
                pe.wait_ge(degT_ready, 1)
                pe.transpose(PS[0:NT, 5, 0:P], degE[:, :], ident).then_inc(kq_ready, 1)
                industry(0)
                pe.wait_ge(kq_ready, 2)
                pe.wait_ge(agg_out, 1)
                pe.matmul(PS[0:1, 4, 0:NT + 1], kq[:, :], CN[0:NT, C_TRI:C_TRI + NT + 1], start=True, stop=True).then_inc(kq_ready, 1)
                industry(1)
                pe.wait_ge(he_ready, 1)
                for a in range(2):
                    ins = pe.transpose(PS[:, 5, tile(a)], HE[:, 2 * a:2 * a + 2, :].rearrange("p a f -> p (a f)"), ident)
                ins.then_inc(heT_ready, 1)
                industry(2)
                pe.wait_ge(heT_out, 1)
                for q in range(BP):
                    ins = pe.matmul(PS[:, 6 + q % 2, tile(q // 2)], wt(W_FC + (q % 2) * P, P), HET[:, q // 2, :], start=True, stop=True)
                ins.then_inc(fce_ready, 1)
                pe.wait_ge(the_done, 2)
                for q in range(BP):
                    ins = pe.matmul(PS[:, 5, q:q + 1], THE[:, q, :], wt(W_AV, 1), start=True, stop=True)
                ins.then_inc(se_ready, 1)
                industry(3)
                pe.wait_ge(sm_ready, 1)
                pe.matmul(PS[:, 5, :], ones, DG[:, :, :].rearrange("p b e -> p (b e)"), start=True, stop=True).then_inc(seB_ready, 1)
                for t in range(4, NT):
                    industry(t)

        GN = node_major(1)
        SEL = rounded("SEL", 6 * SLOT, [P, SLOTS, P])
        AGH = rounded("AGH", 6 * SLOT + SLOTS * P, [P, BF])
        AGL = rounded("AGL", 6 * SLOT + SLOTS * P + BF, [P, BF])
        TS = sb("TS", [P, SLOTS, 17])
        LG = sb("LG", [P, SLOTS, B])
        TH = sb("TH", [P, SLOTS, B])
        XC = sb("XC", [P, SLOTS, B])
        BE = sb("BE", [P, SLOTS, B])
        CC = sb("CC", [P, SLOTS, B])
        ZQ = sb("ZQ", [P, B])
        ZN = sb("ZN", [P, 2, B])
        S0 = arena[:, 0:SLOTS * BF].rearrange("p (s c) -> p s c", c=BF)
        S1 = arena[:, SLOTS * BF:SLOT].rearrange("p (s c) -> p s c", c=BF)
        POOLED = 2
        PE_MIXED = 3
        sel_ready, small_ready, gath_ready, ts_ready, lg_ready, th_ready, xc_ready, be_ready, cc_ready = (
            sem(s) for s in ("sel_ready", "small_ready", "gath_ready", "ts_ready", "lg_ready", "th_ready",
                             "xc_ready", "be_ready", "cc_ready"))
        d_ready, m_ready, z_ready, e_ready, t_ready, wp_ready, wd_ready, zd_ready, acc_done, g_done, zq_step, z_init, agh_ready, agl_ready = (
            sem(s) for s in ("d_ready", "m_ready", "z_ready", "e_ready", "t_ready", "wp_ready", "wd_ready",
                             "zd_ready", "acc_done", "g_done", "zq_step", "z_init", "agh_ready", "agl_ready"))

        def first_turns(eng):
            return [eng.value_load(first_i[0:1, t:t + 1], min_val=0, max_val=NT * QUADS) for t in range(NT + 1)]

        with nc.Block() as block:
            @block.sync
            def _(sp):
                sp.dma_start(XN.rearrange("p t (b f) -> p t b f", f=F),
                             x_nat.rearrange("(t p) b f -> p t b f", p=P)).then_inc(x_in, 16)
                sp.wait_ge(x_in, 16)

            @block.tensor
            def _(pe):
                first = first_turns(pe)

                def small(j):
                    pe.wait_ge(sel_ready, SLOTS * j + SLOTS)
                    for s in range(SLOTS):
                        ins = pe.matmul(PS[:, 4, s * 17:(s + 1) * 17], bits(SEL[:, s, :]), SM[:, :], start=True, stop=True)
                    ins.then_inc(small_ready, 1)

                def gather(s):
                    pe.matmul(PS[:, s, :], SEL[:, s, :], AGH[:, :], start=True, stop=False, skip_group_check=True)
                    pe.matmul(PS[:, s, :], SEL[:, s, :], AGL[:, :], start=False, stop=True,
                              skip_group_check=True).then_inc(gath_ready, 1)

                pe.wait_ge(agl_ready, 1)
                small(0)
                for s in range(SLOTS):
                    gather(s)
                for t in range(NT):
                    acc = PS[:, 5 + t % 2, :]
                    if t >= 2:
                        pe.wait_ge(g_done, t - 1)
                    pe.matmul(acc, zero16[:, 0:P], zero16[:, :], start=True, stop=False, skip_group_check=True)
                    with pe.Fori(first[t], first[t + 1]) as j:
                        for s in range(PE_MIXED):
                            pe.wait_ge(m_ready, SLOTS * j + (s + 1))
                            pe.matmul(PS[:, s, :], ident, S0[:, s, :], start=False, stop=True,
                                      skip_group_check=True).then_inc(z_ready, 1)
                        pe.wait_ge(ts_ready, j + 1)
                        small(j + 1)
                        for s in range(SLOTS):
                            if s < POOLED:
                                pe.wait_ge(wp_ready, POOLED * j + (s + 1))
                            else:
                                pe.wait_ge(wd_ready, (SLOTS - POOLED) * j + (s - POOLED + 1))
                            pe.matmul(acc, ident, S0[:, s, :], start=False, stop=True,
                                      skip_group_check=True).then_inc(acc_done, 1)
                            gather(s)

            @block.vector
            def _(dve):
                first = first_turns(dve)

                def one_hot(k, rank):
                    for s in range(SLOTS):
                        dve.tensor_scalar(SEL[:, s, :], rank, CN[:, bass.ds(C_RANK + s + k, 1)],
                                          None, ALU.is_equal).then_inc(sel_ready, 1)

                def small(j, tile_at):
                    dve.wait_ge(small_ready, j + 1)
                    dve.tensor_tensor(TS[:, :, :], PS[:, 4, 0:SLOTS * 17].rearrange("p (s c) -> p s c", c=17),
                                      HM[:, bass.ds(tile_at, 1), :].broadcast_to([P, SLOTS, 17]), ALU.add).then_inc(ts_ready, 1)
                    dve.wait_ge(ts_ready, j + 1)
                    dve.tensor_scalar(LG[:, :, :], TS[:, :, B:2 * B], low[:, bass.ds(tile_at, 1)], 0.0, ALU.max,
                                      ALU.min).then_inc(lg_ready, 1)

                dve.wait_ge(agh_ready, 1)
                dve.tensor_tensor(AGL[:, :], AGBD[:, :, :].rearrange("p b f -> p (b f)"), bits(AGH[:, :]),
                                  ALU.subtract).then_inc(agl_ready, 1)
                one_hot(0, rankT[:, tile(0)])
                small(0, 0)
                for t in range(NT):
                    if t >= 2:
                        dve.wait_ge(g_done, t - 1)
                    dve.memset(ZN[:, t % 2, :], 0.0).then_inc(z_init, 1)
                    dve.wait_ge(z_init, t + 1)
                    with dve.Fori(first[t], first[t + 1]) as j:
                        k = nc.s_assert_within(SLOTS * (j - first[t]), 0, E - SLOTS, skip_runtime_bounds_check_because=
                                               "a tile takes at most E / SLOTS turns")
                        if t + 1 < NT:
                            more = nc.s_assert_within(j + 1 < first[t + 1], 0, 1, skip_runtime_bounds_check_because="a comparison")
                            k_next = nc.s_assert_within((k + SLOTS) * more, 0, E, skip_runtime_bounds_check_because=
                                                        "k is at most E - SLOTS")
                            t_next = nc.s_assert_within(t + 1 - more, t, t + 1, skip_runtime_bounds_check_because="more is 0 or 1")
                        else:
                            k_next, t_next = k + SLOTS, t

                        for s in range(SLOTS):
                            dve.wait_ge(gath_ready, SLOTS * j + (s + 1))
                            dve.tensor_tensor(S0[:, s, :], HP[:, t, :], PS[:, s, :], ALU.subtract).then_inc(d_ready, 1)
                        one_hot(k_next, rankT[:, bass.ds(t_next * P, P)])
                        def mixed(s):
                            dve.wait_ge(m_ready, SLOTS * j + (s + 1))
                            dve.tensor_tensor(S0[:, s, :], S0[:, s, :], PS[:, s, :], ALU.add).then_inc(zd_ready, 1)

                        def elu(s):
                            dve.wait_ge(e_ready, SLOTS * j + (s + 1))
                            z = PS if s < PE_MIXED else S0
                            dve.scalar_tensor_tensor(S0[:, s, :], S1[:, s, :], 1.0, z[:, s, :], ALU.min,
                                                     ALU.max).then_inc(t_ready, 1)

                        def weigh(s):
                            dve.wait_ge(t_ready, SLOTS * j + (s + 1))
                            dve.tensor_tensor(groups(S0[:, s, :]), groups(S0[:, s, :]), spread(CC[:, s, :]),
                                              ALU.mult).then_inc(wd_ready, 1)

                        elu(0)
                        dve.wait_ge(cc_ready, j + 1)
                        dve.tensor_reduce(ZQ[:, :], CC[:, :, :].rearrange("p s b -> p b s"), AX.X, ALU.add).then_inc(zq_step, 1)
                        elu(1)
                        dve.wait_ge(zq_step, 2 * j + 1)
                        dve.tensor_tensor(ZN[:, t % 2, :], ZN[:, t % 2, :], ZQ[:, :], ALU.add).then_inc(zq_step, 1)
                        mixed(3)
                        elu(2)
                        dve.wait_ge(th_ready, j + 1)
                        small(j + 1, t_next)
                        weigh(2)
                        elu(3)
                        weigh(3)
                    dve.wait_ge(zq_step, 2 * first[t + 1])
                    dve.reciprocal(ZN[:, t % 2, :], ZN[:, t % 2, :]).then_inc(rz_ready, 1)

            @block.scalar
            def _(act):
                first = first_turns(act)
                act.activation(AGH[:, :], AGBD[:, :, :].rearrange("p b f -> p (b f)"), ACT.Copy).then_inc(agh_ready, 1)

                def small(j):
                    act.wait_ge(ts_ready, j + 1)
                    act.activation(TH[:, :, :], TS[:, :, 0:B], ACT.Tanh).then_inc(th_ready, 1)
                    act.wait_ge(lg_ready, j + 1)
                    act.activation(XC[:, :, :], LG[:, :, :], ACT.Exp).then_inc(xc_ready, 1)
                    act.wait_ge(th_ready, j + 1)
                    act.activation(BE[:, :, :], TH[:, :, :], ACT.Copy, scale=0.5, bias=0.5).then_inc(be_ready, 1)

                small(0)
                for t in range(NT):
                    with act.Fori(first[t], first[t + 1]) as j:
                        for s in range(SLOTS):
                            if s < PE_MIXED:
                                act.wait_ge(z_ready, PE_MIXED * j + (s + 1))
                            else:
                                act.wait_ge(zd_ready, (SLOTS - PE_MIXED) * j + (s - PE_MIXED + 1))
                            act.activation(S1[:, s, :], (PS if s < PE_MIXED else S0)[:, s, :], ACT.Exp,
                                           bias=CN[:, C_M1:C_M1 + 1]).then_inc(e_ready, 1)
                        small(j + 1)
                    act.wait_ge(rz_ready, 2 + t)
                    act.wait_ge(acc_done, SLOTS * first[t + 1])
                    for b in range(B):
                        c = slice(b * F, (b + 1) * F)
                        ins = act.activation(GN[:, t, c], PS[:, 5 + t % 2, c], ACT.Copy, bias=-1.0, scale=ZN[:, t % 2, b:b + 1])
                    ins.then_inc(g_done, 1)

            @block.gpsimd
            def _(pool):
                first = first_turns(pool)
                for t in range(NT):
                    with pool.Fori(first[t], first[t + 1]) as j:
                        pool.wait_ge(be_ready, j + 1)
                        for s in range(SLOTS):
                            pool.wait_ge(d_ready, SLOTS * j + (s + 1))
                            if s == POOLED - 1:
                                pool.wait_ge(xc_ready, j + 1)
                                pool.tensor_tensor(CC[:, :, :], XC[:, :, :], TS[:, :, 16:17].broadcast_to([P, SLOTS, B]),
                                                   ALU.mult).then_inc(cc_ready, 1)
                            pool.tensor_tensor(groups(S0[:, s, :]), groups(S0[:, s, :]), spread(BE[:, s, :]),
                                               ALU.mult).then_inc(m_ready, 1)
                        pool.wait_ge(cc_ready, j + 1)
                        for s in range(POOLED):
                            pool.wait_ge(t_ready, SLOTS * j + (s + 1))
                            pool.tensor_tensor(groups(S0[:, s, :]), groups(S0[:, s, :]), spread(CC[:, s, :]),
                                               ALU.mult).then_inc(wp_ready, 1)

        FT = feature_major(0)
        X1 = node_major(3)
        TNH = feature_major(2)
        HRING = 3
        KP = sb("KP", [P, BP, NT, 2])
        th_diff, gT_r, iT_r, gT_o, iT_o, fc_ready, tn_done, av_done, kap_ready, gx_ready, kap_scaled, ig_scaled, ig_ready = (
            sem(s) for s in ("th_diff", "gT_r", "iT_r", "gT_o", "iT_o", "fc_ready", "tn_done", "av_done", "kap_ready",
                             "gx_ready", "kap_scaled", "ig_scaled", "ig_ready"))
        xr_ready, x1_scales, x1_centredP, x1_centredD, x1_doneP, x1_doneD = (
            sem(s) for s in ("xr_ready", "x1_scales", "x1_centredP", "x1_centredD", "x1_doneP", "x1_doneD"))

        def x1_norm(engine, q, half):
            c = slice(4 * half, 4 * half + 4)
            return norm_apply(engine, X1[:, c, tile(q)], 2 * NT * q + 8 * half, 4, 2)

        with nc.Block() as block:
            @block.vector
            def _(dve):
                def difference(b):
                    dve.wait_ge(tn_done, 4 * b + 4)
                    dve.tensor_tensor(TNH[:, (2 * b + 1) % 4, :], TNH[:, (2 * b + 1) % 4, :], TNH[:, 2 * b % 4, :],
                                      ALU.subtract).then_inc(th_diff, 1)

                difference(0)
                difference(1)
                for q in range(BP):
                    if q + 1 < BP:
                        difference(2 * q + 2)
                    x = X1[:, :, tile(q)]
                    dve.wait_ge(kap_ready, q + 1)
                    dve.tensor_scalar(KP[:, q, :, :], KP[:, q, :, :], 0.5, 0.5, ALU.mult, ALU.add).then_inc(kap_scaled, 1)
                    dve.wait_ge(kap_scaled, q + 1)
                    dve.wait_ge(ig_ready, q + 1)
                    v = x.rearrange("p t (b f) -> p t b f", f=F)
                    dve.tensor_tensor(v, v, spread_feature(KP[:, q, :, :]), ALU.mult).then_inc(ig_scaled, 1)
                    dve.wait_ge(ig_scaled, q + 1)
                    dve.wait_ge(gx_ready, q + 1)
                    dve.tensor_tensor(x, x, GN[:, :, tile(q)], ALU.add).then_inc(xr_ready, 1)
                    dve.wait_ge(xr_ready, q + 1)
                    first = 2 * NT * q
                    norm_stats(dve, lambda i: X1[:, (i - first) // 2, (2 * q + i % 2) * F:(2 * q + i % 2 + 1) * F],
                               range(first, first + 2 * NT))
                    if q + 1 < BP:
                        difference(2 * q + 3)
                    norm_scales(dve, 2 * NT, first)
                    dve.nop().then_inc(x1_scales, 1)
                    centre, scale = x1_norm(dve, q, 1)
                    centre().then_inc(x1_centredD, 1)
                    dve.wait_ge(x1_centredD, q + 1)
                    scale().then_inc(x1_doneD, 1)

            @block.gpsimd
            def _(pool):
                def apply_norm(q):
                    centre, scale = x1_norm(pool, q, 0)
                    pool.wait_ge(x1_scales, q + 1)
                    centre().then_inc(x1_centredP, 1)
                    pool.wait_ge(x1_centredP, q + 1)
                    scale().then_inc(x1_doneP, 1)

                for q in range(BP):
                    pool.wait_ge(iT_r, q + 1)
                    pool.tensor_tensor(X1[:, :, tile(q)], IND[:, :, tile(q)], GN[:, :, tile(q)], ALU.subtract).then_inc(ig_ready, 1)
                    pool.wait_ge(gT_r, q + 1)
                    pool.wait_ge(ig_ready, q + 1)
                    pool.tensor_tensor(GN[:, :, tile(q)], GN[:, :, tile(q)], XN[:, :, tile(q)], ALU.add).then_inc(gx_ready, 1)
                    if q >= 2:
                        apply_norm(q - 2)
                apply_norm(BP - 2)
                apply_norm(BP - 1)

            @block.scalar
            def _(act):
                def features_out(q):
                    for ready, dst, bank, done in ((gT_r, q % 2, 0, gT_o), (iT_r, 2 + q % 2, 2, iT_o)):
                        act.wait_ge(ready, q + 1)
                        if q >= 2:
                            act.wait_ge(fc_ready, 8 * (q - 1))
                        act.activation(FT[:, dst, :], PS[:, bank:bank + 2, :].rearrange("p a c -> p (a c)"), ACT.Copy).then_inc(done, 1)

                def kappa(q):
                    act.wait_ge(av_done, 2 * q + 2)
                    act.activation(KP[:, q, :, :], PS[:, 7, q * 2 * NT:(q + 1) * 2 * NT].rearrange("p (t b) -> p t b", b=2), ACT.Tanh,
                                   scale=0.5).then_inc(kap_ready, 1)

                features_out(0)
                for b in range(B):
                    if b >= 2:
                        act.wait_ge(av_done, b - 1)
                    for v in range(4 * b, 4 * b + 4):
                        act.wait_ge(fc_ready, v + 1)
                        half = v % 2
                        act.activation(TNH[:, (v // 2) % 4, half * HALF:(half + 1) * HALF], PS[:, 4 + v % HRING, :], ACT.Tanh,
                                       bias=wt(W_FCB, 1)).then_inc(tn_done, 1)
                    if b % 2 == 0 and b // 2 + 1 < BP:
                        features_out(b // 2 + 1)
                    if b % 2 == 0 and b >= 2:
                        kappa(b // 2 - 1)
                kappa(BP - 1)

            @block.tensor
            def _(pe):
                def turn(q):
                    if q >= 1:
                        pe.wait_ge(gT_o, q)
                    for t in range(NT):
                        ins = pe.transpose(PS[:, t // 4, (t % 4) * P:(t % 4 + 1) * P], GN[:, t, tile(q)], ident)
                    ins.then_inc(gT_r, 1)
                    if q >= 1:
                        pe.wait_ge(iT_o, q)
                    for t in range(NT):
                        ins = pe.transpose(PS[:, 2 + t // 4, (t % 4) * P:(t % 4 + 1) * P], IND[:, t, tile(q)], ident)
                    ins.then_inc(iT_r, 1)

                def hidden(b):
                    q = b // 2
                    for v in range(4 * b, 4 * b + 4):
                        w, half = (v // 2) % 2, v % 2
                        pe.wait_ge(iT_o if w else gT_o, q + 1)
                        if v >= HRING:
                            pe.wait_ge(tn_done, v - HRING + 1)
                        pe.matmul(PS[:, 4 + v % HRING, :], wt(W_FC + (b % 2) * P, P),
                                  FT[:, (2 if w else 0) + q % 2, half * HALF:(half + 1) * HALF],
                                  start=True, stop=True).then_inc(fc_ready, 1)

                def score(b):
                    pe.wait_ge(th_diff, b + 1)
                    for t in range(NT):
                        at = b // 2 * 2 * NT + 2 * t + b % 2
                        ins = pe.matmul(PS[:, 7, at:at + 1], TNH[:, (2 * b + 1) % 4, tile(t)], wt(W_AV, 1), start=True, stop=True)
                    ins.then_inc(av_done, 1)

                turn(0)
                for b in range(B):
                    hidden(b)
                    if b % 2 == 0 and b // 2 + 1 < BP:
                        turn(b // 2 + 1)
                    if b >= 1:
                        score(b - 1)
                score(B - 1)

        free_semaphores()

        X1T = feature_major(0)
        VH = rounded("VH", 5 * SLOT, [P, NT, BF])
        VL = rounded("VL", 6 * SLOT, [P, NT, BF])
        AV = node_major(1)
        EF = feature_major(2)
        RING = 3
        KS = [rounded(f"KS{i}", (4 + i) * SLOT, [P, N]) for i in range(2)]
        QH = [rounded(f"QH{i}", (4 + i) * SLOT + N, [P, N]) for i in range(2)]
        QL = [rounded(f"QL{i}", (4 + i) * SLOT + 2 * N, [P, N]) for i in range(2)]
        EHL = rounded("EHL", 6 * SLOT, [P, 4, N])
        EHM = [rounded(f"EHM{i}", (4 + i) * SLOT + 3 * N, [P, N]) for i in range(2)]
        EH = [EHL[:, 0, :], EHL[:, 1, :], EHM[0][:, :]]
        EL = [EHL[:, 2, :], EHL[:, 3, :], EHM[1][:, :]]
        NMX = sb("NMX", [P, B * NT])
        ZZ = sb("ZZ", [P, B * NT])
        RZ = sb("RZ", [P, B * NT])
        AVN = sb("AVN", [P, RING, 2 * F], F32R)
        SUMT = sb("SUMT", [P, NT, F])
        xT1_ready, xT1_outA, xT1_outD, v_ready, v_h, v_out, av1_ready, av1_outA, av1_outD = (
            sem(s) for s in ("xT1_ready", "xT1_outA", "xT1_outD", "v_ready", "v_h", "v_out", "av1_ready", "av1_outA", "av1_outD"))
        k_ready, k_h, k_out, q_ready, q_h, q_out, s1_ready, max_ready, p_ready, eh_ready, elP_ready, elD_ready = (
            sem(s) for s in ("k_ready", "k_h", "k_out", "q_ready", "q_h", "q_out", "s1_ready", "max_ready", "p_ready",
                             "eh_ready", "elP_ready", "elD_ready"))
        rz1_ready, avn_h, avn_ready, pv_done, o_copied, oT_ready, o_sum, o_out, norm_ready, centred, centredD, x2_done, x2_doneD = (
            sem(s) for s in ("rz1_ready", "avn_h", "avn_ready", "pv_done", "o_copied", "oT_ready", "o_sum", "o_out",
                             "norm_ready", "centred", "centredD", "x2_done", "x2_doneD"))
        TURNS = B * NT
        DVE_LOW = 2

        def low_ready(engine, i):
            b, m = i // NT, i % NT
            if m == DVE_LOW:
                engine.wait_ge(elD_ready, b + 1)
            else:
                engine.wait_ge(elP_ready, (NT - 1) * b + m + 1 - (m > DVE_LOW))

        LAG = RING

        with nc.Block() as block:
            @block.tensor
            def _(pe):
                rest = pe.value_load(has_rest[0:1, 0:1], min_val=0, max_val=1)
                for t in range(NT):
                    if t >= 4:
                        pe.wait_ge(xT1_outD if t % 2 else xT1_outA, (t - 4) // 2 + 1)
                    for q in range(BP):
                        ins = pe.transpose(PS[:, t % 4, tile(q)], X1[:, t, tile(q)], ident)
                    ins.then_inc(xT1_ready, 1)
                pe.wait_ge(xT1_outA, 4)
                pe.wait_ge(xT1_outD, 4)
                for t in range(NT):
                    if t >= 2:
                        pe.wait_ge(v_out, t - 1)
                    for q in range(BP):
                        ins = pe.matmul(PS[:, 4 + t % 2, tile(q)], X1T[:, q, tile(t)], wt(W_V, P), start=True, stop=True)
                    ins.then_inc(v_ready, 1)
                for t in range(NT):
                    if t >= 2:
                        pe.wait_ge(av1_outD if t % 2 else av1_outA, t // 2)
                    adjacent(pe, rest, t, PS[:, 6 + t % 2, :], lambda m: VH[:, m, :], lambda m: VL[:, m, :],
                             None if t else (v_h, v_out, 0)).then_inc(av1_ready, 1)

                def project(b, at, ready, freed, n):
                    if n:
                        pe.wait_ge(freed, n)
                    for half in range(2):
                        ins = pe.matmul(PS[:, 4 + half, :], wt(at + (b % 2) * P, P), X1T[:, b // 2, half * HALF:(half + 1) * HALF],
                                        start=True, stop=True)
                    ins.then_inc(ready, 1)

                def scores(i):
                    b, m = i // NT, i % NT
                    if m == 0:
                        pe.wait_ge(k_out, b + 1)
                        pe.wait_ge(q_out, b + 1)
                    if i >= 2:
                        pe.wait_ge(p_ready, i - 1)
                    for half in range(2):
                        c = slice(half * HALF, (half + 1) * HALF)
                        acc = PS[:, 2 * (i % 2) + half, :]
                        pe.matmul(acc, KS[b % 2][:, tile(m)], QH[b % 2][:, c], start=True, stop=False)
                        ins = pe.matmul(acc, KS[b % 2][:, tile(m)], QL[b % 2][:, c], start=False, stop=True)
                    ins.then_inc(s1_ready, 1)

                def values(i):
                    b, m = i // NT, i % NT
                    pe.wait_ge(avn_ready, i + 1)
                    pe.wait_ge(eh_ready, i + 1)
                    low_ready(pe, i)
                    if m == 0 and b >= 1:
                        pe.wait_ge(o_copied, b)
                    for half in range(2):
                        c = slice(half * HALF, (half + 1) * HALF)
                        acc = PS[:, 6 + half, :]
                        pe.matmul(acc, AVN[:, i % RING, :], EH[i % RING][:, c], start=(m == 0), stop=False)
                        ins = pe.matmul(acc, AVN[:, i % RING, :], EL[i % RING][:, c], start=False, stop=(m == NT - 1))
                    ins.then_inc(pv_done, 1)

                def turn_back(b):
                    pe.wait_ge(o_copied, b + 1)
                    pe.wait_ge(q_out, min(b + 3, B))
                    for t in range(NT):
                        ins = pe.transpose(PS[:, 4 + t // 4, (t % 4) * P:(t % 4 + 1) * P], EF[:, RING, tile(t)], ident)
                    ins.then_inc(oT_ready, 1)

                pe.wait_ge(av1_outA, 4)
                pe.wait_ge(av1_outD, 4)
                project(0, W_K, k_ready, k_out, 0)
                project(0, W_Q, q_ready, k_out, 1)
                for i in range(TURNS + LAG):
                    b, m = i // NT, i % NT
                    if i < TURNS:
                        scores(i)
                    if m == 0 and b + 1 < B:
                        if b >= 2:
                            pe.wait_ge(o_sum, b - 1)
                        project(b + 1, W_K, k_ready, q_out, b + 1)
                    if m == 3 and b + 1 < B:
                        project(b + 1, W_Q, q_ready, k_out, b + 2)
                    if i >= LAG:
                        values(i - LAG)
                    if m == 5 and 1 <= b < B:
                        turn_back(b - 1)
                turn_back(B - 1)

            @block.scalar
            def _(act):
                for t in range(0, NT, 2):
                    act.wait_ge(xT1_ready, t + 1)
                    act.activation(X1T[:, :, tile(t)], PS[:, t % 4, :].rearrange("p (q c) -> p q c", c=P), ACT.Copy).then_inc(xT1_outA, 1)
                for t in range(NT):
                    act.wait_ge(v_ready, t + 1)
                    act.activation(VH[:, t, :], PS[:, 4 + t % 2, :], ACT.Copy).then_inc(v_h, 1)
                for t in range(0, NT, 2):
                    act.wait_ge(av1_ready, t + 1)
                    act.activation(AV[:, t, :], PS[:, 6, :], ACT.Copy).then_inc(av1_outA, 1)

                def high(b, ready, dst, at, done):
                    act.wait_ge(ready, b + 1)
                    if b >= 2:
                        act.wait_ge(s1_ready, NT * (b - 1))
                    act.activation(dst[b % 2][:, :], PS[:, 4:6, :].rearrange("p a c -> p (a c)"), ACT.Identity,
                                   bias=wt(at, 1)).then_inc(done, 1)

                def sums_out(act, b):
                    act.wait_ge(pv_done, NT * (b + 1))
                    if b >= 1:
                        act.wait_ge(oT_ready, b)
                    act.activation(EF[:, RING, :], PS[:, 6:8, :].rearrange("p a c -> p (a c)"), ACT.Copy).then_inc(o_copied, 1)

                act.wait_ge(av1_ready, NT)
                high(0, k_ready, KS, W_BK, k_h)
                high(0, q_ready, QH, W_BQ, q_h)
                for i in range(TURNS):
                    b, m = i // NT, i % NT
                    act.wait_ge(max_ready, i + 1)
                    if i >= RING:
                        low_ready(act, i - RING)
                    bank = 2 * (i % 2)
                    act.activation(EF[:, i % RING, :], PS[:, bank:bank + 2, :].rearrange("p a c -> p (a c)"), ACT.Exp,
                                   bias=NMX[:, i:i + 1], accum_out=ZZ[:, i:i + 1]).then_inc(p_ready, 1)
                    if i >= RING:
                        act.wait_ge(pv_done, i - RING + 1)
                    act.wait_ge(p_ready, i + 1)
                    act.activation(EH[i % RING], EF[:, i % RING, :], ACT.Copy).then_inc(eh_ready, 1)
                    if m == 0 and b + 1 < B:
                        high(b + 1, k_ready, KS, W_BK, k_h)
                    if m == 2 and b >= 1:
                        sums_out(act, b - 1)
                    if m == 3 and b + 1 < B:
                        high(b + 1, q_ready, QH, W_BQ, q_h)
                sums_out(act, B - 1)

            @block.gpsimd
            def _(pool):
                def apply_norm(q, k):
                    half, x = k % 2, X1[:, (k % 2) * 4:(k % 2) * 4 + 4, tile(q)]
                    centre, scale = norm_apply(pool, x, 2 * NT * q + 8 * half, 4, 2)
                    if k < 2:
                        pool.wait_ge(norm_ready, q + 1)
                        centre().then_inc(centred, 1)
                    else:
                        pool.wait_ge(centred, 2 * q + 1 + (half if q < BP - 1 else 0))
                        scale().then_inc(x2_done, 1)

                steps_done = 0
                for i in range(TURNS):
                    if i % NT != DVE_LOW:
                        pool.wait_ge(eh_ready, i + 1)
                        if i >= RING:
                            pool.wait_ge(pv_done, i - RING + 1)
                        pool.tensor_tensor(EL[i % RING], EF[:, i % RING, :], bits(EH[i % RING]), ALU.subtract).then_inc(elP_ready, 1)
                    n = i - 3 * NT - 4
                    if n >= 0 and n % 4 == 1:
                        steps_done += 1
                        apply_norm(n // (2 * NT), n // 4 % 4)
                for k in range(steps_done, 4 * BP):
                    if k // 4 < BP - 1 or k % 2 == 0:
                        apply_norm(k // 4, k % 4)

            @block.vector
            def _(dve):
                for t in range(1, NT, 2):
                    dve.wait_ge(xT1_ready, t + 1)
                    dve.tensor_copy(X1T[:, :, tile(t)], PS[:, t % 4, :].rearrange("p (q c) -> p q c", c=P)).then_inc(xT1_outD, 1)
                for t in range(NT):
                    dve.wait_ge(v_h, t + 1)
                    dve.tensor_tensor(VL[:, t, :], PS[:, 4 + t % 2, :], bits(VH[:, t, :]), ALU.subtract).then_inc(v_out, 1)
                for t in range(1, NT, 2):
                    dve.wait_ge(av1_ready, t + 1)
                    dve.tensor_copy(AV[:, t, :], PS[:, 7, :]).then_inc(av1_outD, 1)
                dve.wait_ge(av1_outA, 4)
                dve.wait_ge(av1_outD, 4)

                def low(b, w):
                    if w == 0:
                        dve.wait_ge(k_h, b + 1)
                        r, dst, src, at, done = slice(64, 128), KS[b % 2], KS[b % 2], W_BK, k_out
                    else:
                        dve.wait_ge(q_h, b + 1)
                        r, dst, src, at, done = slice(0, 128), QL[b % 2], QH[b % 2], W_BQ, q_out
                    dve.scalar_tensor_tensor(dst[r, :], PS[r, 4:6, :].rearrange("p a c -> p (a c)"), WT[r, at:at + 1],
                                             bits(src[r, :]), ALU.add, ALU.subtract).then_inc(done, 1)

                def scaled_values(i):
                    b, m = i // NT, i % NT
                    dve.wait_ge(p_ready, i + 1)
                    dve.reciprocal(RZ[:, i:i + 1], ZZ[:, i:i + 1]).then_inc(rz1_ready, 1)
                    dve.wait_ge(rz1_ready, i + 1)
                    if i >= RING:
                        dve.wait_ge(pv_done, i - RING + 1)
                    av = AV[:, m, b * F:(b + 1) * F]
                    dve.tensor_scalar(AVN[:, i % RING, 0:F], av, RZ[:, i:i + 1], None, ALU.mult).then_inc(avn_h, 1)
                    dve.wait_ge(avn_h, i + 1)
                    dve.scalar_tensor_tensor(AVN[:, i % RING, F:2 * F], av, RZ[:, i:i + 1], bits(AVN[:, i % RING, 0:F]),
                                             ALU.mult, ALU.subtract).then_inc(avn_ready, 1)
                    if m == DVE_LOW:
                        dve.wait_ge(eh_ready, i + 1)
                        dve.tensor_tensor(EL[i % RING], EF[:, i % RING, :], bits(EH[i % RING]), ALU.subtract).then_inc(elD_ready, 1)

                def residual(b):
                    dve.wait_ge(oT_ready, b + 1)
                    dve.tensor_reduce(SUMT[:, :, :], PS[:, 4:6, :].rearrange("p a (t k f) -> p (a t) f k", k=2, f=F), AX.X,
                                      ALU.add).then_inc(o_sum, 1)

                def statistics(b):
                    x2b = X1[:, :, b * F:(b + 1) * F]
                    dve.wait_ge(o_sum, b + 1)
                    dve.scalar_tensor_tensor(x2b, SUMT[:, :, :], 0.0, x2b, ALU.max, ALU.add).then_inc(o_out, 1)
                    dve.wait_ge(o_out, b + 1)
                    norm_stats(dve, lambda i: X1[:, i // 2 % NT, b * F:(b + 1) * F], range(NT * (b - b % 2) + b % 2, NT * (b - b % 2) + 2 * NT, 2))

                def norm_pair(q):
                    norm_scales(dve, 2 * NT, 2 * NT * q)
                    dve.nop().then_inc(norm_ready, 1)

                low(0, 0)
                low(0, 1)
                for i in range(TURNS + 1):
                    if i < TURNS:
                        dve.wait_ge(s1_ready, i + 1)
                        bank = 2 * (i % 2)
                        dve.tensor_reduce(NMX[:, i:i + 1], PS[:, bank:bank + 2, :], AX.XY, ALU.max, negate=True).then_inc(max_ready, 1)
                    if i >= 1:
                        scaled_values(i - 1)
                    b, m = i // NT, i % NT
                    if m == 1 and b + 1 < B:
                        low(b + 1, 0)
                    if m == 4 and b + 1 < B:
                        low(b + 1, 1)
                    if m == 6 and 1 <= b < B:
                        residual(b - 1)
                    if m == 7 and 1 <= b < B:
                        statistics(b - 1)
                    if m == 3 and b % 2 == 1 and 3 <= b < B:
                        norm_pair(b // 2 - 1)
                residual(B - 1)
                statistics(B - 1)
                norm_pair(BP - 1)
                centre, scale = norm_apply(dve, X1[:, 4:8, tile(BP - 1)], 2 * NT * (BP - 1) + 8, 4, 2)
                centre().then_inc(centredD, 1)
                dve.wait_ge(centredD, 1)
                scale().then_inc(x2_doneD, 1)

        X2 = node_major(3)
        XA = node_major(4)
        XX = sb("XX", [P, B, 2, F])
        ZH = rounded("ZH", 5 * SLOT, [P, NT, BF])
        ZL = rounded("ZL", 6 * SLOT, [P, NT, BF])
        XG = node_major(1)
        X3 = node_major(0)
        W01F = arena[:, 0:D * F]
        W2F = arena[:, D * F:2 * D * F]
        EB = arena[0:D, 2 * D * F:2 * D * F + N + F]
        WH = rounded("WH", 2 * SLOT, [P, 2, D * F])
        WL = rounded("WL", 2 * SLOT + 2 * D * F, [P, 2, D * F])
        KH = rounded("KH", 5 * SLOT, [P, 2, B, P])
        KL = rounded("KL", 5 * SLOT + 2 * B * P, [P, 2, B, P])
        GK = rounded("GK", 6 * SLOT, [P, 2, B, P])
        GS = arena[:, 6 * SLOT + 2 * B * P:7 * SLOT].rearrange("p (r b k f) -> p r b k f", r=2, k=2, f=F)
        BO = SUMT[:, :, :]
        w_in, wh_ready, wl_ready, bo_ready, bo_out, init_done = (
            sem(s) for s in ("w_in", "wh_ready", "wl_ready", "bo_ready", "bo_out", "init_done"))
        z_h, z_l, a1_ready, a1_outA, a1_outD, a2_ready, a2_out = (
            sem(s) for s in ("z_h", "z_l", "a1_ready", "a1_outA", "a1_outD", "a2_ready", "a2_out"))
        kT_ready, k2_h, k2_l, gs_h, gs_l, gT_ready, g2_out, y_ready, acc_step, x3_done = (
            sem(s) for s in ("kT_ready", "k2_h", "k2_l", "gs_h", "gs_l", "gT_ready", "g2_out", "y_ready", "acc_step", "x3_done"))
        n_h, n_l, xx_ready, sy_ready, sy_added, x3_sum, x3_scales, x3_centred = (
            sem(s) for s in ("n_h", "n_l", "xx_ready", "sy_ready", "sy_added", "x3_sum", "x3_scales", "x3_centred"))
        NH = rounded("NH", 4 * SLOT, [P, NT, BF])
        NL = rounded("NL", 3 * SLOT, [P, NT, BF])
        DH = 8
        DS = 2
        YD = [AGBD[:, :, :].rearrange("p b f -> p (b f)"), sb("YD", [P, BF])[:, :]]
        SY = sb("SY", [P, 4, 4 * F])

        rounds = [(0, None)]
        for t in range(NT):
            rounds += [(t, 0), (t, 1)] + ([(t + 1, None)] if t + 1 < NT else []) + [(t, 2), (t, 3)]

        def turn_round(t):
            return rounds.index((t, None))

        def product_round(t, j):
            return rounds.index((t, j))

        with nc.Block() as block:
            @block.sync
            def _(sp):
                sp.dma_start(W01F, w01).then_inc(w_in, 16)
                sp.dma_start(W2F, w2).then_inc(w_in, 16)
                sp.dma_start(EB, emb_bias).then_inc(w_in, 16)

            @block.gpsimd
            def _(pool):
                pool.wait_ge(w_in, 48)
                for k, w in ((0, W01F), (1, W2F)):
                    pool.tensor_copy(WH[:, k, :], w).then_inc(wh_ready, 1)
                pool.wait_ge(wh_ready, 2)
                for k, w in ((0, W01F), (1, W2F)):
                    pool.tensor_tensor(WL[:, k, :], w, bits(WH[:, k, :]), ALU.subtract).then_inc(wl_ready, 1)
                pool.wait_ge(bo_out, 1)
                pool.wait_ge(wl_ready, 2)
                for t in range(NT):
                    pool.tensor_tensor(groups(X3[:, t, :]), groups(X2[:, t, :]),
                                       BO[:, t:t + 1, :].broadcast_to([P, B, F]), ALU.add).then_inc(init_done, 1)

                def low_parts(t):
                    pool.wait_ge(gs_h, t + 1)
                    pool.tensor_tensor(GS[:, t % 2, :, 1, :], groups(XG[:, t, :]), GS[:, t % 2, :, 0, :], ALU.subtract).then_inc(gs_l, 1)

                def apply_norm(t):
                    centre, scale = norm_apply(pool, X3[:, t:t + 1, :], B * t, 1, B)
                    pool.wait_ge(x3_scales, t + 1)
                    centre().then_inc(x3_centred, 1)
                    pool.wait_ge(x3_centred, t + 1)
                    scale().then_inc(x3_done, 1)

                low_parts(0)
                pool.wait_ge(init_done, NT)
                for t in range(NT):
                    if t + 1 < NT:
                        low_parts(t + 1)
                    for j in range(4):
                        x = X3[:, t, (j // 2) * 4 * F:(j // 2 + 1) * 4 * F]
                        for d in range(DS):
                            n = DS * (4 * t + j) + d
                            pool.wait_ge(sy_ready, n + 1)
                            if n:
                                pool.wait_ge(sy_added, n)
                            pool.tensor_tensor(x, x, SY[:, n % 4, :], ALU.add).then_inc(sy_added, 1)
                    if t >= 1:
                        apply_norm(t - 1)
                apply_norm(NT - 1)

            @block.scalar
            def _(act):
                for t in range(NT):
                    act.activation(ZH[:, t, :], X2[:, t, :], ACT.Copy).then_inc(z_h, 1)
                act.wait_ge(bo_ready, 1)
                act.activation(BO[:, :, :], PS[:, 7, :].rearrange("p (t f) -> p t f", f=F), ACT.Copy).then_inc(bo_out, 1)
                for t in range(0, NT, 2):
                    act.wait_ge(a1_ready, t + 1)
                    act.activation(XA[:, t, :], PS[:, t % 2, :], ACT.Copy).then_inc(a1_outA, 1)
                act.wait_ge(a1_ready, NT)
                act.wait_ge(a1_outA, 4)
                act.wait_ge(a1_outD, 4)
                for t in range(NT):
                    act.activation(ZH[:, t, :], XA[:, t, :], ACT.Copy).then_inc(z_h, 1)
                act.wait_ge(a2_ready, NT)

                def inputs(t):
                    if t >= 1:
                        act.wait_ge(kT_ready, t)
                    act.activation(XX[:, :, 0, :], groups(X2[:, t, :]), ACT.Copy).then_inc(xx_ready, 1)
                    act.activation(XX[:, :, 1, :], groups(XA[:, t, :]), ACT.Copy).then_inc(xx_ready, 1)
                    if t >= 2:
                        act.wait_ge(gT_ready, t - 1)
                    act.wait_ge(a2_out, t + 1)
                    act.activation(GS[:, t % 2, :, 0, :].bitcast(F32R), groups(XG[:, t, :]), ACT.Copy).then_inc(gs_h, 1)

                def turned(t):
                    at = 4 * (turn_round(t) % 2)
                    for h in range(2):
                        act.wait_ge(kT_ready, t + 1)
                        if t >= 2:
                            act.wait_ge(y_ready, 4 * (t - 1))
                        act.activation(KH[:, t % 2, 4 * h:4 * h + 4, :], PS[:, at + h, :].rearrange("p (b c) -> p b c", c=P),
                                       ACT.Copy).then_inc(k2_h, 1)
                    for h in range(2):
                        act.wait_ge(gT_ready, t + 1)
                        act.activation(GK[:, t % 2, 4 * h:4 * h + 4, :], PS[:, at + 2 + h, :].rearrange("p (b c) -> p b c", c=P),
                                       ACT.Copy).then_inc(g2_out, 1)
                    if t + 1 < NT:
                        inputs(t + 1)

                def scaled(t, j):
                    at = 4 * (product_round(t, j) % 2)
                    act.wait_ge(acc_step, (DH - DS) * (4 * t + j + 1))
                    for d in range(DH - DS, DH):
                        n = DS * (4 * t + j) + d - (DH - DS)
                        if n >= 4:
                            act.wait_ge(sy_added, n - 3)
                        e = W_EMB + t * D + (j % 2) * DH + d
                        act.activation(groups(SY[:, n % 4, :]), PS[:, at:at + 4, d * F:(d + 1) * F], ACT.Copy,
                                       scale=WT[:, e:e + 1]).then_inc(sy_ready, 1)

                def next_high(t):
                    act.wait_ge(x3_done, t + 1)
                    act.activation(NH[:, t, :], X3[:, t, :], ACT.Copy).then_inc(n_h, 1)

                inputs(0)
                for t, j in rounds:
                    if j is None:
                        turned(t)
                    else:
                        scaled(t, j)
                        if j == 3 and t >= 2:
                            next_high(t - 2)
                next_high(NT - 2)
                next_high(NT - 1)

            @block.vector
            def _(dve):
                for t in range(NT):
                    dve.wait_ge(z_h, t + 1)
                    dve.tensor_tensor(ZL[:, t, :], X2[:, t, :], bits(ZH[:, t, :]), ALU.subtract).then_inc(z_l, 1)
                for t in range(1, NT, 2):
                    dve.wait_ge(a1_ready, t + 1)
                    dve.tensor_copy(XA[:, t, :], PS[:, t % 2, :]).then_inc(a1_outD, 1)
                dve.wait_ge(a1_outA, 4)
                for t in range(NT):
                    dve.wait_ge(z_h, NT + t + 1)
                    dve.tensor_tensor(ZL[:, t, :], XA[:, t, :], bits(ZH[:, t, :]), ALU.subtract).then_inc(z_l, 1)
                for t in range(NT):
                    dve.wait_ge(a2_ready, t + 1)
                    dve.scalar_tensor_tensor(XG[:, t, :], PS[:, 2 + t % 2, :], 2.0, X2[:, t, :],
                                             ALU.mult, ALU.subtract).then_inc(a2_out, 1)

                def low_parts(t):
                    at = 4 * (turn_round(t) % 2)
                    for h in range(2):
                        dve.wait_ge(k2_h, 2 * t + h + 1)
                        dve.tensor_tensor(KL[:, t % 2, 4 * h:4 * h + 4, :], PS[:, at + h, :].rearrange("p (b c) -> p b c", c=P),
                                          bits(KH[:, t % 2, 4 * h:4 * h + 4, :]), ALU.subtract).then_inc(k2_l, 1)

                def statistics(t):
                    dve.wait_ge(acc_step, (DH - DS) * 4 * (t + 1))
                    dve.wait_ge(sy_added, DS * 4 * (t + 1))
                    dve.tensor_tensor(X3[:, t, :], X3[:, t, :], YD[t % 2], ALU.add).then_inc(x3_sum, 1)
                    dve.wait_ge(x3_sum, t + 1)
                    norm_stats(dve, lambda i: X3[:, t, (i - B * t) * F:(i - B * t + 1) * F], range(B * t, B * t + B))

                def scales(t):
                    norm_scales(dve, B, B * t)
                    dve.nop().then_inc(x3_scales, 1)

                def next_low(t):
                    dve.wait_ge(n_h, t + 1)
                    dve.tensor_tensor(NL[:, t, :], X3[:, t, :], bits(NH[:, t, :]), ALU.subtract).then_inc(n_l, 1)

                low_parts(0)
                steps = 0
                for t in range(NT):
                    for j in range(4):
                        if j == 2 and t + 1 < NT:
                            low_parts(t + 1)
                        g, dh = j // 2, j % 2
                        acc = groups(YD[t % 2][:, g * 4 * F:(g + 1) * 4 * F])
                        at = 4 * (product_round(t, j) % 2)
                        dve.wait_ge(y_ready, 4 * t + j + 1)
                        for d in range(DH - DS):
                            e = W_EMB + t * D + dh * DH + d
                            y = PS[:, at:at + 4, d * F:(d + 1) * F]
                            if dh == 0 and d == 0:
                                ins = dve.tensor_scalar(acc, y, WT[:, e:e + 1], None, ALU.mult)
                            else:
                                dve.wait_ge(acc_step, steps)
                                ins = dve.scalar_tensor_tensor(acc, y, WT[:, e:e + 1], acc, ALU.mult, ALU.add)
                            ins.then_inc(acc_step, 1)
                            steps += 1
                        if t >= 1 and j == 0:
                            statistics(t - 1)
                        if t >= 1 and j == 2:
                            scales(t - 1)
                        if t >= 3 and j == 1:
                            next_low(t - 3)
                next_low(NT - 3)
                statistics(NT - 1)
                scales(NT - 1)
                next_low(NT - 2)
                next_low(NT - 1)

            @block.tensor
            def _(pe):
                rest = pe.value_load(has_rest[0:1, 0:1], min_val=0, max_val=1)
                pe.wait_ge(w_in, 48)
                for t in range(NT):
                    ins = pe.matmul(PS[:, 7, t * F:(t + 1) * F], EB[:, tile(t)], EB[:, N:N + F], start=True, stop=True)
                ins.then_inc(bo_ready, 1)
                for t in range(NT):
                    if t >= 2:
                        pe.wait_ge(a1_outD if t % 2 else a1_outA, t // 2)
                    adjacent(pe, rest, t, PS[:, t % 2, :], lambda m: ZH[:, m, :], lambda m: ZL[:, m, :],
                             None if t else (z_h, z_l, 0)).then_inc(a1_ready, 1)
                for t in range(NT):
                    if t >= 2:
                        pe.wait_ge(a2_out, t - 1)
                    adjacent(pe, rest, t, PS[:, 2 + t % 2, :], lambda m: ZH[:, m, :], lambda m: ZL[:, m, :],
                             None if t else (z_h, z_l, NT)).then_inc(a2_ready, 1)
                pe.wait_ge(a2_out, NT)
                pe.wait_ge(bo_out, 1)

                def banks_free(rnd):
                    if rnd < 2:
                        return
                    t, j = rounds[rnd - 2]
                    if j is None:
                        pe.wait_ge(k2_l, 2 * t + 2)
                        pe.wait_ge(g2_out, 2 * t + 2)
                    else:
                        pe.wait_ge(acc_step, (DH - DS) * (4 * t + j + 1))
                        pe.wait_ge(sy_ready, DS * (4 * t + j + 1))

                def turn(t):
                    at = 4 * (turn_round(t) % 2)
                    banks_free(turn_round(t))
                    pe.wait_ge(xx_ready, 2 * t + 2)
                    for b in range(B):
                        ins = pe.transpose(PS[:, at + b // 4, tile(b % 4)], XX[:, b, :, :].rearrange("p k f -> p (k f)"), ident)
                    ins.then_inc(kT_ready, 1)
                    pe.wait_ge(gs_l, t + 1)
                    for b in range(B):
                        ins = pe.transpose(PS[:, at + 2 + b // 4, tile(b % 4)], GS[:, t % 2, b, :, :].rearrange("p k f -> p (k f)"), ident)
                    ins.then_inc(gT_ready, 1)

                def products(t, j):
                    g, dh = j // 2, j % 2
                    at = 4 * (product_round(t, j) % 2)
                    banks_free(product_round(t, j))
                    pe.wait_ge(k2_l, 2 * t + g + 1)
                    pe.wait_ge(g2_out, 2 * t + g + 1)
                    c = slice(dh * DH * F, (dh + 1) * DH * F)
                    r = t % 2
                    for i in range(4):
                        b, acc = 4 * g + i, PS[:, at + i, :]
                        pe.matmul(acc, KH[:, r, b, :], WH[:, 0, c], start=True, stop=False)
                        pe.matmul(acc, KH[:, r, b, :], WL[:, 0, c], start=False, stop=False)
                        pe.matmul(acc, KL[:, r, b, :], WH[:, 0, c], start=False, stop=False)
                        pe.matmul(acc, GK[:, r, b, :], WH[:, 1, c], start=False, stop=False)
                        ins = pe.matmul(acc, GK[:, r, b, :], WL[:, 1, c], start=False, stop=True)
                    ins.then_inc(y_ready, 1)

                pe.wait_ge(wl_ready, 2)
                for t, j in rounds:
                    if j is None:
                        turn(t)
                    else:
                        products(t, j)

        LT = feature_major(1)
        X4 = node_major(2)
        lt_ready, lt_out, z_r, z1_h, z1_l, z2_out, x4_scales, x4_centredP, x4_centredD, x4_doneP, x4_doneD, stored = (
            sem(s) for s in ("lt_ready", "lt_out", "z_r", "z1_h", "z1_l", "z2_out", "x4_scales", "x4_centredP", "x4_centredD",
                             "x4_doneP", "x4_doneD", "stored"))
        NB = 2 * BP

        with nc.Block() as block:
            @block.sync
            def _(sp):
                for b in range(B):
                    sp.wait_ge(x4_doneP, b // 2 + 1)
                    sp.wait_ge(x4_doneD, b // 2 + 1)
                    sp.dma_start(out[b].rearrange("(t p) f -> p t f", p=P), X4[:, :, b * F:(b + 1) * F]).then_inc(stored, 16)
                sp.wait_ge(stored, 16 * B)

            @block.tensor
            def _(pe):
                rest = pe.value_load(has_rest[0:1, 0:1], min_val=0, max_val=1)

                def spread_nodes(u):
                    layer, q = u // BP, u % BP
                    if layer:
                        pe.wait_ge(z1_l, q + 1)
                    for half in range(2):
                        c = slice(half * HALF, (half + 1) * HALF)
                        acc = PS[:, 2 * (u % 2) + half, :]
                        if u >= 2:
                            pe.wait_ge(lt_out, u - 1)
                        for m in range(NT):
                            pe.matmul(acc, NH[:, m, tile(q)], ADJH[:, m, c], start=(m == 0), stop=False, skip_group_check=True)
                        with pe.If(rest > 0):
                            for m in range(NT):
                                pe.matmul(acc, NH[:, m, tile(q)], ADJL[:, m, c], start=False, stop=False, skip_group_check=True)
                        for m in range(NT):
                            ins = pe.matmul(acc, NL[:, m, tile(q)], ADJH[:, m, c], start=False, stop=(m == NT - 1), skip_group_check=True)
                        ins.then_inc(lt_ready, 1)

                def features(u):
                    layer, q = u // BP, u % BP
                    pe.wait_ge(lt_out, u + 1)
                    if 2 <= u < BP + 2:
                        pe.wait_ge(z1_l, u - 1)
                    elif u >= BP + 2:
                        pe.wait_ge(z2_out, u - 1 - BP)
                    for t in range(NT):
                        ins = pe.matmul(PS[:, 4 + 2 * (u % 2) + t // 4, (t % 4) * P:(t % 4 + 1) * P], LT[:, u % 4, tile(t)],
                                        wt(W_L3 + layer * P, P), start=True, stop=True)
                    ins.then_inc(z_r, 1)

                spread_nodes(0)
                for u in range(1, NB):
                    spread_nodes(u)
                    features(u - 1)
                features(NB - 1)

            def product(u):
                return PS[:, 4 + 2 * (u % 2):6 + 2 * (u % 2), :].rearrange("p a (t c) -> p (a t) c", c=P)

            @block.scalar
            def _(act):
                def lt_copy(u):
                    act.wait_ge(lt_ready, 2 * u + 2)
                    act.activation(LT[:, u % 4, :], PS[:, 2 * (u % 2):2 * (u % 2) + 2, :].rearrange("p a c -> p (a c)"),
                                   ACT.Copy).then_inc(lt_out, 1)

                lt_copy(0)
                for u in range(NB):
                    if u + 1 < NB:
                        lt_copy(u + 1)
                    if u < BP:
                        act.wait_ge(z_r, u + 1)
                        act.activation(NH[:, :, tile(u)], product(u), ACT.Relu).then_inc(z1_h, 1)

            def x4_norm(engine, q, half):
                return norm_apply(engine, X4[:, 4 * half:4 * half + 4, tile(q)], 2 * NT * q + 8 * half, 4, 2)

            @block.gpsimd
            def _(pool):
                for q in range(BP):
                    centre, scale = x4_norm(pool, q, 0)
                    pool.wait_ge(x4_scales, q + 1)
                    centre().then_inc(x4_centredP, 1)
                    pool.wait_ge(x4_centredP, q + 1)
                    scale().then_inc(x4_doneP, 1)

            @block.vector
            def _(dve):
                for u in range(BP):
                    dve.wait_ge(z1_h, u + 1)
                    dve.scalar_tensor_tensor(NL[:, :, tile(u)], product(u), 0.0, bits(NH[:, :, tile(u)]),
                                             ALU.max, ALU.subtract).then_inc(z1_l, 1)
                for q in range(BP):
                    dve.wait_ge(z_r, BP + q + 1)
                    dve.scalar_tensor_tensor(X4[:, :, tile(q)], product(BP + q), 0.0, X3[:, :, tile(q)],
                                             ALU.max, ALU.add).then_inc(z2_out, 1)
                    dve.wait_ge(z2_out, q + 1)
                    first = 2 * NT * q
                    norm_stats(dve, lambda i: X4[:, (i - first) // 2, (2 * q + i % 2) * F:(2 * q + i % 2 + 1) * F],
                               range(first, first + 2 * NT))
                    norm_scales(dve, 2 * NT, first)
                    dve.nop().then_inc(x4_scales, 1)
                    centre, scale = x4_norm(dve, q, 1)
                    centre().then_inc(x4_centredD, 1)
                    dve.wait_ge(x4_centredD, q + 1)
                    scale().then_inc(x4_doneD, 1)


def kernel(**inputs):
    import numpy as np
    import concourse.bacc as bacc
    from concourse.bass_utils import run_bass_kernel_spmd

    a = {k: np.asarray(v) for k, v in inputs.items()}

    consts = np.zeros((P, CW), np.float32)
    consts[:, C_ID:C_ID + P] = np.eye(P)
    consts[:, C_ID2:C_ID2 + F] = np.concatenate([np.eye(F)] * 2)
    consts[:, C_ONE:C_ONE + P] = 1
    consts[0:64, C_UP:C_UP + P] = np.concatenate([np.triu(np.ones((E, E)))] * 2, 1)
    consts[0:NT, C_TRI:C_TRI + NT + 1] = np.triu(np.ones((NT, NT + 1)), 1)
    consts[:, C_STEP:C_STEP + QUADS] = SLOTS * np.arange(QUADS)
    consts[:, C_RANK:C_RANK + E + SLOTS] = 1 + np.arange(E + SLOTS)
    consts[:, C_M1] = -1

    weights = np.zeros((P, WW), np.float32)

    def diagonal(at, w):
        n = w.shape[1]
        weights[0:64, at:at + n] = w
        weights[64:128, at + n:at + 2 * n] = w

    def twice(at, w):
        weights[0:64, at:at + w.shape[1]] = w
        weights[64:128, at:at + w.shape[1]] = w

    diagonal(W_H, a["L0_gnn_W"])
    diagonal(W_IND, a["L0_gnn_W_ind"])
    diagonal(W_AN, np.repeat(a["L0_gnn_a_node"][:, None], E, 1))
    diagonal(W_GN, a["L0_gnn_a_gn"][:, None])
    weights[0:64, W_FC:W_FC + P] = a["L0_gnn_fcW"]
    weights[64:128, W_FC + P:W_FC + 2 * P] = a["L0_gnn_fcW"]
    weights[:, W_FCB] = a["L0_gnn_fcb"]
    weights[:, W_AV] = a["L0_gnn_av"]
    weights[:, W_GE:W_GE + F] = a["L0_gnn_a_ge"][None, :]
    for at, w in ((W_Q, a["L1_gnn_Wq"]), (W_K, a["L1_gnn_Wk"])):
        weights[0:64, at:at + P] = np.concatenate([w, w], 1)
        weights[64:128, at + P:at + 2 * P] = np.concatenate([w, w], 1)
    diagonal(W_V, a["L1_gnn_Wv"])
    twice(W_BQ, a["L1_gnn_bq"][:, None])
    twice(W_BK, a["L1_gnn_bk"][:, None])
    weights[:, W_EMB:W_EMB + NT * D] = a["L2_gnn_embedding"].reshape(NT, P, D).transpose(1, 0, 2).reshape(P, NT * D)
    l3 = a["L3_gnn_net_params"].reshape(2, F, F)
    diagonal(W_L3, l3[0])
    diagonal(W_L3 + P, l3[1])

    w = a["L2_gnn_weight"].transpose(1, 2, 0, 3).reshape(3, F, D * F)
    arrays = {
        "in_x_nat": np.ascontiguousarray(a["x"].transpose(1, 0, 2)),
        "in_x_tr": np.ascontiguousarray(a["x"].transpose(0, 2, 1)).reshape(B * F, N),
        "in_adj_tr": np.ascontiguousarray(a["adj"].T),
        "in_h_nat": np.ascontiguousarray(a["L0_gnn_H"]),
        "in_h_tr": np.ascontiguousarray(a["L0_gnn_H"].T),
        "in_consts": consts,
        "in_weights": weights,
        "in_w01": np.ascontiguousarray(w[0:2].reshape(2 * F, D * F)),
        "in_w2": np.ascontiguousarray(np.concatenate([w[2], w[2]])),
        "in_emb_bias": np.ascontiguousarray(np.concatenate([a["L2_gnn_embedding"].T, a["L2_gnn_bias"]], 1)),
    }
    nc = bacc.Bacc("TRN2", target_bir_lowering=False, num_devices=1)
    args = [nc.dram_tensor(n, v.shape, mybir.dt.from_np(v.dtype), kind="ExternalInput").ap() for n, v in arrays.items()]
    out = nc.dram_tensor("out_0", (B, N, F), F32, kind="ExternalOutput").ap()
    program(nc, *args, out)
    r = run_bass_kernel_spmd(nc, [arrays], core_ids=[0])
    return r.results[0]["out_0"]
```
